# Optimizing a Trainium2 kernel written in Bass

```python
import numpy as np
import jax
import jax.numpy as jnp

def _softmax(x, axis=-1):
    return jax.nn.softmax(x, axis=axis)
def _gelu(x):
    return jax.nn.gelu(x, approximate=True)
def _silu(x):
    return jax.nn.silu(x)
def _sigmoid(x):
    return jax.nn.sigmoid(x)
def _layernorm(x, axis=-1, eps=1e-5):
    m = jnp.mean(x, axis=axis, keepdims=True)
    v = jnp.var(x, axis=axis, keepdims=True)
    return (x - m) / jnp.sqrt(v + eps)
def _scatter_add(tgt, idx, src, axis=0):
    return tgt.at[idx].add(src)
def _segment_sum(src, seg, n):
    return jax.ops.segment_sum(src, seg, n)

kernel_name = 'mk_conv_preact_d2_conv_nchw32_a29c12'

def setup_inputs(seed: int = 0):
    np.random.seed(seed)
    _w = jnp.asarray
    def _rec_inputs():
        import jax
        import jax.numpy as jnp
        _gk = jax.random.key(seed)
        x = -0.000125 + 0.9999 * jax.random.normal(jax.random.fold_in(_gk, 1), (16, 32, 256, 256), jnp.float32)
        return x
    x = _rec_inputs()
    def _L0_conv_setup():
        import jax, jax.numpy as jnp
        import numpy as np
        E = 4
        OUT_CH = 32
        IN_CH = 32
        KSIZE = 3
        PAD = 1
        TEMPERATURE = 30.0
        HIDDEN = IN_CH // 4

        def _dyn_conv(x, w):

            def one(xi, wi):
                return jax.lax.conv_general_dilated(xi[None], wi, window_strides=(1, 1), padding=[(PAD, PAD), (PAD, PAD)], dimension_numbers=('NCHW', 'OIHW', 'NCHW'))[0]
            return jax.vmap(one)(x, w)
        key = jax.random.key(seed)
        ks = jax.random.split(key, 6)
        x = jax.random.normal(ks[0], (16, IN_CH, 256, 256), dtype=jnp.float32)
        w_c1 = jax.random.normal(ks[1], (HIDDEN, IN_CH), dtype=jnp.float32) * (2.0 / IN_CH) ** 0.5
        w_c2 = jax.random.normal(ks[2], (E * OUT_CH, HIDDEN), dtype=jnp.float32) * (2.0 / HIDDEN) ** 0.5
        weight1 = jax.random.normal(ks[3], (E, OUT_CH, IN_CH, KSIZE, KSIZE), dtype=jnp.float32)
        weight2 = jax.random.normal(ks[4], (E, OUT_CH, OUT_CH, KSIZE, KSIZE), dtype=jnp.float32)
        weight3 = jax.random.normal(ks[5], (E, OUT_CH, OUT_CH, KSIZE, KSIZE), dtype=jnp.float32)
        return {'x': x, 'w_c1': w_c1, 'w_c2': w_c2, 'weight1': weight1, 'weight2': weight2, 'weight3': weight3}
    _L0_conv_all = _L0_conv_setup()
    _L0_conv_in = {k: v for k, v in _L0_conv_all.items() if k in ('w_c1', 'w_c2', 'weight1', 'weight2', 'weight3', )}
    del _L0_conv_all

    def _L1_conv_setup():
        import jax, jax.numpy as jnp
        import numpy as np
        MODES_H, MODES_W = (32, 32)
        IN_CH, OUT_CH = (32, 32)

        def dht2d(x, is_inverse=False):
            X = jnp.fft.fft2(x)
            h = X.real - X.imag
            if is_inverse:
                h = h / (x.shape[-2] * x.shape[-1])
            return h

        def flip_periodic(x):
            for ax in (-2, -1):
                x = jnp.roll(jnp.flip(x, axis=ax), 1, axis=ax)
            return x
        key = jax.random.key(seed)
        k1, k2, k3 = jax.random.split(key, 3)
        init_std = (2.0 / (IN_CH + OUT_CH)) ** 0.5
        x = jax.random.normal(k1, (16, IN_CH, 256, 256), dtype=jnp.float32)
        weight = init_std * jax.random.normal(k2, (IN_CH, OUT_CH, 2 * MODES_H, 2 * MODES_W), dtype=jnp.float32)
        bias = init_std * jax.random.normal(k3, (OUT_CH, 1, 1), dtype=jnp.float32)
        return {'x': x, 'weight': weight, 'bias': bias}
    _L1_conv_all = _L1_conv_setup()
    _L1_conv_in = {k: v for k, v in _L1_conv_all.items() if k in ('weight', 'bias', )}
    del _L1_conv_all

    return {
        "x": x,
        "L0_conv_w_c1": _L0_conv_in["w_c1"],
        "L0_conv_w_c2": _L0_conv_in["w_c2"],
        "L0_conv_weight1": _L0_conv_in["weight1"],
        "L0_conv_weight2": _L0_conv_in["weight2"],
        "L0_conv_weight3": _L0_conv_in["weight3"],
        "L1_conv_weight": _L1_conv_in["weight"],
        "L1_conv_bias": _L1_conv_in["bias"],
    }

def reference(x, L0_conv_w_c1, L0_conv_w_c2, L0_conv_weight1, L0_conv_weight2, L0_conv_weight3, L1_conv_weight, L1_conv_bias):
    import jax
    import jax.numpy as jnp
    def _L0_conv_ref(x, w_c1, w_c2, weight1, weight2, weight3):
        import jax, jax.numpy as jnp
        import numpy as np
        E = 4
        OUT_CH = 32
        IN_CH = 32
        KSIZE = 3
        PAD = 1
        TEMPERATURE = 30.0
        HIDDEN = IN_CH // 4

        def _dyn_conv(x, w):

            def one(xi, wi):
                return jax.lax.conv_general_dilated(xi[None], wi, window_strides=(1, 1), padding=[(PAD, PAD), (PAD, PAD)], dimension_numbers=('NCHW', 'OIHW', 'NCHW'))[0]
            return jax.vmap(one)(x, w)
        B = x.shape[0]
        gap = x.mean(axis=(2, 3))
        h = jax.nn.relu(gap @ w_c1.T)
        coeff = (h @ w_c2.T).reshape(B, OUT_CH, E)
        coeff = jax.nn.softmax(coeff / TEMPERATURE, axis=2)

        def assemble(w):
            flat = w.reshape(E, OUT_CH, -1)
            agg = jnp.einsum('boe,eoc->boc', coeff, flat)
            return agg.reshape(B, OUT_CH, *w.shape[2:])
        w1 = assemble(weight1)
        w2 = assemble(weight2)
        w3 = assemble(weight3)
        out = _dyn_conv(x, w1)
        out = _dyn_conv(out, w2)
        out = _dyn_conv(out, w3)
        return out

    def _L1_conv_ref(x, weight, bias):
        import jax, jax.numpy as jnp
        import numpy as np
        MODES_H, MODES_W = (32, 32)
        IN_CH, OUT_CH = (32, 32)

        def dht2d(x, is_inverse=False):
            X = jnp.fft.fft2(x)
            h = X.real - X.imag
            if is_inverse:
                h = h / (x.shape[-2] * x.shape[-1])
            return h

        def flip_periodic(x):
            for ax in (-2, -1):
                x = jnp.roll(jnp.flip(x, axis=ax), 1, axis=ax)
            return x
        b, c, h, w = x.shape
        X = dht2d(x)
        Xr = flip_periodic(X)
        ch, cw = (h // 2, w // 2)
        sl_h = slice(ch - MODES_H, ch + MODES_H)
        sl_w = slice(cw - MODES_W, cw + MODES_W)
        Xc = X[:, :, sl_h, sl_w]
        Xrc = Xr[:, :, sl_h, sl_w]
        kernel = weight
        kernel_rev = flip_periodic(weight)
        x_even = (Xc + Xrc) * 0.5
        x_odd = (Xc - Xrc) * 0.5
        total = jnp.einsum('bixy,ioxy->boxy', x_even, kernel) + jnp.einsum('bixy,ioxy->boxy', x_odd, kernel_rev)
        pw_l = (w - 2 * MODES_W) // 2
        pw_r = pw_l + int(w % 2 == 1)
        ph_l = (h - 2 * MODES_H) // 2
        ph_r = ph_l + int(h % 2 == 1)
        total = jnp.pad(total, ((0, 0), (0, 0), (ph_l, ph_r), (pw_l, pw_r)))
        out = dht2d(total, is_inverse=True)
        out = out + bias
        return out

    def _gn(v, G=16, eps=1e-5):
        B_, C_, H_, W_ = v.shape
        g = v.reshape(B_, G, C_ // G, H_, W_)
        m = jnp.mean(g, axis=(2, 3, 4), keepdims=True)
        s = jnp.var(g, axis=(2, 3, 4), keepdims=True)
        return ((g - m) / jnp.sqrt(s + eps)).reshape(v.shape)

    def _ln_c(v, eps=1e-6):
        m = jnp.mean(v, axis=1, keepdims=True)
        s = jnp.var(v, axis=1, keepdims=True)
        return (v - m) / jnp.sqrt(s + eps)

    def _ln_t(v, eps=1e-5):
        m = jnp.mean(v, axis=-1, keepdims=True)
        s = jnp.var(v, axis=-1, keepdims=True)
        return (v - m) / jnp.sqrt(s + eps)

    def _to_tokens(v):
        B_, C_, H_, W_ = v.shape
        return v.reshape(B_, C_, H_ * W_).transpose(0, 2, 1)
    def _from_tokens(t, like):
        B_, C_, H_, W_ = like.shape
        return t.transpose(0, 2, 1).reshape(B_, C_, H_, W_)

    x = x + _L0_conv_ref(_gn(x), L0_conv_w_c1, L0_conv_w_c2, L0_conv_weight1, L0_conv_weight2, L0_conv_weight3)
    x = x + _L1_conv_ref(_gn(x), L1_conv_weight, L1_conv_bias)
    return x


_drawn_inputs = setup_inputs


def setup_inputs(seed=0):
    import zlib

    import numpy as np

    out = dict(_drawn_inputs(seed))
    spreads = {}
    factors = {'L0_conv_w_c1': 37.102,
     'L0_conv_w_c2': 32.198,
     'L1_conv_weight': 64.0,
     'L1_conv_bias': 199.64}
    for name, (base, spread) in spreads.items():
        noise = np.random.default_rng([zlib.crc32(name.encode()), seed]).standard_normal(out[name].shape)
        drawn = base * np.exp(spread * noise) if base else spread * noise
        out[name] = jnp.asarray(drawn.astype(out[name].dtype))
    for name, factor in factors.items():
        out[name] = (out[name] * factor).astype(out[name].dtype)
    return out
```

```python
import numpy as np
import concourse.bass as bass
from concourse import mybir
from contextlib import ExitStack

P = 128
C = 32
IMG = 256
W2 = IMG + 2
E = 4
TAPS = 9
Q = 4
CHUNK = 2
NCH = 33
SLOTS = 3
CREDIT = 3
WSCALE = 1024.0
HALF = 2.0
TEMP = 30.0
EPS = 1e-5
MW = 3 * 64


def constants():
    c4 = np.arange(P) // 4
    cq = np.arange(P) % C
    same_group = (c4[:, None] // 2 == c4[None, :] // 2) / 8.0
    to_group = (c4[:, None] // 2 == cq[None, :] // 2) / 8.0
    to_channel = (c4[:, None] == cq[None, :]) / 4.0
    ident = np.eye(P)
    q = np.arange(P) // C
    masks = np.zeros((P, 8))
    masks[:, 0] = (q >= 1) / WSCALE
    masks[:, 1] = (q == 0) / WSCALE
    masks[:, 2] = (q >= 2) / (WSCALE * HALF)
    masks[:, 3] = (q <= 1) / (WSCALE * HALF)
    groupq = (cq[:, None] // 2 == cq[None, :] // 2) / 8.0
    return np.concatenate([same_group, to_group, to_channel, ident, groupq, masks], axis=1).astype(np.float32)


NCONST = 5 * P + 8


def build_convs(nc, x, w_c1, w_c2, w1, w2, w3, consts, x1d, stats1_d, S):
    f32, f16 = mybir.dt.float32, mybir.dt.float16
    ALU, ACT, AX = mybir.AluOpType, mybir.ActivationFunctionType, mybir.AxisListType
    experts_d = [w1, w2, w3]

    with ExitStack() as ctx:
        sb = lambda n, s, d=f32: ctx.enter_context(nc.sbuf_tensor(n, s, d))
        ps = lambda n, s, d=f32: ctx.enter_context(nc.psum_tensor(n, s, d))
        sem = lambda n: ctx.enter_context(nc.semaphore(n))

        cst = sb("cst", [P, NCONST])
        same_group, to_group, to_channel, ident = (cst[:, i * P:(i + 1) * P] for i in range(4))
        mask = lambda i: cst[:, 5 * P + i:5 * P + i + 1]

        x_in = {k: sb(f"x_in_{k}", [P, 6, IMG]) for k in "CAB"}
        st_in = {k: sb(f"st_in_{k}", [P, 4, 512]) for k in "AB"}
        res = {k: sb(f"res_{k}", [P, n, IMG]) for k, n in (("C", 2), ("A", 6), ("B", 6), ("D", 4))}
        out = {k: sb(f"out_{k}", [P, n, IMG]) for k, n in (("C", 2), ("A", 6), ("B", 6), ("D", 4))}
        ring = [{k: sb(f"ring{n}_{k}", [P, SLOTS * CHUNK, W2], f16) for k in ("Ahi", "Alo", "Bhi", "Blo")}
                for n in range(3)]
        xn = sb("xn", [P, CHUNK, IMG])
        ex = [sb(f"ex{n}", [P, E, 6, C]) for n in range(3)]
        mixed = sb("mixed", [P, E, 6, C])
        whi = [sb(f"whi{n}", [P, MW], f16) for n in range(3)]
        wlo = [sb(f"wlo{n}", [P, MW], f16) for n in range(3)]
        stage = sb("stage", [P, 3, C * TAPS])
        taps = sb("taps", [P, 3, 3, 5, C])
        sumsq = sb("sumsq", [P, 3])
        maxsq = sb("maxsq", [P, 3])
        norms = sb("norms", [P, 3])
        alpha = sb("alpha", [P, 3])
        squares = sb("squares", [P, C * TAPS])
        final_scale = sb("final_scale", [P, 1])
        wc1_in = sb("wc1_in", [8, C])
        wc1t = sb("wc1t", [P, 8])
        wc1r = sb("wc1r", [8, P])
        wc2_in = sb("wc2_in", [P, 8])
        wc2t = sb("wc2t", [8, P])
        ones = sb("ones", [P, P])
        bn0 = sb("bn0", [P, 32, 6])
        bn1 = sb("bn1", [P, NCH, 6])
        mv = sb("mv", [P, 2])
        mv1 = sb("mv1", [P, S, 2])
        mv1_now = sb("mv1_now", [P, 2])
        dev = sb("dev", [P, 2])
        me = sb("me", [P, 2])
        stq = sb("stq", [P, 3])
        norm_next = sb("norm_next", [P, 2])
        norm_now = sb("norm_now", [P, 2])
        var_eps = sb("var_eps", [P, 1])
        minus_half = sb("minus_half", [P, 1])
        gap = sb("gap", [P, 1])
        gapb = sb("gapb", [P, P])
        hbs = sb("hbs", [8, P])
        mx = sb("mx", [P, C])
        lg = sb("lg", [P, C, E])
        ex_l = sb("ex_l", [P, C, E])
        den = sb("den", [P, C])
        rden = sb("rden", [P, C])
        coeff = sb("coeff", [P, E, C])
        first = sb("first", [P, 8, 512 * 4])

        bank = [[ps(f"bank{n}{i}", [P, 512]) for i in range(2)] for n in range(3)]
        prep_ps = ps("prep_ps", [P, 512])
        prep_ps2 = ps("prep_ps2", [P, 512])

        loaded, first_in, sq_done, mx_done, sc_done, tr_done, ex_done, zeroed, dch, pch, ach, tiny, res_zeroed, passed = (
            sem(n) for n in ("loaded", "first_in", "sq_done", "mx_done", "sc_done", "tr_done", "ex_done", "zeroed",
                             "dch", "pch", "ach", "tiny", "res_zeroed", "passed"))
        x_here = {k: sem(f"x_here_{k}") for k in "CAB"}
        st_here = {k: sem(f"st_here_{k}") for k in "AB"}
        res_here = {k: sem(f"res_here_{k}") for k in "CABD"}
        stored = {k: sem(f"stored_{k}") for k in "CABD"}
        hi_ready = [sem(f"hi{n}_ready") for n in range(3)]
        lo_ready = [sem(f"lo{n}_ready") for n in range(3)]
        bhi_ready = [sem(f"bhi{n}_ready") for n in range(3)]
        blo_ready = [sem(f"blo{n}_ready") for n in range(3)]
        conv_done = [sem(f"conv{n}_done") for n in range(3)]
        x1_ready, x1_stat, stat_read, bn1_aggr = (sem(n) for n in ("x1_ready", "x1_stat", "stat_read", "bn1_aggr"))
        w_ready = [sem(f"w{n}_ready") for n in range(3)]
        mean_ready, gm_ready, e_ready, stq_ps, stq_ready, gap_ready, hid_ps, hid_ready, log_ps, lg_ready, exp_ready, \
            coeff_ready, stored_stats = (
                sem(n) for n in ("mean_ready", "gm_ready", "e_ready", "stq_ps", "stq_ready", "gap_ready", "hid_ps",
                                 "hid_ready", "log_ps", "lg_ready", "exp_ready", "coeff_ready", "stored_stats"))

        block = ctx.enter_context(nc.Block())

        def rows(t, s, r0, n):
            return t[s, :, bass.ds(r0, n, 4) if not isinstance(r0, int) else slice(r0, r0 + 4 * (n - 1) + 1, 4), :]

        @block.sync
        def _(sp):
            sp.dma_start(cst[:], consts).then_inc(loaded, 16)
            for n in range(3):
                sp.dma_start(stage[:, n, :], experts_d[n].rearrange("e o c h w -> (e o) (c h w)")).then_inc(loaded, 16)
            sp.dma_start(wc1_in[:], w_c1).then_inc(loaded, 16)
            sp.dma_start(wc2_in[:], w_c2).then_inc(loaded, 16)
            for i in range(4):
                sp.dma_start(first[:, 2 * i:2 * i + 2, :],
                             x[0].rearrange("c (r h) w -> (c r) (h w)", r=4)
                             [:, 4096 * i:4096 * (i + 1)].rearrange("p (a b) -> p a b", a=2)).then_inc(first_in, 16)

            xs = x.rearrange("s c (b q) w -> s q c b w", q=Q)
            x1s = x1d.rearrange("s c (b q) w -> s q c b w", q=Q)
            xflat = x.rearrange("s c (r h) w -> s (c r) (h w)", r=4)

            def load_x(buf, s, b0, n):
                for q in range(Q):
                    sp.dma_start(x_in[buf][q * C:(q + 1) * C, 0:n, :], xs[s, q, :, bass.ds(b0, n), :]).then_inc(x_here[buf], 16)

            def shifted(t, s, q, b0, n):
                return t[s, 0, :, bass.ds(b0, n), :] if q == 3 else t[s, q + 1, :, bass.ds(b0 - 1, n), :]

            def load_res(buf, s, b0):
                for q in range(Q):
                    sp.dma_start(res[buf][q * C:(q + 1) * C, :, :], shifted(xs, s, q, b0, 6)).then_inc(res_here[buf], 16)

            def store_out(buf, s, b0):
                for q in range(Q):
                    sp.dma_start(shifted(x1s, s, q, b0, 6), out[buf][q * C:(q + 1) * C, :, :]).then_inc(stored[buf], 16)

            def load_stat(buf, s, k):
                sp.dma_start(st_in[buf][:, :, :], xflat[s, :, bass.ds(2048 * k, 2048)].rearrange("p (a b) -> p a b", a=4)
                             ).then_inc(st_here[buf], 16)

            def edge(q):
                return ((0, 2), (0, 2)) if q == 3 else ((1, 1), (0, 3))

            def load_first(s, s2):
                load_x("C", s, 0, 6)
                for q in range(Q):
                    b, n = edge(q)[0]
                    sp.dma_start(res["C"][q * C:(q + 1) * C, b:b + n, :], shifted(xs, s, q, b, n)).then_inc(res_here["C"], 16)
                for g, buf in ((1, "A"), (2, "B")):
                    load_x(buf, s, 6 * g, 6)
                    load_res(buf, s, 6 * g - 4)
                    load_stat(buf, s2, g - 1)

            sp.wait_ge(res_zeroed, 1)
            load_first(0, 1 % S)
            with sp.Fori(0, S) as s:
                nxt = sp.snap((s + 1) % S)
                n0 = sp.snap(s * NCH)
                with sp.Fori(0, 3) as i:
                    ni = sp.snap(n0 + i * 6)
                    for k, buf in ((0, "A"), (1, "B")):
                        g = 1 + k
                        sp.wait_ge(x1_ready, ni + (3 * g + 1) + 1)
                        store_out(buf, s, i * 12 + (6 * g - 4))
                        sp.wait_ge(lo_ready[0], ni + (3 * g + 3) + 1)
                        load_x(buf, s, i * 12 + 6 * (g + 2), 6)
                        load_res(buf, s, i * 12 + (6 * (g + 2) - 4))
                        sp.wait_ge(stat_read, s * 8 + i * 2 + (k + 1))
                        load_stat(buf, nxt, i * 2 + (g + 1))
                for g, buf in ((7, "A"), (8, "B")):
                    sp.wait_ge(x1_ready, n0 + (3 * g + 1) + 1)
                    store_out(buf, s, 6 * g - 4)
                    sp.wait_ge(lo_ready[0], n0 + (3 * g + 3) + 1)
                    load_x(buf, s, 6 * (g + 2), 6 if g == 7 else 4)
                    load_res(buf, s, 6 * (g + 2) - 4)
                    if g == 7:
                        for q in range(Q):
                            b, n = edge(q)[0]
                            sp.dma_start(shifted(x1s, s, q, b, n), out["C"][q * C:(q + 1) * C, b:b + n, :]).then_inc(stored["C"], 16)
                        for q in range(Q):
                            b, n = edge(q)[1]
                            sp.dma_start(res["D"][q * C:(q + 1) * C, b:b + n, :], shifted(xs, s, q, 62 + b, n)).then_inc(res_here["D"], 16)
                sp.wait_ge(lo_ready[0], n0 + NCH + 1)
                load_x("C", nxt, 0, 6)
                for q in range(Q):
                    b, n = edge(q)[0]
                    sp.dma_start(res["C"][q * C:(q + 1) * C, b:b + n, :], shifted(xs, nxt, q, b, n)).then_inc(res_here["C"], 16)
                nxt2 = sp.snap((s + 2) % S)
                sp.wait_ge(stat_read, s * 8 + 8)
                sp.sem_inc(passed, 1)
                for g, buf, done in ((1, "A", 9), (2, "B", 10)):
                    sp.wait_ge(x1_ready, n0 + (3 * done + 1) + 1)
                    store_out(buf, s, 6 * done - 4)
                    load_x(buf, nxt, 6 * g, 6)
                    load_res(buf, nxt, 6 * g - 4)
                    load_stat(buf, nxt2, g - 1)
                sp.wait_ge(x1_ready, n0 + NCH + 1)
                for q in range(Q):
                    b, n = edge(q)[1]
                    sp.dma_start(shifted(x1s, s, q, 62 + b, n), out["D"][q * C:(q + 1) * C, b:b + n, :]).then_inc(stored["D"], 16)
            sp.wait_ge(bn1_aggr, S)
            sp.dma_start(stats1_d, mv1[:]).then_inc(stored_stats, 16)
            for k, n in (("C", 1), ("A", 5), ("B", 5), ("D", 1)):
                sp.wait_ge(stored[k], 64 * n * S + 1)
                if k != "D":
                    sp.wait_ge(x_here[k], 64 * (n * S + 1))
                sp.wait_ge(res_here[k], 64 * (n * S + (k != "D")))
                if k in "AB":
                    sp.wait_ge(st_here[k], 16 * (4 * S + 1))
            sp.wait_ge(stored_stats, 16)

        def taps_view(m, n, dx):
            return taps[:, n, dx, 1 - m:5 - m, :]

        def copy_b(engine, n, kind, slot):
            a, b = ring[n]["A" + kind], ring[n]["B" + kind]
            s0 = slot * CHUNK
            v = lambda t, p, i, k: t[p * 64:(p + 1) * 64, i:i + k, :].bitcast(f32)
            engine(v(b, 1, s0, 2), v(a, 0, s0, 2))
            if slot:
                return engine(v(b, 0, s0, 2), v(a, 1, s0 - 1, 2))
            engine(v(b, 0, 0, 1), v(a, 1, SLOTS * CHUNK - 1, 1))
            return engine(v(b, 0, 1, 1), v(a, 1, 0, 1))

        def spans(n, t, base):
            if t == 0:
                return [(0, 1, mask(0 if n == 1 else 2)), (1, 1, base)]
            if t == NCH - 1:
                return [(0, 1, mask(1 if n == 1 else 3)), (1, 1, 0.0)]
            return [(0, 2, base)]

        @block.tensor
        def _(pe):
            pe.wait_ge(loaded, 6 * 16)
            pe.wait_ge(zeroed, 1)
            for k in range(18):
                n, m, dx = k // 6, (k // 3) % 2, k % 3
                if k >= 2:
                    pe.wait_ge(ex_done, k - 1)
                dst = (prep_ps, prep_ps2)[k % 2]
                nc.tensor.matmul(dst[:, 0:P], taps_view(m, n, dx), ident, start=True, stop=True).then_inc(tr_done, 1)
            pe.wait_ge(ex_done, 18)
            pe.wait_ge(tiny, 1)
            nc.tensor.matmul(prep_ps[:, 0:8], wc1r[:], cst[0:8, 3 * P:3 * P + 8], start=True, stop=True)
            nc.tensor.matmul(prep_ps2[0:8, 0:P], wc2_in[:], ident, start=True, stop=True).then_inc(tr_done, 1)
            pe.wait_ge(tiny, 2)

            def group_mean(k):
                pe.wait_ge(mean_ready, k + 1)
                nc.tensor.matmul(prep_ps[:, 0:1], same_group, mv[:, 0:1], start=True, stop=True).then_inc(gm_ready, 1)

            def moments(k):
                pe.wait_ge(e_ready, k + 1)
                nc.tensor.matmul(prep_ps2[:, 0:2], to_group, me[:, 0:2], start=True, stop=True)
                nc.tensor.matmul(prep_ps[:, 0:1], to_channel, me[:, 0:1], start=True, stop=True).then_inc(stq_ps, 1)

            def hidden(k):
                pe.wait_ge(gap_ready, k + 1)
                nc.tensor.matmul(prep_ps[0:8, 0:P], wc1t[:], gapb[:], start=True, stop=True).then_inc(hid_ps, 1)

            def logits(k):
                pe.wait_ge(hid_ready, k + 1)
                nc.tensor.matmul(prep_ps2[:, 0:P], hbs[:], wc2t[:], start=True, stop=True).then_inc(log_ps, 1)

            def conv(n, t, slot, count, first):
                pe.wait_ge(bhi_ready[n], count + (1 + CREDIT))
                pe.wait_ge(blo_ready[n], count + (1 + CREDIT))
                emptied = x1_ready if n == 2 else lo_ready[n + 1]
                pe.wait_ge(emptied, (count if first else count - 1) + 1)
                r, s0, dst = ring[n], slot * CHUNK, bank[n][t % 2]
                terms = [("hi", whi[n], 0), ("lo", whi[n], 0), ("hi", wlo[n], 0)]
                k = 0
                for dx in range(3):
                    for kind, w, _ in terms:
                        for half, side in ((0, "B"), (1, "A")):
                            last = nc.tensor.matmul(dst[64 * half:64 * half + 64, :], w[:, 64 * dx:64 * dx + 64],
                                                    r[side + kind][:, s0:s0 + CHUNK, dx:dx + IMG],
                                                    start=(k == 0), stop=(k == 8))
                        k += 1
                last.then_inc(conv_done[n], 1)

            def step(n0, t, after=(None, None, None)):
                for n in range(3):
                    if 0 <= t - n < NCH:
                        conv(n, (t - n), (t - n) % SLOTS, n0 + (t - n), t == n)
                    if after[n] is not None:
                        after[n][0](after[n][1])

            group_mean(0)
            moments(0)
            hidden(0)
            logits(0)
            with pe.Fori(0, S) as s:
                n0 = pe.snap(s * NCH)
                k1 = pe.snap(s + 1)
                for t in range(3):
                    pe.wait_ge(w_ready[t], k1)
                    step(n0, t)
                with pe.Fori(0, 4) as i:
                    ni = pe.snap(n0 + i * 6)
                    for t in range(3, 9):
                        step(ni, t)
                step(n0, 27, (None, (group_mean, k1), None))
                step(n0, 28, ((moments, k1), None, None))
                step(n0, 29, ((hidden, k1), None, (logits, k1)))
                for t in range(30, NCH + 2):
                    step(n0, t)

        @block.scalar
        def _(act):
            act.wait_ge(loaded, 6 * 16)
            for n in range(3):
                nc.scalar.activation(squares[:], stage[:, n, :], ACT.Square,
                                     accum_out=sumsq[:, n:n + 1]).then_inc(sq_done, 1)
                act.wait_ge(sq_done, n + 1)
            act.wait_ge(mx_done, 1)
            nc.scalar.activation(norms[:], maxsq[:], ACT.Sqrt).then_inc(ach, 1)
            act.wait_ge(zeroed, 1)

            def softmax_exp(k):
                act.wait_ge(lg_ready, k + 1)
                nc.scalar.activation(ex_l[:], lg[:], ACT.Exp, scale=1.0 / TEMP).then_inc(exp_ready, 1)

            def b_ring(n, slot, count):
                act.wait_ge(hi_ready[n], count + 1)
                act.wait_ge(conv_done[n], count - 2 + CREDIT)
                copy_b(nc.scalar.copy, n, "hi", slot).then_inc(bhi_ready[n], 1)

            def hi(n, t, edges, count):
                act.wait_ge(conv_done[n - 1], count + (1 + CREDIT))
                act.wait_ge(conv_done[n], count - 2 + CREDIT)
                slot, src = t % SLOTS, bank[n - 1][t % 2]
                base = 1.0 / WSCALE if n == 1 else 1.0 / (WSCALE * HALF)
                for b, k, sc in spans(n, edges, base):
                    last = nc.scalar.activation(ring[n]["Ahi"][:, slot * CHUNK + b:slot * CHUNK + b + k, 1:1 + IMG],
                                                src[:, b * IMG:(b + k) * IMG].rearrange("p (b w) -> p b w", b=k), ACT.Copy,
                                                scale=sc)
                last.then_inc(hi_ready[n], 1)
                b_ring(n, slot, count)

            def step(n0, t, edges=False):
                if t < NCH:
                    hi(1, t, t if edges else None, n0 + t)
                if t + 1 < NCH:
                    b_ring(0, (t + 1) % SLOTS, n0 + (t + 1))
                if 0 <= t - 1 < NCH:
                    hi(2, t - 1, (t - 1) if edges else None, n0 + (t - 1))

            softmax_exp(0)
            with act.Fori(0, S) as s:
                n0 = act.snap(s * NCH)
                b_ring(0, 0, n0)
                for t in range(3):
                    step(n0, t, True)
                with act.Fori(0, 4) as i:
                    ni = act.snap(n0 + i * 6)
                    for t in range(3, 9):
                        step(ni, t)
                for t in range(27, NCH + 1):
                    step(n0, t, True)
                    if t == 30:
                        softmax_exp(s + 1)

        @block.vector
        def _(dve):
            n_ch = [0]

            def link(ins):
                n_ch[0] += 1
                ins.then_inc(dch, 1)
                dve.wait_ge(dch, n_ch[0])

            nc.vector.memset(res["C"][:], 0.0)
            nc.vector.memset(res["D"][:], 0.0).then_inc(res_zeroed, 1)
            dve.wait_ge(res_zeroed, 1)
            for n in range(3):
                for r in ring[n].values():
                    nc.vector.memset(r[:].rearrange("p a b -> p (a b)").bitcast(f32), 0.0)
            link(nc.vector.memset(taps[:], 0.0))
            dve.wait_ge(loaded, 6 * 16)
            for n in range(3):
                nc.vector.tensor_copy(taps[:, n, :, 1:4, :], stage[:, n, :].rearrange("p (c y x) -> p x y c", y=3, x=3))
            nc.vector.memset(minus_half[:], -0.5)
            link(nc.vector.memset(ones[:], 1.0))
            ones_done = n_ch[0]
            for n in range(3):
                for counter in (conv_done[n], bhi_ready[n], blo_ready[n]):
                    dve.sem_inc(counter, CREDIT)
                dve.sem_inc(lo_ready[n], 1)
            for counter in (x1_ready, x1_stat, *stored.values()):
                dve.sem_inc(counter, 1)
            nc.vector.memset(dev[:, 0:1], 0.0).then_inc(zeroed, 1)
            dve.wait_ge(ach, 1)
            link(nc.vector.tensor_scalar(alpha[:], norms[:], 1e-15, None, ALU.max))
            link(nc.vector.tensor_tensor(final_scale[:], alpha[:, 0:1], alpha[:, 1:2], ALU.mult))
            link(nc.vector.scalar_tensor_tensor(final_scale[:], final_scale[:], HALF / WSCALE, alpha[:, 2:3], ALU.mult, ALU.mult))
            link(nc.vector.reciprocal(alpha[:], alpha[:]))
            link(nc.vector.tensor_scalar(alpha[:], alpha[:], WSCALE, None, ALU.mult))
            for k in range(18):
                n, m, dx = k // 6, (k // 3) % 2, k % 3
                dve.wait_ge(tr_done, k + 1)
                src = (prep_ps, prep_ps2)[k % 2]
                nc.vector.tensor_scalar(ex[n][:, :, 2 * dx + m, :], src[:, 0:P].rearrange("p (e o) -> p e o", e=E),
                                        alpha[:, n:n + 1], None, ALU.mult).then_inc(ex_done, 1)
            dve.wait_ge(loaded, 6 * 16)
            for q in range(Q):
                nc.vector.tensor_scalar(wc1r[:, q * C:(q + 1) * C], wc1_in[:], 0.25, None, ALU.mult)
            nc.vector.memset(dev[:, 1:2], 0.0).then_inc(tiny, 1)
            dve.wait_ge(tr_done, 19)
            link(nc.vector.tensor_copy(wc1t[:], prep_ps[:, 0:8]))
            nc.vector.tensor_copy(wc2t[:], prep_ps2[0:8, 0:P]).then_inc(tiny, 1)
            dve.wait_ge(tiny, 2)
            dve.wait_ge(first_in, 64)
            for k in range(32):
                ins = nc.vector.bn_stats(bn0[:, k, :], first[:, k // 4, (k % 4) * 512:(k % 4 + 1) * 512])
            link(ins)

            dk = [0]

            def chain(ins, n_before):
                dk[0] += 1
                ins.then_inc(dch, 1)
                dve.wait_ge(dch, n_before + dk[0])

            def take_mean(k, nb):
                dve.sem_inc(passed, 1)
                nc.vector.bn_aggr(mv[:], bn0[:].rearrange("p a b -> p (a b)")).then_inc(mean_ready, 1)
                dve.wait_ge(mean_ready, k + 1)

            def take_dev(k, nb):
                dve.wait_ge(gm_ready, k + 1)
                chain(nc.vector.tensor_tensor(dev[:, 0:1], mv[:, 0:1], prep_ps[:, 0:1], ALU.subtract), nb)
                chain(nc.vector.tensor_copy(me[:, 0:1], mv[:, 0:1]), nb)
                nc.vector.scalar_tensor_tensor(me[:, 1:2], dev[:, 0:1], dev[:, 0:1], mv[:, 1:2], ALU.mult, ALU.add
                                               ).then_inc(e_ready, 1)

            def take_moments(k, nb):
                dve.wait_ge(stq_ps, k + 1)
                chain(nc.vector.tensor_copy(stq[:, 0:2], prep_ps2[:, 0:2]), nb)
                nc.vector.tensor_copy(stq[:, 2:3], prep_ps[:, 0:1]).then_inc(stq_ready, 1)

            def take_hidden(k, nb):
                dve.wait_ge(hid_ps, k + 1)
                nc.vector.tensor_scalar(hbs[:], prep_ps[0:8, 0:P], 0.0, None, ALU.max).then_inc(hid_ready, 1)

            def take_logits(k, nb):
                dve.wait_ge(log_ps, k + 1)
                lp = prep_ps2[:, 0:P].rearrange("p (o e) -> p o e", e=E)
                chain(nc.vector.tensor_reduce(mx[:], lp, AX.X, ALU.max), nb)
                nc.vector.tensor_tensor(lg[:], lp, mx[:].unsqueeze(2).to_broadcast([P, C, E]), ALU.subtract
                                        ).then_inc(lg_ready, 1)

            def take_coeff(k, nb):
                dve.wait_ge(exp_ready, k + 1)
                chain(nc.vector.tensor_reduce(den[:], ex_l[:], AX.X, ALU.add), nb)
                chain(nc.vector.reciprocal(rden[:], den[:]), nb)
                nc.vector.tensor_tensor(coeff[:].rearrange("p e o -> p o e"), ex_l[:],
                                        rden[:].unsqueeze(2).to_broadcast([P, C, E]), ALU.mult).then_inc(coeff_ready, 1)

            def b_ring(n, slot, count):
                dve.wait_ge(lo_ready[n], count + 1 + 1)
                dve.wait_ge(conv_done[n], count - 2 + CREDIT)
                copy_b(nc.vector.tensor_copy, n, "lo", slot).then_inc(blo_ready[n], 1)

            def lo(n, t, edges, count):
                dve.wait_ge(hi_ready[n], count + 1)
                dve.wait_ge(conv_done[n], count - 2 + CREDIT)
                slot, src = t % SLOTS, bank[n - 1][t % 2]
                base = 1.0 / WSCALE if n == 1 else 1.0 / (WSCALE * HALF)
                for b, k, sc in spans(n, edges, base):
                    at = lambda kind: ring[n][kind][:, slot * CHUNK + b:slot * CHUNK + b + k, 1:1 + IMG]
                    last = nc.vector.scalar_tensor_tensor(at("Alo"), src[:, b * IMG:(b + k) * IMG].rearrange("p (b w) -> p b w", b=k),
                                                          sc, at("Ahi"), ALU.mult, ALU.subtract)
                last.then_inc(lo_ready[n], 1)
                b_ring(n, slot, count)

            def x1(t, buf, at_block, uses, bn_slot, count):
                dve.wait_ge(conv_done[2], count + (1 + CREDIT))
                if uses is not None:
                    dve.wait_ge(res_here[buf], uses * 64 + 64)
                    dve.wait_ge(stored[buf], uses * 64 + 1)
                dst = out[buf][:, at_block:at_block + CHUNK, :]
                nc.vector.scalar_tensor_tensor(dst, bank[2][t % 2][:].rearrange("p (b w) -> p b w", b=CHUNK),
                                               final_scale[:], res[buf][:, at_block:at_block + CHUNK, :],
                                               ALU.mult, ALU.add).then_inc(x1_ready, 1)
                dve.wait_ge(x1_ready, count + 1 + 1)
                if t == 0:
                    nc.vector.bn_stats(bn1[:, 0, :], out[buf][:, 1, :])
                    last = nc.vector.bn_stats(bn1[96:128, 32, :], out[buf][96:128, 0, :])
                elif t == NCH - 1:
                    last = nc.vector.bn_stats(bn1[0:96, 32, :], out[buf][0:96, 2, :])
                else:
                    last = nc.vector.bn_stats(bn_slot, out[buf][:, at_block:at_block + CHUNK, :])
                last.then_inc(x1_stat, 1)

            def step(n0, t, x1_args=None, edges=False, extra=None):
                if t < NCH:
                    lo(1, t, t if edges else None, n0 + t)
                if extra is not None:
                    extra[0](*extra[1:])
                if t + 1 < NCH:
                    b_ring(0, (t + 1) % SLOTS, n0 + (t + 1))
                if 0 <= t - 1 < NCH:
                    lo(2, t - 1, (t - 1) if edges else None, n0 + (t - 1))
                if 0 <= t - 2:
                    x1(t - 2, *x1_args, n0 + (t - 2))

            nb0 = n_ch[0]
            take_mean(0, nb0)
            take_dev(0, nb0)
            take_moments(0, nb0)
            take_hidden(0, nb0)
            take_logits(0, nb0)
            take_coeff(0, nb0)
            before = nb0 + dk[0]
            per_sample = dk[0] + 1
            with dve.Fori(0, S) as s:
                n0 = dve.snap(s * NCH)
                k1 = dve.snap(s + 1)
                nb = dve.snap(s * per_sample + before)
                dk[0] = 0
                if True:
                    dve.wait_ge(x1_stat, n0 + 1)
                b_ring(0, 0, n0)
                step(n0, 0, edges=True)
                step(n0, 1, edges=True)
                step(n0, 2, ("C", 0, s, None), edges=True)
                with dve.Fori(0, 4) as i:
                    ni = dve.snap(n0 + i * 6)
                    for t in range(3, 9):
                        buf, first_t, k = ("A", 3, 0) if t < 6 else ("B", 6, 1)
                        st = 4 * (2 * i + k)
                        if t == first_t:
                            dve.wait_ge(st_here[buf], s * 64 + i * 16 + 16)
                        for c in ((0, 1), (2,), (3,))[t - first_t]:
                            ins = nc.vector.bn_stats(bn0[:, bass.ds(i * 8 + (4 * k + c), 1), :], st_in[buf][:, c, :])
                        if t - first_t == 2:
                            ins.then_inc(stat_read, 1)
                        step(ni, t, (buf, 2 * (t - first_t), s * 5 + i if t == first_t else None,
                                     bn1[:, bass.ds(i * 6 + (t - 2), 1), :]))
                dve.wait_ge(stat_read, s * 8 + 8)
                take_mean(k1, nb)
                for t in range(27, NCH + 2):
                    buf, first_t = ("A", 27) if t < 30 else ("B", 30) if t < 33 else ("D", 33)
                    u = None if t != first_t else s if buf == "D" else s * 5 + 4
                    extra = {28: (take_dev, k1, nb), 29: (take_hidden, k1, nb), 30: (take_logits, k1, nb),
                             31: (take_coeff, k1, nb)}.get(t)
                    if t == 27:
                        step(n0, t, (buf, 2 * (t - first_t), u, bn1[:, t - 2, :]), edges=True)
                        take_dev(k1, nb)
                        continue
                    if t == 28:
                        extra = (take_moments, k1, nb)
                    step(n0, t, (buf, 2 * (t - first_t), u, bn1[:, t - 2, :] if t - 2 < 32 else None), edges=True, extra=extra)
                dve.wait_ge(x1_stat, n0 + NCH + 1)
                dve.sem_inc(passed, 1)
                chain(nc.vector.bn_aggr(mv1_now[:], bn1[:].rearrange("p a b -> p (a b)")), nb)
                nc.vector.tensor_copy(mv1[:, bass.ds(s, 1), :].rearrange("p a b -> p (a b)"), mv1_now[:]).then_inc(bn1_aggr, 1)
                dve.wait_ge(bn1_aggr, k1)
                assert dk[0] == per_sample

        @block.gpsimd
        def _(pool):
            pool.wait_ge(sq_done, 3)
            nc.gpsimd.partition_all_reduce(maxsq[:], sumsq[:], P, bass.bass_isa.ReduceOp.max).then_inc(mx_done, 1)
            pool.wait_ge(ex_done, 18)

            def norms_of(k, pb):
                pool.wait_ge(stq_ready, k + 1)
                pool.sem_inc(passed, 1)
                link(nc.gpsimd.tensor_scalar(var_eps[:], stq[:, 1:2], EPS, None, ALU.add), pb)
                link(nc.gpsimd.tensor_tensor(norm_next[:, 0:1], var_eps[:], minus_half[:], ALU.pow), pb)
                link(nc.gpsimd.tensor_scalar(norm_next[:, 1:2], stq[:, 0:1], norm_next[:, 0:1], -1.0, ALU.mult, ALU.mult), pb)
                link(nc.gpsimd.tensor_scalar(gap[:], stq[:, 2:3], norm_next[:, 0:1], norm_next[:, 1:2], ALU.mult, ALU.add), pb)
                nc.gpsimd.tensor_scalar(gapb[:], ones[:], gap[:], None, ALU.mult).then_inc(gap_ready, 1)
                pool.wait_ge(gap_ready, k + 1)
                pool.sem_inc(passed, 1)

            pk = [0]

            def link(ins, before):
                pk[0] += 1
                ins.then_inc(pch, 1)
                pool.wait_ge(pch, before + pk[0])
                pool.sem_inc(passed, 1)

            def weights(n, s1, all_done, pb):
                link(nc.gpsimd.tensor_tensor(mixed[:], ex[n][:], coeff[:].unsqueeze(2).to_broadcast([P, E, 6, C]), ALU.mult), pb)
                link(nc.gpsimd.tensor_tensor(mixed[:, 0:2], mixed[:, 0:2], mixed[:, 2:4], ALU.add), pb)
                link(nc.gpsimd.tensor_tensor(mixed[:, 0:1], mixed[:, 0:1], mixed[:, 1:2], ALU.add), pb)
                pool.wait_ge(conv_done[n], all_done + CREDIT)
                pool.sem_inc(passed, 1)
                m = mixed[:, 0].rearrange("p a o -> p (a o)")
                link(nc.gpsimd.tensor_scalar(whi[n][:], m, 1.0, None, ALU.mult), pb)
                nc.gpsimd.tensor_tensor(wlo[n][:], m, whi[n][:], ALU.subtract).then_inc(w_ready[n], 1)
                pool.wait_ge(w_ready[n], s1)
                pool.sem_inc(passed, 1)

            def normalise(t, buf, at_block, here, count, pb):
                if here is not None:
                    pool.wait_ge(x_here[buf], here)
                pool.wait_ge(lo_ready[0], count + 1)
                pool.wait_ge(conv_done[0], count - 2 + CREDIT)
                pool.wait_ge(bhi_ready[0], count - 1 + CREDIT)
                pool.wait_ge(blo_ready[0], count - 1 + CREDIT)
                pool.sem_inc(passed, 1)
                s0 = (t % SLOTS) * CHUNK
                hi, lo = (ring[0][k][:, s0:s0 + CHUNK, 1:1 + IMG] for k in ("Ahi", "Alo"))
                if t == NCH - 1:
                    nc.gpsimd.memset(ring[0]["Ahi"][:, s0:s0 + CHUNK, :].rearrange("p a b -> p (a b)").bitcast(f32), 0.0).then_inc(hi_ready[0], 1)
                    nc.gpsimd.memset(ring[0]["Alo"][:, s0:s0 + CHUNK, :].rearrange("p a b -> p (a b)").bitcast(f32), 0.0).then_inc(lo_ready[0], 1)
                    return
                src = x_in[buf][:, at_block:at_block + CHUNK, :]
                nc.gpsimd.tensor_scalar(hi, src, norm_now[:, 0:1], norm_now[:, 1:2], ALU.mult, ALU.add).then_inc(hi_ready[0], 1)
                link(nc.gpsimd.tensor_scalar(xn[:], src, norm_now[:, 0:1], norm_now[:, 1:2], ALU.mult, ALU.add), pb)
                pool.wait_ge(hi_ready[0], count + 1)
                nc.gpsimd.tensor_tensor(lo, xn[:], hi, ALU.subtract).then_inc(lo_ready[0], 1)

            norms_of(0, 0)
            before = pk[0]
            pk[0] = 0
            in_loop = 6
            after_loop = [0]
            with pool.Fori(0, S) as s:
                s1 = pool.snap(s + 1)
                n0 = pool.snap(s * NCH)
                total = 1 + 3 * 4 + 3 + 4 * in_loop + 5 + 4
                pb = pool.snap(s * total + before)
                pool.wait_ge(coeff_ready, s1)
                pool.wait_ge(lo_ready[0], n0 + 1)
                pool.sem_inc(passed, 1)
                link(nc.gpsimd.tensor_scalar(norm_now[:], norm_next[:], 1.0, None, ALU.mult), pb)
                for t in range(3):
                    weights(t, s1, n0, pb)
                    normalise(t, "C", 2 * t, s * 64 + 64 if t == 0 else None, n0 + t, pb)
                base = pk[0]
                with pool.Fori(0, 4) as i:
                    ni = pool.snap(n0 + i * 6)
                    pi = pool.snap(pb + i * in_loop)
                    for t in range(3, 9):
                        buf, first_t = ("A", 3) if t < 6 else ("B", 6)
                        normalise(t, buf, 2 * (t - first_t), s * 320 + i * 64 + 64 if t == first_t else None, ni + t, pi)
                assert pk[0] == base + in_loop
                pk[0] = base + 4 * in_loop
                for t in range(27, NCH):
                    buf, first_t = ("A", 27) if t < 30 else ("B", 30)
                    normalise(t, buf, 2 * (t - first_t), s * 320 + 320 if t == first_t else None, n0 + t, pb)
                    if t == 30:
                        norms_of(s1, pb)
                assert pk[0] == total, pk[0]
                pk[0] = 0


M = 64
KY = 16


def spectral_constants():
    k = np.arange(M) + (IMG // 2 - M // 2)
    ang = 2 * np.pi * ((np.arange(IMG)[:, None] * k[None, :]) % IMG) / IMG
    c, s = np.cos(ang), np.sin(ang)
    half = lambda a: a.reshape(2, P, -1).transpose(1, 0, 2).reshape(P, -1)
    along_h = np.concatenate([c[:P, 0::2], s[:P, 0::2], c[:P, 1::2], s[:P, 1::2]], 1)
    cos_part = half(np.concatenate([c, s], 1))
    sin_part = half(np.concatenate([-s, c], 1))
    back_h = np.concatenate([c.T, s.T], 0)
    back_w = np.concatenate([(c + s).T, (c - s).T], 0) / (IMG * IMG)
    q, cc = np.arange(P) // C, np.arange(P) % C
    groupq = (cc[:, None] // 2 == cc[None, :] // 2) / 8.0
    pick = (q[:, None] == 0) & (cc[:, None] == np.arange(C)[None, :])
    return np.concatenate([along_h, cos_part, sin_part, back_h, back_w, groupq, pick], axis=1).astype(np.float32)


OFF_W, OFF_BACK = P, 5 * P
OFF_GROUP = OFF_BACK + 2 * IMG
OFF_PICK = OFF_GROUP + P
NSPEC = OFF_PICK + C


def build_forward(nc, x1d, stats_d, spec, f_d, S):
    f32 = mybir.dt.float32
    ALU, ACT = mybir.AluOpType, mybir.ActivationFunctionType
    with ExitStack() as ctx:
        sb = lambda n, s: ctx.enter_context(nc.sbuf_tensor("f_" + n, s, f32))
        ps = lambda n, s: ctx.enter_context(nc.psum_tensor("f_" + n, s, f32))
        sem = lambda n: ctx.enter_context(nc.semaphore("f_" + n))
        cst = sb("cst", [P, NSPEC])
        along_h = lambda parity: cst[:, parity * M:(parity + 1) * M]
        part_w = lambda cs, wc: cst[:, OFF_W + (2 * cs + wc) * P:OFF_W + (2 * cs + wc + 1) * P]
        groupq = cst[:, OFF_GROUP:OFF_GROUP + P]
        pick = cst[:, OFF_PICK:OFF_PICK + C]
        mv = sb("mv", [P, S, 2])
        gm = sb("gm", [P, 2, S])
        dev = sb("dev", [P, S])
        var = sb("var", [P, S])
        expo = sb("expo", [P, S])
        ones = sb("ones", [P, P])
        spread = sb("spread", [P, 2, S, C])
        norm = sb("norm", [P, 2, S, C])
        mean_now = sb("mean_now", [P, C])
        rs_now = sb("rs_now", [P, C])
        xt = [sb(f"xt{i}", [P, 2, 4, IMG]) for i in range(2)]
        xg = [sb(f"xg{i}", [P, 2, 4, IMG]) for i in range(2)]
        y = [sb(f"y{i}", [P, 2, 2, 4, M]) for i in range(2)]
        fs = [sb(f"fs{i}", [P, 8, P]) for i in range(2)]
        b1 = [[ps(f"b1{i}{j}", [P, 512]) for j in range(2)] for i in range(2)]
        b2 = [ps(f"b2{i}", [P, 512]) for i in range(2)]
        bs = [ps(f"bs{i}", [P, 512]) for i in range(2)]
        here, pch, dch, pw, sp_ready, now_ready, prep, norm_ready, rs_ready = (
            sem(n) for n in ("here", "pch", "dch", "pw", "sp_ready", "now_ready", "prep", "norm_ready", "rs_ready"))
        x_here = [sem(f"x_here{i}") for i in range(2)]
        xg_ready = [sem(f"xg_ready{i}") for i in range(2)]
        y_ps = [sem(f"y_ps{i}") for i in range(2)]
        y_ready = [sem(f"y_ready{i}") for i in range(2)]
        f_ps = [sem(f"f_ps{i}") for i in range(2)]
        f_ready = [sem(f"f_ready{i}") for i in range(2)]
        f_out = [sem(f"f_out{i}") for i in range(2)]
        block = ctx.enter_context(nc.Block())
        xv = x1d.rearrange("s c (a p) w -> s a p c w", p=P)
        fv = f_d.rearrange("s (k c) (r a) n -> s c a r k n", c=2, a=2)

        @block.sync
        def _(sp):
            sp.dma_start(cst[:], spec).then_inc(here, 16)
            sp.dma_start(mv[:], stats_d).then_inc(here, 16)

            def load(buf, s, c0):
                for a in range(2):
                    sp.dma_start(xt[buf][:, a], xv[s, a, :, bass.ds(c0, 4), :]).then_inc(x_here[buf], 16)

            with sp.Fori(0, S) as s:
                with sp.Fori(0, 4) as i:
                    n = sp.snap(s * 4 + i)
                    for buf in range(2):
                        sp.wait_ge(xg_ready[buf], n + 1)
                        load(buf, s, i * 8 + 4 * buf)
            for buf in range(2):
                sp.wait_ge(x_here[buf], 32 * 4 * S)

        @block.tensor
        def _(pe):
            pe.wait_ge(here, 32)
            nc.tensor.matmul(bs[0][:, 0:S], groupq, mv[:, :, 0], start=True, stop=True).then_inc(pw, 1)
            pe.wait_ge(prep, 1)
            nc.tensor.matmul(bs[1][:, 0:S], groupq, var[:], start=True, stop=True).then_inc(pw, 1)
            pe.wait_ge(sp_ready, 1)
            nc.tensor.matmul(bs[0][:, 0:S * C], ones[:], spread[:, 0].rearrange("p s c -> p (s c)"), start=True, stop=True)
            nc.tensor.matmul(bs[1][:, 0:S * C], ones[:], spread[:, 1].rearrange("p s c -> p (s c)"), start=True, stop=True).then_inc(pw, 1)

            def over_h(buf, n):
                pe.wait_ge(xg_ready[buf], n + 1 + 1)
                pe.wait_ge(y_ready[buf], n * 2 + 1)
                for c in range(4):
                    for wc in range(2):
                        for a in range(2):
                            at = ((wc * 2 + c % 2) * 2 + a) * M
                            last = nc.tensor.matmul(b1[buf][c // 2][:, at:at + M], xg[buf][:, a, c, wc * P:(wc + 1) * P],
                                                    along_h(a), start=True, stop=True)
                    if c % 2:
                        last.then_inc(y_ps[buf], 1)

            def over_w(buf, n):
                pe.wait_ge(y_ready[buf], n * 2 + 2 + 1)
                pe.wait_ge(f_ready[buf], n + 1)
                for pair in range(2):
                    for k in range(4):
                        cs, wc = k // 2, k % 2
                        last = nc.tensor.matmul(b2[buf][:, pair * P:(pair + 1) * P],
                                                y[buf][:, wc, cs, 2 * pair:2 * pair + 2, :].rearrange("p c k -> p (c k)"),
                                                part_w(cs, wc), start=(k == 0), stop=(k == 3))
                last.then_inc(f_ps[buf], 1)

            with pe.Fori(0, S * 4) as n:
                over_h(0, n)
                over_h(1, n)
                over_w(0, n)
                over_w(1, n)

        @block.vector
        def _(dve):
            k = [0]

            def link(ins):
                k[0] += 1
                ins.then_inc(dch, 1)
                dve.wait_ge(dch, k[0])

            for counters in (f_out, f_ps, xg_ready, y_ps, f_ready, y_ready):
                for counter in counters:
                    dve.sem_inc(counter, 1)
            nc.vector.memset(ones[:], 1.0)
            link(nc.vector.memset(expo[:], -0.5))
            dve.wait_ge(here, 32)
            dve.wait_ge(pw, 1)
            link(nc.vector.tensor_copy(gm[:, 0], bs[0][:, 0:S]))
            link(nc.vector.tensor_tensor(dev[:], mv[:, :, 0], gm[:, 0], ALU.subtract))
            link(nc.vector.tensor_tensor(dev[:], dev[:], dev[:], ALU.mult))
            nc.vector.tensor_tensor(var[:], dev[:], mv[:, :, 1], ALU.add).then_inc(prep, 1)
            dve.wait_ge(pw, 2)
            nc.vector.tensor_scalar(dev[:], bs[1][:, 0:S], EPS, None, ALU.add).then_inc(prep, 1)
            dve.wait_ge(pch, 1)
            bc = lambda i: gm[:, i].unsqueeze(2).to_broadcast([P, S, C])
            pb = pick.unsqueeze(1).to_broadcast([P, S, C])
            nc.vector.tensor_tensor(spread[:, 0], bc(0), pb, ALU.mult)
            nc.vector.tensor_tensor(spread[:, 1], bc(1), pb, ALU.mult).then_inc(sp_ready, 1)
            dve.wait_ge(pw, 3)
            link(nc.vector.tensor_scalar(norm[:, 0].rearrange("p s c -> p (s c)"), bs[0][:, 0:S * C], 2.0, None, ALU.mult))
            nc.vector.tensor_copy(norm[:, 1].rearrange("p s c -> p (s c)"), bs[1][:, 0:S * C]).then_inc(norm_ready, 1)
            dve.wait_ge(norm_ready, 1)
            with dve.Fori(0, S) as s:
                dve.wait_ge(xg_ready[0], s * 4 + 1)
                dve.wait_ge(xg_ready[1], s * 4 + 1)
                nc.vector.tensor_copy(mean_now[:], norm[:, 0, bass.ds(s, 1), :].rearrange("p a c -> p (a c)")).then_inc(now_ready, 1)
                dve.wait_ge(now_ready, s + 1)
                for i in range(4):
                    n = dve.snap(s * 4 + i)
                    for buf in range(2):
                        dve.wait_ge(x_here[buf], n * 32 + 32)
                        dve.wait_ge(y_ps[buf], n * 2 + 1)
                        for c in range(0, 4, 2):
                            ch = i * 8 + buf * 4 + c
                            nc.vector.scalar_tensor_tensor(xg[buf][:, 0, c:c + 2, :], xt[buf][:, 0, c:c + 2, :], mean_now[:, ch:ch + 1],
                                                           xt[buf][:, 1, c:c + 2, :], ALU.subtract, ALU.add)
                        nc.vector.tensor_tensor(xg[buf][:, 1], xt[buf][:, 0], xt[buf][:, 1], ALU.subtract).then_inc(xg_ready[buf], 1)

        @block.gpsimd
        def _(pool):
            pool.wait_ge(prep, 2)
            nc.gpsimd.tensor_tensor(gm[:, 1], dev[:], expo[:], ALU.pow).then_inc(pch, 1)

        @block.scalar
        def _(act):
            def copy_y(buf, n):
                for j in range(2):
                    act.wait_ge(y_ps[buf], n * 2 + (j + 1) + 1)
                    act.wait_ge(f_ps[buf], n + 1)
                    for cs in range(2):
                        last = nc.scalar.copy(y[buf][:, :, cs, 2 * j:2 * j + 2, :].rearrange("p x c (a k) -> p x (c a) k", a=2),
                                              b1[buf][j][:].rearrange("p (x c t k) -> p t x c k", x=2, c=4, t=2)[:, cs])
                    last.then_inc(y_ready[buf], 1)

            def copy_f(buf, n, half, i):
                act.wait_ge(f_ps[buf], n + 1 + 1)
                for pair in range(2):
                    k = i * 4 + 2 * buf + pair
                    last = nc.scalar.activation(fs[half][:, k, :], b2[buf][:, pair * P:(pair + 1) * P], ACT.Copy,
                                                scale=rs_now[:, 2 * (8 * half + k):2 * (8 * half + k) + 1])
                last.then_inc(f_ready[buf], 1)

            with act.Fori(0, S) as s:
                act.wait_ge(norm_ready, 1)
                nc.scalar.copy(rs_now[:], norm[:, 1, bass.ds(s, 1), :].rearrange("p a c -> p (a c)")).then_inc(rs_ready, 1)
                act.wait_ge(rs_ready, s + 1)
                for half in range(2):
                    act.wait_ge(f_out[half], s * 64 + 1)
                    for i in range(2):
                        n = act.snap(s * 4 + (half * 2 + i))
                        copy_y(0, n)
                        copy_y(1, n)
                        copy_f(0, n, half, i)
                        copy_f(1, n, half, i)
                    n1 = act.snap(s * 4 + (half * 2 + 2))
                    act.wait_ge(f_ready[0], n1 + 1)
                    act.wait_ge(f_ready[1], n1 + 1)
                    for c in range(2):
                        for a in range(2):
                            p0 = c * M + a * 32
                            act.dma_start(fv[s, c, a, :, 8 * half:8 * half + 8, :], fs[half][p0:p0 + 32]).then_inc(f_out[half], 16)
            for half in range(2):
                act.wait_ge(f_out[half], 64 * S + 1)


def build_mix(nc, f_d, w, t_d, S):
    f32 = mybir.dt.float32
    T = 4
    with ExitStack() as ctx:
        sb = lambda n, s: ctx.enter_context(nc.sbuf_tensor("m_" + n, s, f32))
        ps = lambda n, s: ctx.enter_context(nc.psum_tensor("m_" + n, s, f32))
        sem = lambda n: ctx.enter_context(nc.semaphore("m_" + n))
        ft = [sb(f"ft{i}", [P, S, T, M]) for i in range(2)]
        wt = [sb(f"wt{i}", [P, C, T, M]) for i in range(2)]
        wr = sb("wr", [P, C, T, M])
        to = [sb(f"to{i}", [P, S, M]) for i in range(2)]
        bank = [[[ps(f"bank{i}{g}{h}", [P, 512]) for h in range(2)] for g in range(2)] for i in range(2)]
        here = [sem(f"here{i}") for i in range(2)]
        wr_here, turned, emptied, passed = (sem(n) for n in ("wr_here", "turned", "emptied", "passed"))
        done = sem("done")
        packed = [sem(f"packed{g}") for g in range(2)]
        gone = [sem(f"gone{g}") for g in range(2)]
        block = ctx.enter_context(nc.Block())
        NCK = M // 2 // T
        re = lambda g: slice(g * M, g * M + C)
        im = lambda g: slice(g * M + C, (g + 1) * M)

        @block.sync
        def _(sp):
            for k in range(NCK):
                buf = k % 2
                if k >= 2:
                    sp.wait_ge(done, k - 1)
                for g in range(2):
                    y0 = 32 * g + T * k
                    for part, p in ((0, re(g)), (1, im(g))):
                        for t in range(T):
                            sp.dma_start(ft[buf][p, :, t, :], f_d[:, :, y0 + t, part * M:(part + 1) * M].rearrange("b i n -> i b n")
                                         ).then_inc(here[buf], 16)
                    sp.dma_start(wt[buf][re(g)], w[:, :, y0:y0 + T, :].rearrange("i o t x -> i o (t x)")).then_inc(here[buf], 16)
                if k:
                    sp.wait_ge(turned, k)
                for g in range(2):
                    y0 = 32 * g + T * k
                    lo, n = M - y0 - T + 1, T if y0 else T - 1
                    sp.dma_start(wr[im(g), :, 0:n], w[:, :, lo:lo + n, :].rearrange("i o t x -> i o (t x)")).then_inc(wr_here, 16)
                    if n < T:
                        sp.dma_start(wr[im(g), :, n], w[:, :, 0, :]).then_inc(wr_here, 16)
            for g in range(2):
                sp.wait_ge(gone[g], 16 * NCK)

        @block.tensor
        def _(pe):
            def chunk(buf, n):
                for kx in range(M):
                    half, col = kx // 32, (kx % 32) * S
                    for t in range(T):
                        for g in range(2):
                            pg = slice(g * M, (g + 1) * M)
                            last = nc.tensor.matmul(bank[buf][g][half][t * C:(t + 1) * C, col:col + S], wt[buf][pg, :, t, kx],
                                                    ft[buf][pg, :, t, kx], start=True, stop=True)
                last.then_inc(done, 1)

            with pe.Fori(1, NCK // 2 + 1) as k2:
                for buf in range(2):
                    pe.wait_ge(here[buf], k2 * (18 * 16))
                    pe.wait_ge(turned, k2 * 2 + (buf - 1))
                    pe.wait_ge(emptied, k2 * 2 + (buf - 1))
                    pe.sem_inc(passed, 1)
                    chunk(buf, k2)

        @block.vector
        def _(dve):
            dve.sem_inc(emptied, 2)

            def turn(k):
                dve.wait_ge(wr_here, 16 * (2 * k + 3))
                if k >= 2:
                    dve.wait_ge(done, k - 1)
                for g in range(2):
                    for t in range(T):
                        p, dst, src = im(g), wt[k % 2][im(g), :, t, :], wr[im(g), :, T - 1 - t, :]
                        nc.vector.tensor_copy(dst[:, :, 0:1], src[:, :, 0:1])
                        last = nc.vector.tensor_copy(dst[:, :, 1:M], src[:, :, :0:-1])
                last.then_inc(turned, 1)

            def pack(k):
                for g in range(2):
                    dve.wait_ge(done, k + 1)
                    if k:
                        dve.wait_ge(gone[g], 16 * k)
                    for half in range(2):
                        last = nc.vector.tensor_copy(to[g][:, :, 32 * half:32 * half + 32],
                                                     bank[k % 2][g][half][:, 0:32 * S].rearrange("p (x b) -> p b x", b=S))
                    last.then_inc(packed[g] if g == 0 else emptied, 1)

            turn(0)
            for k in range(NCK):
                if k + 1 < NCK:
                    turn(k + 1)
                pack(k)

        @block.scalar
        def _(act):
            for k in range(NCK):
                for g in range(2):
                    y0 = 32 * g + k * T
                    if g == 0:
                        act.wait_ge(packed[0], k + 1)
                    else:
                        act.wait_ge(emptied, k + 3)
                    act.dma_start(t_d[:, y0:y0 + T].rearrange("b t o x -> (t o) b x"), to[g][:]).then_inc(gone[g], 16)


def build_inverse(nc, t_d, x1d, bias, spec, out_d, S):
    f32 = mybir.dt.float32
    ALU = mybir.AluOpType
    NB = 4
    with ExitStack() as ctx:
        sb = lambda n, s: ctx.enter_context(nc.sbuf_tensor("i_" + n, s, f32))
        ps = lambda n, s: ctx.enter_context(nc.psum_tensor("i_" + n, s, f32))
        sem = lambda n: ctx.enter_context(nc.semaphore("i_" + n))
        back = sb("back", [P, 2 * IMG])
        back_h, back_w = back[:, 0:IMG], back[:, IMG:2 * IMG]
        bias_bc = sb("bias_bc", [P, C])
        t2 = [sb(f"t2{i}", [P, 16, P]) for i in range(2)]
        u = [sb(f"u{i}", [P, IMG]) for i in range(2)]
        xt = [sb(f"xt{i}", [P, 2, 4, IMG]) for i in range(NB)]
        ot = [sb(f"ot{i}", [P, 2, 4, IMG]) for i in range(NB)]
        ub = [ps(f"ub{i}", [P, 512]) for i in range(2)]
        ob = [ps(f"ob{i}", [P, 512]) for i in range(4)]
        here, zeroed, u_ps, u_ready, o_ps, o_ready = (sem(n) for n in ("here", "zeroed", "u_ps", "u_ready", "o_ps", "o_ready"))
        t_here = [sem(f"t_here{i}") for i in range(2)]
        x_here = [sem(f"x_here{i}") for i in range(NB)]
        gone = [sem(f"gone{i}") for i in range(NB)]
        block = ctx.enter_context(nc.Block())
        xv = x1d.rearrange("s c (a p) w -> s a p c w", p=P)
        ov = out_d.rearrange("s c (a p) w -> s a p c w", p=P)

        @block.sync
        def _(sp):
            sp.dma_start(back[:], spec[:, OFF_BACK:OFF_BACK + 2 * IMG]).then_inc(here, 16)
            sp.dma_start(bias_bc[:], bias.rearrange("c a b -> (a b) c").to_broadcast([P, C])).then_inc(here, 16)
            sp.wait_ge(zeroed, 1)
            with sp.Fori(0, S) as s:
                for g in range(8):
                    if g % 4 == 0:
                        h = g // 4
                        sp.wait_ge(u_ps, (s * 32 if h == 0 else s * 32) + 1)
                        for d in range(2):
                            sp.dma_start(t2[h][d * M:(d + 1) * M, :, d * M:(d + 1) * M], t_d[s, :, 16 * h:16 * h + 16, :]).then_inc(t_here[h], 16)
                    b = g % NB
                    sp.wait_ge(o_ready, (s * 32 + 4 * (g - NB) + 4 if g >= NB else s * 32) + 1)
                    for a in range(2):
                        sp.dma_start(xt[b][:, a], xv[s, a, :, 4 * g:4 * g + 4, :]).then_inc(x_here[b], 16)
            for b in range(NB):
                sp.wait_ge(gone[b], 32 * 2 * S + 1)

        @block.tensor
        def _(pe):
            pe.wait_ge(here, 32)

            def over_ky(c, n):
                pe.wait_ge(u_ready, (n - 1 if c else n) + 1)
                nc.tensor.matmul(ub[c % 2][:, 0:IMG], t2[c // 16][:, c % 16, :], back_h, start=True, stop=True).then_inc(u_ps, 1)

            with pe.Fori(0, S) as s:
                n0 = pe.snap(s * C)
                pe.wait_ge(t_here[0], s * 32 + 32)
                over_ky(0, n0)
                for c in range(C):
                    if c + 1 == 16:
                        pe.wait_ge(t_here[1], s * 32 + 32)
                    if c + 1 < C:
                        over_ky(c + 1, n0 + (c + 1))
                    pe.wait_ge(u_ready, n0 + (c + 1) + 1)
                    pe.wait_ge(o_ready, (n0 + (c - 3) if c >= 3 else n0) + 1)
                    for a in range(2):
                        last = nc.tensor.matmul(ob[c % 4][:, a * IMG:(a + 1) * IMG], u[c % 2][:, a * P:(a + 1) * P], back_w,
                                                start=True, stop=True)
                    last.then_inc(o_ps, 1)

        @block.scalar
        def _(act):
            def store(s, n0, g):
                act.wait_ge(o_ready, n0 + (4 * g + 5))
                for a in range(2):
                    act.dma_start(ov[s, a, :, 4 * g:4 * g + 4, :], ot[g % NB][:, a]).then_inc(gone[g % NB], 16)

            with act.Fori(0, S) as s:
                n0 = act.snap(s * C)
                for c in range(C):
                    act.wait_ge(u_ps, n0 + (c + 1) + 1)
                    act.wait_ge(o_ps, (n0 + (c - 1) if c else n0) + 1)
                    nc.scalar.copy(u[c % 2][:], ub[c % 2][:, 0:IMG]).then_inc(u_ready, 1)
                    if c % 4 == 2 and c > 4:
                        store(s, n0, c // 4 - 1)
                store(s, n0, C // 4 - 1)

        @block.vector
        def _(dve):
            for counter in (o_ps, o_ready, u_ready, u_ps, *gone):
                dve.sem_inc(counter, 1)
            nc.vector.memset(t2[0][:], 0.0)
            nc.vector.memset(t2[1][:], 0.0).then_inc(zeroed, 1)
            dve.wait_ge(zeroed, 1)
            dve.wait_ge(here, 32)
            with dve.Fori(0, S) as s:
                n0 = dve.snap(s * C)
                for c in range(C):
                    g = c // 4
                    b = g % NB
                    if c % 4 == 0:
                        dve.wait_ge(x_here[b], s * 64 + (g // NB) * 32 + 32)
                        dve.wait_ge(gone[b], s * 64 + (g // NB) * 32 + 1)
                    dve.wait_ge(o_ps, n0 + (c + 1) + 1)
                    nc.vector.scalar_tensor_tensor(ot[b][:, :, c % 4, :], ob[c % 4][:].rearrange("p (a w) -> p a w", a=2),
                                                   bias_bc[:, c:c + 1], xt[b][:, :, c % 4, :], ALU.add, ALU.add).then_inc(o_ready, 1)


def build(nc, x, w_c1, w_c2, weight1, weight2, weight3, mode_w, bias, consts, spec, out):
    f32, S = mybir.dt.float32, x.shape[0]
    scratch = lambda name, shape: nc.dram_tensor(name, shape, f32, kind="Internal").ap()
    x1 = scratch("x1", [S, C, IMG, IMG])
    x1_stats = scratch("x1_stats", [P, S, 2])
    modes = scratch("modes", [S, C, M, 2 * M])
    mixed_modes = scratch("mixed_modes", [S, M, C, M])
    build_convs(nc, x, w_c1, w_c2, weight1, weight2, weight3, consts, x1, x1_stats, S)
    build_forward(nc, x1, x1_stats, spec, modes, S)
    build_mix(nc, modes, mode_w, mixed_modes, S)
    build_inverse(nc, mixed_modes, x1, bias, spec, out, S)


_INS = ["x", "L0_conv_w_c1", "L0_conv_w_c2", "L0_conv_weight1", "L0_conv_weight2", "L0_conv_weight3",
        "L1_conv_weight", "L1_conv_bias"]


def kernel(**inputs):
    import concourse.bacc as bacc
    from concourse.bass_utils import run_bass_kernel_spmd

    nc = bacc.Bacc("TRN2", target_bir_lowering=False, num_devices=1)
    arrays = {f"in_{name}": np.ascontiguousarray(inputs[name]) for name in _INS}
    arrays["consts"] = constants()
    arrays["spec"] = spectral_constants()
    args = [nc.dram_tensor(n, a.shape, mybir.dt.from_np(a.dtype), kind="ExternalInput").ap() for n, a in arrays.items()]
    out = nc.dram_tensor("out", inputs["x"].shape, mybir.dt.float32, kind="ExternalOutput").ap()
    build(nc, *args, out)
    r = run_bass_kernel_spmd(nc, [arrays], core_ids=[0])
    return r.results[0]["out"]
```

```python
import numpy as np
import concourse.bass as bass
from concourse import mybir
from contextlib import ExitStack

P = 128
C = 32
IMG = 256
W2 = IMG + 2
E = 4
TAPS = 9
Q = 4
CHUNK = 2
NCH = 33
SLOTS = 3
CREDIT = 3
WSCALE = 1024.0
HALF = 2.0
TEMP = 30.0
EPS = 1e-5
MW = 3 * 64


def constants():
    c4 = np.arange(P) // 4
    cq = np.arange(P) % C
    same_group = (c4[:, None] // 2 == c4[None, :] // 2) / 8.0
    to_group = (c4[:, None] // 2 == cq[None, :] // 2) / 8.0
    to_channel = (c4[:, None] == cq[None, :]) / 4.0
    ident = np.eye(P)
    q = np.arange(P) // C
    masks = np.zeros((P, 8))
    masks[:, 0] = (q >= 1) / WSCALE
    masks[:, 1] = (q == 0) / WSCALE
    masks[:, 2] = (q >= 2) / (WSCALE * HALF)
    masks[:, 3] = (q <= 1) / (WSCALE * HALF)
    groupq = (cq[:, None] // 2 == cq[None, :] // 2) / 8.0
    return np.concatenate([same_group, to_group, to_channel, ident, groupq, masks], axis=1).astype(np.float32)


NCONST = 5 * P + 8


def build_convs(nc, x, w_c1, w_c2, w1, w2, w3, consts, x1d, stats1_d, S):
    f32, f16 = mybir.dt.float32, mybir.dt.float16
    ALU, ACT, AX = mybir.AluOpType, mybir.ActivationFunctionType, mybir.AxisListType
    experts_d = [w1, w2, w3]

    with ExitStack() as ctx:
        sb = lambda n, s, d=f32: ctx.enter_context(nc.sbuf_tensor(n, s, d))
        ps = lambda n, s, d=f32: ctx.enter_context(nc.psum_tensor(n, s, d))
        sem = lambda n: ctx.enter_context(nc.semaphore(n))

        cst = sb("cst", [P, NCONST])
        same_group, to_group, to_channel, ident = (cst[:, i * P:(i + 1) * P] for i in range(4))
        mask = lambda i: cst[:, 5 * P + i:5 * P + i + 1]
        zero = mask(4)

        x_in = {k: sb(f"x_in_{k}", [P, 6, IMG]) for k in "CAB"}
        st_in = {k: sb(f"st_in_{k}", [P, 4, 512]) for k in "AB"}
        res = {k: sb(f"res_{k}", [P, n, IMG]) for k, n in (("C", 2), ("A", 6), ("B", 6), ("D", 4))}
        out = {k: sb(f"out_{k}", [P, n, IMG]) for k, n in (("C", 2), ("A", 6), ("B", 6), ("D", 4))}
        ring = [{k: sb(f"ring{n}_{k}", [P, SLOTS * CHUNK, W2], f16) for k in ("Ahi", "Alo", "Bhi", "Blo")}
                for n in range(3)]
        xn = sb("xn", [P, CHUNK, IMG])
        ex = [sb(f"ex{n}", [P, E, 6, C]) for n in range(3)]
        mixed = sb("mixed", [P, E, 6, C])
        w_now = [sb(f"w_now{n}", [P, 2, MW], f16) for n in range(3)]
        w_next = [sb(f"w_next{n}", [P, 2, MW], f16) for n in range(3)]
        stage = sb("stage", [P, 3, C * TAPS])
        taps = sb("taps", [P, 3, 3, 5, C])
        sumsq = sb("sumsq", [P, 3])
        maxsq = sb("maxsq", [P, 3])
        norms = sb("norms", [P, 3])
        alpha = sb("alpha", [P, 3])
        final_scale = sb("final_scale", [P, 1])
        wc1_in = sb("wc1_in", [8, C])
        wc1t = sb("wc1t", [P, 8])
        wc1r = sb("wc1r", [8, P])
        wc2_in = sb("wc2_in", [P, 8])
        wc2t = sb("wc2t", [8, P])
        ones = sb("ones", [P, P])
        bn0 = sb("bn0", [P, 32, 6])
        bn1 = sb("bn1", [P, NCH, 6])
        mv = sb("mv", [P, 2])
        mv1 = sb("mv1", [P, S, 2])
        mv1_now = sb("mv1_now", [P, 2])
        dev = sb("dev", [P, 2])
        me = sb("me", [P, 2])
        stq = sb("stq", [P, 3])
        norm_next = sb("norm_next", [P, 2])
        norm_now = sb("norm_now", [P, 2])
        var_eps = sb("var_eps", [P, 1])
        minus_half = sb("minus_half", [P, 1])
        gap = sb("gap", [P, 1])
        gapb = sb("gapb", [P, P])
        hbs = sb("hbs", [8, P])
        mx = sb("mx", [P, C])
        lg = sb("lg", [P, C, E])
        ex_l = sb("ex_l", [P, C, E])
        den = sb("den", [P, C])
        rden = sb("rden", [P, C])
        coeff = sb("coeff", [P, E, C])
        first = sb("first", [P, 8, 512 * 4])

        bank = [[ps(f"bank{n}{i}", [P, 512]) for i in range(2)] for n in range(3)]
        prep_ps = ps("prep_ps", [P, 512])
        prep_ps2 = ps("prep_ps2", [P, 512])

        loaded, first_in, sq_done, mx_done, sc_done, tr_done, ex_done, zeroed, dch, pch, ach, tiny, res_zeroed, passed = (
            sem(n) for n in ("loaded", "first_in", "sq_done", "mx_done", "sc_done", "tr_done", "ex_done", "zeroed",
                             "dch", "pch", "ach", "tiny", "res_zeroed", "passed"))
        x_here = {k: sem(f"x_here_{k}") for k in "CAB"}
        st_here = {k: sem(f"st_here_{k}") for k in "AB"}
        res_here = {k: sem(f"res_here_{k}") for k in "CABD"}
        stored = {k: sem(f"stored_{k}") for k in "CABD"}
        hi_ready = [sem(f"hi{n}_ready") for n in range(3)]
        lo_ready = [sem(f"lo{n}_ready") for n in range(3)]
        bhi_ready = [sem(f"bhi{n}_ready") for n in range(3)]
        blo_ready = [sem(f"blo{n}_ready") for n in range(3)]
        conv_done = [sem(f"conv{n}_done") for n in range(3)]
        x1_ready, x1_stat, stat_read, bn1_aggr = (sem(n) for n in ("x1_ready", "x1_stat", "stat_read", "bn1_aggr"))
        w_mixed = [sem(f"w{n}_mixed") for n in range(3)]
        w_ready = [sem(f"w{n}_ready") for n in range(3)]
        mean_ready, gm_ready, e_ready, stq_ps, stq_ready, gap_ready, hid_ps, hid_ready, log_ps, lg_ready, exp_ready, \
            coeff_ready, stored_stats = (
                sem(n) for n in ("mean_ready", "gm_ready", "e_ready", "stq_ps", "stq_ready", "gap_ready", "hid_ps",
                                 "hid_ready", "log_ps", "lg_ready", "exp_ready", "coeff_ready", "stored_stats"))

        block = ctx.enter_context(nc.Block())

        def rows(t, s, r0, n):
            return t[s, :, bass.ds(r0, n, 4) if not isinstance(r0, int) else slice(r0, r0 + 4 * (n - 1) + 1, 4), :]

        @block.sync
        def _(sp):
            sp.dma_start(cst[:], consts).then_inc(loaded, 16)
            for n in range(3):
                sp.dma_start(stage[:, n, :], experts_d[n].rearrange("e o c h w -> (e o) (c h w)")).then_inc(loaded, 16)
            sp.dma_start(wc1_in[:], w_c1).then_inc(loaded, 16)
            sp.dma_start(wc2_in[:], w_c2).then_inc(loaded, 16)
            for i in range(4):
                sp.dma_start(first[:, 2 * i:2 * i + 2, :],
                             x[0].rearrange("c (r h) w -> (c r) (h w)", r=4)
                             [:, 4096 * i:4096 * (i + 1)].rearrange("p (a b) -> p a b", a=2)).then_inc(first_in, 16)

            xs = x.rearrange("s c (b q) w -> s q c b w", q=Q)
            x1s = x1d.rearrange("s c (b q) w -> s q c b w", q=Q)
            xflat = x.rearrange("s c (r h) w -> s (c r) (h w)", r=4)

            def load_x(buf, s, b0, n):
                for q in range(Q):
                    sp.dma_start(x_in[buf][q * C:(q + 1) * C, 0:n, :], xs[s, q, :, bass.ds(b0, n), :]).then_inc(x_here[buf], 16)

            def shifted(t, s, q, b0, n):
                return t[s, 0, :, bass.ds(b0, n), :] if q == 3 else t[s, q + 1, :, bass.ds(b0 - 1, n), :]

            def load_res(buf, s, b0):
                for q in range(Q):
                    sp.dma_start(res[buf][q * C:(q + 1) * C, :, :], shifted(xs, s, q, b0, 6)).then_inc(res_here[buf], 16)

            def store_out(buf, s, b0):
                for q in range(Q):
                    sp.dma_start(shifted(x1s, s, q, b0, 6), out[buf][q * C:(q + 1) * C, :, :]).then_inc(stored[buf], 16)

            def load_stat(buf, s, k):
                sp.dma_start(st_in[buf][:, :, :], xflat[s, :, bass.ds(2048 * k, 2048)].rearrange("p (a b) -> p a b", a=4)
                             ).then_inc(st_here[buf], 16)

            def edge(q):
                return ((0, 2), (0, 2)) if q == 3 else ((1, 1), (0, 3))

            def load_c(s):
                load_x("C", s, 0, 6)
                for q in range(Q):
                    b, n = edge(q)[0]
                    sp.dma_start(res["C"][q * C:(q + 1) * C, b:b + n, :], shifted(xs, s, q, b, n)).then_inc(res_here["C"], 16)

            def load_first(s, s2):
                load_c(s)
                for g, buf in ((1, "A"), (2, "B")):
                    load_x(buf, s, 6 * g, 6)
                    load_res(buf, s, 6 * g - 4)
                    load_stat(buf, s2, g - 1)

            sp.wait_ge(res_zeroed, 1)
            load_first(0, 1 % S)
            with sp.Fori(0, S) as s:
                nxt = sp.snap((s + 1) % S)
                n0 = sp.snap(s * NCH)
                with sp.Fori(0, 3) as i:
                    ni = sp.snap(n0 + i * 6)
                    for k, buf in ((0, "A"), (1, "B")):
                        g = 1 + k
                        sp.wait_ge(x1_ready, ni + (3 * g + 1) + 1)
                        store_out(buf, s, i * 12 + (6 * g - 4))
                        sp.wait_ge(lo_ready[0], ni + (3 * g + 3) + 1)
                        load_x(buf, s, i * 12 + 6 * (g + 2), 6)
                        load_res(buf, s, i * 12 + (6 * (g + 2) - 4))
                        sp.wait_ge(stat_read, s * 8 + i * 2 + (k + 1))
                        load_stat(buf, nxt, i * 2 + (g + 1))
                for g, buf in ((7, "A"), (8, "B")):
                    sp.wait_ge(x1_ready, n0 + (3 * g + 1) + 1)
                    store_out(buf, s, 6 * g - 4)
                    sp.wait_ge(lo_ready[0], n0 + (3 * g + 3) + 1)
                    load_x(buf, s, 6 * (g + 2), 6 if g == 7 else 4)
                    load_res(buf, s, 6 * (g + 2) - 4)
                    if g == 7:
                        for q in range(Q):
                            b, n = edge(q)[0]
                            sp.dma_start(shifted(x1s, s, q, b, n), out["C"][q * C:(q + 1) * C, b:b + n, :]).then_inc(stored["C"], 16)
                        for q in range(Q):
                            b, n = edge(q)[1]
                            sp.dma_start(res["D"][q * C:(q + 1) * C, b:b + n, :], shifted(xs, s, q, 62 + b, n)).then_inc(res_here["D"], 16)
                        load_c(nxt)
                nxt2 = sp.snap((s + 2) % S)
                sp.wait_ge(stat_read, s * 8 + 8)
                sp.sem_inc(passed, 1)
                for g, buf, done in ((1, "A", 9), (2, "B", 10)):
                    sp.wait_ge(x1_ready, n0 + (3 * done + 1) + 1)
                    store_out(buf, s, 6 * done - 4)
                    load_x(buf, nxt, 6 * g, 6)
                    load_res(buf, nxt, 6 * g - 4)
                    load_stat(buf, nxt2, g - 1)
                sp.wait_ge(x1_ready, n0 + NCH + 1)
                for q in range(Q):
                    b, n = edge(q)[1]
                    sp.dma_start(shifted(x1s, s, q, 62 + b, n), out["D"][q * C:(q + 1) * C, b:b + n, :]).then_inc(stored["D"], 16)
            sp.wait_ge(bn1_aggr, S)
            sp.dma_start(stats1_d, mv1[:]).then_inc(stored_stats, 16)
            for k, n in (("C", 1), ("A", 5), ("B", 5), ("D", 1)):
                sp.wait_ge(stored[k], 64 * n * S + 1)
                if k != "D":
                    sp.wait_ge(x_here[k], 64 * (n * S + 1))
                sp.wait_ge(res_here[k], 64 * (n * S + (k != "D")))
                if k in "AB":
                    sp.wait_ge(st_here[k], 16 * (4 * S + 1))
            sp.wait_ge(stored_stats, 16)

        def taps_view(m, n, dx):
            return taps[:, n, dx, 1 - m:5 - m, :]

        def copy_b(engine, n, kind, slot):
            a, b = ring[n]["A" + kind], ring[n]["B" + kind]
            s0 = slot * CHUNK
            v = lambda t, p, i, k: t[p * 64:(p + 1) * 64, i:i + k, :].bitcast(f32)
            engine(v(b, 1, s0, 2), v(a, 0, s0, 2))
            if slot:
                return engine(v(b, 0, s0, 2), v(a, 1, s0 - 1, 2))
            engine(v(b, 0, 0, 1), v(a, 1, SLOTS * CHUNK - 1, 1))
            return engine(v(b, 0, 1, 1), v(a, 1, 0, 1))

        def spans(n, t, base):
            if t == 0:
                return [(0, 1, mask(0 if n == 1 else 2)), (1, 1, base)]
            if t == NCH - 1:
                return [(0, 1, mask(1 if n == 1 else 3)), (1, 1, None)]
            return [(0, 2, base)]

        @block.tensor
        def _(pe):
            pe.wait_ge(loaded, 6 * 16)
            pe.wait_ge(zeroed, 1)
            for k in range(18):
                n, m, dx = k // 6, (k // 3) % 2, k % 3
                if k >= 2:
                    pe.wait_ge(ex_done, k - 1)
                dst = (prep_ps, prep_ps2)[k % 2]
                nc.tensor.matmul(dst[:, 0:P], taps_view(m, n, dx), ident, start=True, stop=True).then_inc(tr_done, 1)
            pe.wait_ge(ex_done, 18)
            pe.wait_ge(tiny, 1)
            nc.tensor.matmul(prep_ps[:, 0:8], wc1r[:], cst[0:8, 3 * P:3 * P + 8], start=True, stop=True)
            nc.tensor.matmul(prep_ps2[0:8, 0:P], wc2_in[:], ident, start=True, stop=True).then_inc(tr_done, 1)
            pe.wait_ge(tiny, 2)

            def group_mean(k):
                pe.wait_ge(mean_ready, k + 1)
                nc.tensor.matmul(prep_ps[:, 0:1], same_group, mv[:, 0:1], start=True, stop=True).then_inc(gm_ready, 1)

            def moments(k):
                pe.wait_ge(e_ready, k + 1)
                nc.tensor.matmul(prep_ps2[:, 0:2], to_group, me[:, 0:2], start=True, stop=True)
                nc.tensor.matmul(prep_ps[:, 0:1], to_channel, me[:, 0:1], start=True, stop=True).then_inc(stq_ps, 1)

            def hidden(k):
                pe.wait_ge(gap_ready, k + 1)
                nc.tensor.matmul(prep_ps[0:8, 0:P], wc1t[:], gapb[:], start=True, stop=True).then_inc(hid_ps, 1)

            def logits(k):
                pe.wait_ge(hid_ready, k + 1)
                nc.tensor.matmul(prep_ps2[:, 0:P], hbs[:], wc2t[:], start=True, stop=True).then_inc(log_ps, 1)

            def conv(n, t, slot, count, first):
                pe.wait_ge(bhi_ready[n], count + (1 + CREDIT))
                pe.wait_ge(blo_ready[n], count + (1 + CREDIT))
                emptied = x1_ready if n == 2 else lo_ready[n + 1]
                pe.wait_ge(emptied, (count if first else count - 1) + 1)
                r, s0, dst = ring[n], slot * CHUNK, bank[n][t % 2]
                nb = 1 if t == NCH - 1 else CHUNK
                terms = [("hi", 0), ("lo", 0), ("hi", 1)]
                k = 0
                for dx in range(3):
                    for kind, w in terms:
                        for half, side in ((0, "B"), (1, "A")):
                            last = nc.tensor.matmul(dst[64 * half:64 * half + 64, 0:nb * IMG], w_now[n][:, w, 64 * dx:64 * dx + 64],
                                                    r[side + kind][:, s0:s0 + nb, dx:dx + IMG],
                                                    start=(k == 0), stop=(k == 8))
                        k += 1
                last.then_inc(conv_done[n], 1)

            def step(n0, t, after=(None, None, None), weights=None):
                for n in range(3):
                    m = (t - n) % NCH
                    if m == 0 and t >= n:
                        pe.wait_ge(w_ready[n], weights)
                    if t >= n:
                        conv(n, m, m % SLOTS, n0 + (t - n), m == 0)
                    if after[n] is not None:
                        after[n][0](after[n][1])

            group_mean(0)
            moments(0)
            hidden(0)
            logits(0)
            step(0, 0, weights=2)
            step(0, 1, weights=2)
            with pe.Fori(0, S) as s:
                n0 = pe.snap(s * NCH)
                k1 = pe.snap(s + 1)
                step(n0, 2, weights=k1 + 1)
                with pe.Fori(0, 4) as i:
                    ni = pe.snap(n0 + i * 6)
                    for t in range(3, 9):
                        step(ni, t)
                step(n0, 27, ((group_mean, k1), None, (moments, k1)))
                step(n0, 28, (None, None, (hidden, k1)))
                step(n0, 29, (None, (logits, k1), None))
                for t in range(30, NCH + 2):
                    step(n0, t, weights=k1 + 2)

        @block.scalar
        def _(act):
            act.wait_ge(loaded, 6 * 16)
            for n in range(3):
                nc.scalar.activation(mixed[:].rearrange("p e a o -> p (e a o)")[:, 0:C * TAPS], stage[:, n, :], ACT.Square,
                                     accum_out=sumsq[:, n:n + 1]).then_inc(sq_done, 1)
                act.wait_ge(sq_done, n + 1)
            act.wait_ge(mx_done, 1)
            nc.scalar.activation(norms[:], maxsq[:], ACT.Sqrt).then_inc(ach, 1)
            act.wait_ge(zeroed, 1)

            def softmax_exp(k):
                act.wait_ge(lg_ready, k + 1)
                nc.scalar.activation(ex_l[:], lg[:], ACT.Exp, scale=1.0 / TEMP).then_inc(exp_ready, 1)

            def b_ring(n, slot, count):
                act.wait_ge(hi_ready[n], count + 1)
                act.wait_ge(conv_done[n], count - 2 + CREDIT)
                copy_b(nc.scalar.copy, n, "hi", slot).then_inc(bhi_ready[n], 1)

            def hi(n, t, edges, count):
                act.wait_ge(conv_done[n - 1], count + (1 + CREDIT))
                act.wait_ge(conv_done[n], count - 2 + CREDIT)
                slot, src = t % SLOTS, bank[n - 1][t % 2]
                base = 1.0 / WSCALE if n == 1 else 1.0 / (WSCALE * HALF)
                for b, k, sc in spans(n, edges, base):
                    dst = ring[n]["Ahi"][:, slot * CHUNK + b:slot * CHUNK + b + k, 1:1 + IMG]
                    if sc is None:
                        last = nc.scalar.copy(dst, zero.unsqueeze(2).to_broadcast([P, 1, IMG]))
                        continue
                    last = nc.scalar.activation(dst, src[:, b * IMG:(b + k) * IMG].rearrange("p (b w) -> p b w", b=k),
                                                ACT.Copy, scale=sc)
                last.then_inc(hi_ready[n], 1)
                b_ring(n, slot, count)

            def step(n0, t, edges=False):
                m, up, down = (k % NCH for k in (t, t + 1, t - 1))
                hi(1, m, m if edges else None, n0 + t)
                b_ring(0, up % SLOTS, n0 + (t + 1))
                if t:
                    hi(2, down, down if edges else None, n0 + (t - 1))

            softmax_exp(0)
            b_ring(0, 0, 0)
            step(0, 0, True)
            step(0, 1, True)
            with act.Fori(0, S) as s:
                n0 = act.snap(s * NCH)
                step(n0, 2)
                with act.Fori(0, 4) as i:
                    ni = act.snap(n0 + i * 6)
                    for t in range(3, 9):
                        step(ni, t)
                for t in range(27, NCH + 2):
                    if t == 30:
                        softmax_exp(s + 1)
                    step(n0, t, True)

        @block.vector
        def _(dve):
            n_ch = [0]

            def link(ins):
                n_ch[0] += 1
                ins.then_inc(dch, 1)
                dve.wait_ge(dch, n_ch[0])

            nc.vector.memset(res["C"][:], 0.0)
            nc.vector.memset(res["D"][:], 0.0).then_inc(res_zeroed, 1)
            dve.wait_ge(res_zeroed, 1)
            for n in range(3):
                for r in ring[n].values():
                    nc.vector.memset(r[:].rearrange("p a b -> p (a b)").bitcast(f32), 0.0)
            link(nc.vector.memset(taps[:], 0.0))
            dve.wait_ge(loaded, 6 * 16)
            for n in range(3):
                nc.vector.tensor_copy(taps[:, n, :, 1:4, :], stage[:, n, :].rearrange("p (c y x) -> p x y c", y=3, x=3))
            nc.vector.memset(minus_half[:], -0.5)
            link(nc.vector.memset(ones[:], 1.0))
            ones_done = n_ch[0]
            for n in range(3):
                for counter in (conv_done[n], bhi_ready[n], blo_ready[n]):
                    dve.sem_inc(counter, CREDIT)
                dve.sem_inc(lo_ready[n], 1)
                dve.sem_inc(w_ready[n], 1)
            for counter in (x1_ready, x1_stat, *stored.values()):
                dve.sem_inc(counter, 1)
            nc.vector.memset(dev[:, 0:1], 0.0).then_inc(zeroed, 1)
            dve.wait_ge(ach, 1)
            link(nc.vector.tensor_scalar(alpha[:], norms[:], 1e-15, None, ALU.max))
            link(nc.vector.tensor_tensor(final_scale[:], alpha[:, 0:1], alpha[:, 1:2], ALU.mult))
            link(nc.vector.scalar_tensor_tensor(final_scale[:], final_scale[:], HALF / WSCALE, alpha[:, 2:3], ALU.mult, ALU.mult))
            link(nc.vector.reciprocal(alpha[:], alpha[:]))
            link(nc.vector.tensor_scalar(alpha[:], alpha[:], WSCALE, None, ALU.mult))
            for k in range(18):
                n, m, dx = k // 6, (k // 3) % 2, k % 3
                dve.wait_ge(tr_done, k + 1)
                src = (prep_ps, prep_ps2)[k % 2]
                nc.vector.tensor_scalar(ex[n][:, :, 2 * dx + m, :], src[:, 0:P].rearrange("p (e o) -> p e o", e=E),
                                        alpha[:, n:n + 1], None, ALU.mult).then_inc(ex_done, 1)
            dve.wait_ge(loaded, 6 * 16)
            for q in range(Q):
                nc.vector.tensor_scalar(wc1r[:, q * C:(q + 1) * C], wc1_in[:], 0.25, None, ALU.mult)
            nc.vector.memset(dev[:, 1:2], 0.0).then_inc(tiny, 1)
            dve.wait_ge(tr_done, 19)
            link(nc.vector.tensor_copy(wc1t[:], prep_ps[:, 0:8]))
            nc.vector.tensor_copy(wc2t[:], prep_ps2[0:8, 0:P]).then_inc(tiny, 1)
            dve.wait_ge(tiny, 2)
            dve.wait_ge(first_in, 64)
            for k in range(32):
                ins = nc.vector.bn_stats(bn0[:, k, :], first[:, k // 4, (k % 4) * 512:(k % 4 + 1) * 512])
            link(ins)

            dk = [0]

            def chain(ins, n_before):
                dk[0] += 1
                ins.then_inc(dch, 1)
                dve.wait_ge(dch, n_before + dk[0])

            def take_mean(k, nb):
                dve.sem_inc(passed, 1)
                nc.vector.bn_aggr(mv[:], bn0[:].rearrange("p a b -> p (a b)")).then_inc(mean_ready, 1)
                dve.wait_ge(mean_ready, k + 1)

            def take_dev(k, nb):
                dve.wait_ge(gm_ready, k + 1)
                chain(nc.vector.tensor_tensor(dev[:, 0:1], mv[:, 0:1], prep_ps[:, 0:1], ALU.subtract), nb)
                chain(nc.vector.tensor_copy(me[:, 0:1], mv[:, 0:1]), nb)
                nc.vector.scalar_tensor_tensor(me[:, 1:2], dev[:, 0:1], dev[:, 0:1], mv[:, 1:2], ALU.mult, ALU.add
                                               ).then_inc(e_ready, 1)

            def take_moments(k, nb):
                dve.wait_ge(stq_ps, k + 1)
                chain(nc.vector.tensor_copy(stq[:, 0:2], prep_ps2[:, 0:2]), nb)
                nc.vector.tensor_copy(stq[:, 2:3], prep_ps[:, 0:1]).then_inc(stq_ready, 1)

            def take_hidden(k, nb):
                dve.wait_ge(hid_ps, k + 1)
                nc.vector.tensor_scalar(hbs[:], prep_ps[0:8, 0:P], 0.0, None, ALU.max).then_inc(hid_ready, 1)

            def take_logits(k, nb):
                dve.wait_ge(log_ps, k + 1)
                lp = prep_ps2[:, 0:P].rearrange("p (o e) -> p o e", e=E)
                chain(nc.vector.tensor_reduce(mx[:], lp, AX.X, ALU.max), nb)
                nc.vector.tensor_tensor(lg[:], lp, mx[:].unsqueeze(2).to_broadcast([P, C, E]), ALU.subtract
                                        ).then_inc(lg_ready, 1)

            def take_coeff(k, nb):
                dve.wait_ge(exp_ready, k + 1)
                chain(nc.vector.tensor_reduce(den[:], ex_l[:], AX.X, ALU.add), nb)
                chain(nc.vector.reciprocal(rden[:], den[:]), nb)
                nc.vector.tensor_tensor(coeff[:].rearrange("p e o -> p o e"), ex_l[:],
                                        rden[:].unsqueeze(2).to_broadcast([P, C, E]), ALU.mult).then_inc(coeff_ready, 1)

            def install(n, all_done, k):
                dve.wait_ge(w_mixed[n], k)
                dve.wait_ge(conv_done[n], all_done + CREDIT)
                nc.vector.tensor_copy(w_now[n][:], w_next[n][:]).then_inc(w_ready[n], 1)

            def b_ring(n, slot, count):
                dve.wait_ge(lo_ready[n], count + 1 + 1)
                dve.wait_ge(conv_done[n], count - 2 + CREDIT)
                copy_b(nc.vector.tensor_copy, n, "lo", slot).then_inc(blo_ready[n], 1)

            def lo(n, t, edges, count):
                dve.wait_ge(hi_ready[n], count + 1)
                dve.wait_ge(conv_done[n], count - 2 + CREDIT)
                slot, src = t % SLOTS, bank[n - 1][t % 2]
                base = 1.0 / WSCALE if n == 1 else 1.0 / (WSCALE * HALF)
                for b, k, sc in spans(n, edges, base):
                    at = lambda kind: ring[n][kind][:, slot * CHUNK + b:slot * CHUNK + b + k, 1:1 + IMG]
                    if sc is None:
                        last = nc.vector.memset(ring[n]["Alo"][:, slot * CHUNK + b, :].bitcast(f32), 0.0)
                        continue
                    last = nc.vector.scalar_tensor_tensor(at("Alo"), src[:, b * IMG:(b + k) * IMG].rearrange("p (b w) -> p b w", b=k),
                                                          sc, at("Ahi"), ALU.mult, ALU.subtract)
                last.then_inc(lo_ready[n], 1)
                b_ring(n, slot, count)

            def x1(t, buf, at_block, uses, bn_slot, count):
                dve.wait_ge(conv_done[2], count + (1 + CREDIT))
                if uses is not None:
                    dve.wait_ge(res_here[buf], uses * 64 + 64)
                    dve.wait_ge(stored[buf], uses * 64 + 1)
                nb = 1 if t == NCH - 1 else CHUNK
                dst = out[buf][:, at_block:at_block + nb, :]
                nc.vector.scalar_tensor_tensor(dst, bank[2][t % 2][:, 0:nb * IMG].rearrange("p (b w) -> p b w", b=nb),
                                               final_scale[:], res[buf][:, at_block:at_block + nb, :],
                                               ALU.mult, ALU.add).then_inc(x1_ready, 1)
                dve.wait_ge(x1_ready, count + 1 + 1)
                if t == 0:
                    nc.vector.bn_stats(bn1[:, 0, :], out[buf][:, 1, :])
                    last = nc.vector.bn_stats(bn1[96:128, 32, :], out[buf][96:128, 0, :])
                elif t == NCH - 1:
                    last = nc.vector.bn_stats(bn1[0:96, 32, :], out[buf][0:96, 2, :])
                else:
                    last = nc.vector.bn_stats(bn_slot, out[buf][:, at_block:at_block + CHUNK, :])
                last.then_inc(x1_stat, 1)

            def step(n0, t, x1_args=None, edges=False, extra=None):
                m, up, down = (k % NCH for k in (t, t + 1, t - 1))
                lo(1, m, m if edges else None, n0 + t)
                if extra is not None and t != NCH:
                    extra[0](*extra[1:])
                b_ring(0, up % SLOTS, n0 + (t + 1))
                if t:
                    lo(2, down, down if edges else None, n0 + (t - 1))
                if extra is not None and t == NCH:
                    extra[0](*extra[1:])
                if t >= 2:
                    x1(t - 2, *x1_args, n0 + (t - 2))

            nb0 = n_ch[0]
            take_mean(0, nb0)
            take_dev(0, nb0)
            take_moments(0, nb0)
            take_hidden(0, nb0)
            take_logits(0, nb0)
            take_coeff(0, nb0)
            b_ring(0, 0, 0)
            install(0, 0, 1)
            step(0, 0, edges=True)
            install(1, 0, 1)
            step(0, 1, edges=True)
            install(2, 0, 1)
            before = nb0 + dk[0]
            per_sample = dk[0] + 1
            with dve.Fori(0, S) as s:
                n0 = dve.snap(s * NCH)
                k1 = dve.snap(s + 1)
                nb = dve.snap(s * per_sample + before)
                dk[0] = 0
                step(n0, 2, ("C", 0, s, None))
                with dve.Fori(0, 4) as i:
                    ni = dve.snap(n0 + i * 6)
                    for t in range(3, 9):
                        buf, first_t, k = ("A", 3, 0) if t < 6 else ("B", 6, 1)
                        st = 4 * (2 * i + k)
                        if t == first_t:
                            dve.wait_ge(st_here[buf], s * 64 + i * 16 + 16)
                        for c in ((0, 1), (2,), (3,))[t - first_t]:
                            ins = nc.vector.bn_stats(bn0[:, bass.ds(i * 8 + (4 * k + c), 1), :], st_in[buf][:, c, :])
                        if t - first_t == 2:
                            ins.then_inc(stat_read, 1)
                        step(ni, t, (buf, 2 * (t - first_t), s * 5 + i if t == first_t else None,
                                     bn1[:, bass.ds(i * 6 + (t - 2), 1), :]))
                dve.wait_ge(stat_read, s * 8 + 8)
                take_mean(k1, nb)
                k2 = dve.snap(s + 2)
                for t in range(27, NCH + 2):
                    buf, first_t = ("A", 27) if t < 30 else ("B", 30) if t < 33 else ("D", 33)
                    u = None if t != first_t else s if buf == "D" else s * 5 + 4
                    extra = {27: (take_dev, k1, nb), 29: (take_hidden, k1, nb), 30: (take_coeff, k1, nb),
                             NCH - 1: (install, 0, n0 + NCH, k2), NCH: (install, 1, n0 + NCH, k2)}.get(t)
                    step(n0, t, (buf, 2 * (t - first_t), u, bn1[:, t - 2, :] if t - 2 < 32 else None), edges=True, extra=extra)
                    if t == 27:
                        take_moments(k1, nb)
                    if t == 29:
                        take_logits(k1, nb)
                install(2, n0 + NCH, k2)
                dve.wait_ge(x1_stat, n0 + NCH + 1)
                dve.sem_inc(passed, 1)
                chain(nc.vector.bn_aggr(mv1_now[:], bn1[:].rearrange("p a b -> p (a b)")), nb)
                nc.vector.tensor_copy(mv1[:, bass.ds(s, 1), :].rearrange("p a b -> p (a b)"), mv1_now[:]).then_inc(bn1_aggr, 1)
                dve.wait_ge(bn1_aggr, k1)
                assert dk[0] == per_sample

        @block.gpsimd
        def _(pool):
            pool.wait_ge(sq_done, 3)
            nc.gpsimd.partition_all_reduce(maxsq[:], sumsq[:], P, bass.bass_isa.ReduceOp.max).then_inc(mx_done, 1)
            pool.wait_ge(ex_done, 18)

            def norms_of(k, pb):
                pool.wait_ge(stq_ready, k + 1)
                pool.sem_inc(passed, 1)
                link(nc.gpsimd.tensor_scalar(var_eps[:], stq[:, 1:2], EPS, None, ALU.add), pb)
                link(nc.gpsimd.tensor_tensor(norm_next[:, 0:1], var_eps[:], minus_half[:], ALU.pow), pb)
                link(nc.gpsimd.tensor_scalar(norm_next[:, 1:2], stq[:, 0:1], norm_next[:, 0:1], -1.0, ALU.mult, ALU.mult), pb)
                link(nc.gpsimd.tensor_scalar(gap[:], stq[:, 2:3], norm_next[:, 0:1], norm_next[:, 1:2], ALU.mult, ALU.add), pb)
                nc.gpsimd.tensor_scalar(gapb[:], ones[:], gap[:], None, ALU.mult).then_inc(gap_ready, 1)
                pool.wait_ge(gap_ready, k + 1)
                pool.sem_inc(passed, 1)

            pk = [0]

            def link(ins, before):
                pk[0] += 1
                ins.then_inc(pch, 1)
                pool.wait_ge(pch, before + pk[0])
                pool.sem_inc(passed, 1)

            def weights(n, k, pb):
                link(nc.gpsimd.tensor_tensor(mixed[:], ex[n][:], coeff[:].unsqueeze(2).to_broadcast([P, E, 6, C]), ALU.mult), pb)
                link(nc.gpsimd.tensor_tensor(mixed[:, 0:2], mixed[:, 0:2], mixed[:, 2:4], ALU.add), pb)
                link(nc.gpsimd.tensor_tensor(mixed[:, 0:1], mixed[:, 0:1], mixed[:, 1:2], ALU.add), pb)
                m = mixed[:, 0].rearrange("p a o -> p (a o)")
                link(nc.gpsimd.tensor_scalar(w_next[n][:, 0], m, 1.0, None, ALU.mult), pb)
                nc.gpsimd.tensor_tensor(w_next[n][:, 1], m, w_next[n][:, 0], ALU.subtract).then_inc(w_mixed[n], 1)
                pool.wait_ge(w_mixed[n], k)
                pool.sem_inc(passed, 1)

            def normalise(t, buf, at_block, here, count, pb):
                if here is not None:
                    pool.wait_ge(x_here[buf], here)
                pool.wait_ge(lo_ready[0], count + 1)
                pool.wait_ge(conv_done[0], count - 2 + CREDIT)
                pool.wait_ge(bhi_ready[0], count - 1 + CREDIT)
                pool.wait_ge(blo_ready[0], count - 1 + CREDIT)
                pool.sem_inc(passed, 1)
                s0 = (t % SLOTS) * CHUNK
                hi, lo = (ring[0][k][:, s0:s0 + CHUNK, 1:1 + IMG] for k in ("Ahi", "Alo"))
                if t == NCH - 1:
                    nc.gpsimd.memset(ring[0]["Ahi"][:, s0:s0 + CHUNK, :].rearrange("p a b -> p (a b)").bitcast(f32), 0.0).then_inc(hi_ready[0], 1)
                    nc.gpsimd.memset(ring[0]["Alo"][:, s0:s0 + CHUNK, :].rearrange("p a b -> p (a b)").bitcast(f32), 0.0).then_inc(lo_ready[0], 1)
                    return
                src = x_in[buf][:, at_block:at_block + CHUNK, :]
                nc.gpsimd.tensor_scalar(hi, src, norm_now[:, 0:1], norm_now[:, 1:2], ALU.mult, ALU.add).then_inc(hi_ready[0], 1)
                link(nc.gpsimd.tensor_scalar(xn[:], src, norm_now[:, 0:1], norm_now[:, 1:2], ALU.mult, ALU.add), pb)
                pool.wait_ge(hi_ready[0], count + 1)
                nc.gpsimd.tensor_tensor(lo, xn[:], hi, ALU.subtract).then_inc(lo_ready[0], 1)

            def start(k, count, here, pb):
                pool.wait_ge(lo_ready[0], count + 1)
                pool.sem_inc(passed, 1)
                link(nc.gpsimd.tensor_scalar(norm_now[:], norm_next[:], 1.0, None, ALU.mult), pb)
                for n in range(3):
                    normalise(n, "C", 2 * n, here if n == 0 else None, count + n, pb)
                    pool.wait_ge(coeff_ready, k)
                    pool.wait_ge(w_ready[n], k)
                    pool.sem_inc(passed, 1)
                    weights(n, k, pb)

            norms_of(0, 0)
            start(1, 0, 64, 0)
            before = pk[0]
            in_loop, total = 6, before + 4 * 6 + 5
            pk[0] = 0
            with pool.Fori(0, S) as s:
                s1 = pool.snap(s + 1)
                n0 = pool.snap(s * NCH)
                pb = pool.snap(s * total + before)
                base = pk[0]
                with pool.Fori(0, 4) as i:
                    ni = pool.snap(n0 + i * 6)
                    pi = pool.snap(pb + i * in_loop)
                    for t in range(3, 9):
                        buf, first_t = ("A", 3) if t < 6 else ("B", 6)
                        normalise(t, buf, 2 * (t - first_t), s * 320 + i * 64 + 64 if t == first_t else None, ni + t, pi)
                assert pk[0] == base + in_loop
                pk[0] = base + 4 * in_loop
                for t in range(27, NCH):
                    buf, first_t = ("A", 27) if t < 30 else ("B", 30)
                    normalise(t, buf, 2 * (t - first_t), s * 320 + 320 if t == first_t else None, n0 + t, pb)
                    if t == 29:
                        norms_of(s1, pb)
                start(s + 2, n0 + NCH, s * 64 + 128, pb)
                assert pk[0] == total, (pk[0], total)
                pk[0] = 0


M = 64
KY = 16


def spectral_constants():
    k = np.arange(M) + (IMG // 2 - M // 2)
    ang = 2 * np.pi * ((np.arange(IMG)[:, None] * k[None, :]) % IMG) / IMG
    c, s = np.cos(ang), np.sin(ang)
    half = lambda a: a.reshape(2, P, -1).transpose(1, 0, 2).reshape(P, -1)
    along_h = np.concatenate([c[:P, 0::2], s[:P, 0::2], c[:P, 1::2], s[:P, 1::2]], 1)
    cos_part = half(np.concatenate([c, s], 1))
    sin_part = half(np.concatenate([-s, c], 1))
    back_h = np.concatenate([c.T, s.T], 0)
    back_w = np.concatenate([(c + s).T, (c - s).T], 0) / (IMG * IMG)
    q, cc = np.arange(P) // C, np.arange(P) % C
    groupq = (cc[:, None] // 2 == cc[None, :] // 2) / 8.0
    pick = (q[:, None] == 0) & (cc[:, None] == np.arange(C)[None, :])
    return np.concatenate([along_h, cos_part, sin_part, back_h, back_w, groupq, pick], axis=1).astype(np.float32)


OFF_W, OFF_BACK = P, 5 * P
OFF_GROUP = OFF_BACK + 2 * IMG
OFF_PICK = OFF_GROUP + P
NSPEC = OFF_PICK + C


def build_forward(nc, x1d, stats_d, spec, f_d, S):
    f32 = mybir.dt.float32
    ALU, ACT = mybir.AluOpType, mybir.ActivationFunctionType
    with ExitStack() as ctx:
        sb = lambda n, s: ctx.enter_context(nc.sbuf_tensor("f_" + n, s, f32))
        ps = lambda n, s: ctx.enter_context(nc.psum_tensor("f_" + n, s, f32))
        sem = lambda n: ctx.enter_context(nc.semaphore("f_" + n))
        cst = sb("cst", [P, NSPEC])
        along_h = lambda parity: cst[:, parity * M:(parity + 1) * M]
        part_w = lambda cs, wc: cst[:, OFF_W + (2 * cs + wc) * P:OFF_W + (2 * cs + wc + 1) * P]
        groupq = cst[:, OFF_GROUP:OFF_GROUP + P]
        pick = cst[:, OFF_PICK:OFF_PICK + C]
        mv = sb("mv", [P, S, 2])
        gm = sb("gm", [P, 2, S])
        dev = sb("dev", [P, S])
        var = sb("var", [P, S])
        expo = sb("expo", [P, S])
        ones = sb("ones", [P, P])
        spread = sb("spread", [P, 2, S, C])
        norm = sb("norm", [P, 2, S, C])
        mean_now = sb("mean_now", [P, C])
        rs_now = sb("rs_now", [P, C])
        xt = [sb(f"xt{i}", [P, 2, 4, IMG]) for i in range(2)]
        xg = [sb(f"xg{i}", [P, 2, 4, IMG]) for i in range(2)]
        y = [sb(f"y{i}", [P, 2, 2, 4, M]) for i in range(2)]
        fs = [sb(f"fs{i}", [P, 8, P]) for i in range(2)]
        b1 = [[ps(f"b1{i}{j}", [P, 512]) for j in range(2)] for i in range(2)]
        b2 = [ps(f"b2{i}", [P, 512]) for i in range(2)]
        bs = [ps(f"bs{i}", [P, 512]) for i in range(2)]
        here, pch, dch, pw, sp_ready, now_ready, prep, norm_ready, rs_ready = (
            sem(n) for n in ("here", "pch", "dch", "pw", "sp_ready", "now_ready", "prep", "norm_ready", "rs_ready"))
        x_here = [sem(f"x_here{i}") for i in range(2)]
        xg_ready = [sem(f"xg_ready{i}") for i in range(2)]
        y_ps = [sem(f"y_ps{i}") for i in range(2)]
        y_ready = [sem(f"y_ready{i}") for i in range(2)]
        f_ps = [sem(f"f_ps{i}") for i in range(2)]
        f_ready = [sem(f"f_ready{i}") for i in range(2)]
        f_out = [sem(f"f_out{i}") for i in range(2)]
        block = ctx.enter_context(nc.Block())
        xv = x1d.rearrange("s c (a p) w -> s a p c w", p=P)
        fv = f_d.rearrange("s (k c) (r a) n -> s c a r k n", c=2, a=2)

        @block.sync
        def _(sp):
            sp.dma_start(cst[:], spec).then_inc(here, 16)
            sp.dma_start(mv[:], stats_d).then_inc(here, 16)

            def load(buf, s, c0):
                for a in range(2):
                    sp.dma_start(xt[buf][:, a], xv[s, a, :, bass.ds(c0, 4), :]).then_inc(x_here[buf], 16)

            with sp.Fori(0, S) as s:
                with sp.Fori(0, 4) as i:
                    n = sp.snap(s * 4 + i)
                    for buf in range(2):
                        sp.wait_ge(xg_ready[buf], n + 1)
                        load(buf, s, i * 8 + 4 * buf)
            for buf in range(2):
                sp.wait_ge(x_here[buf], 32 * 4 * S)

        @block.tensor
        def _(pe):
            pe.wait_ge(here, 32)
            nc.tensor.matmul(bs[0][:, 0:S], groupq, mv[:, :, 0], start=True, stop=True).then_inc(pw, 1)
            pe.wait_ge(prep, 1)
            nc.tensor.matmul(bs[1][:, 0:S], groupq, var[:], start=True, stop=True).then_inc(pw, 1)
            pe.wait_ge(sp_ready, 1)
            nc.tensor.matmul(bs[0][:, 0:S * C], ones[:], spread[:, 0].rearrange("p s c -> p (s c)"), start=True, stop=True)
            nc.tensor.matmul(bs[1][:, 0:S * C], ones[:], spread[:, 1].rearrange("p s c -> p (s c)"), start=True, stop=True).then_inc(pw, 1)

            def over_h(buf, n):
                pe.wait_ge(xg_ready[buf], n + 1 + 1)
                pe.wait_ge(y_ready[buf], n * 2 + 1)
                for c in range(4):
                    for wc in range(2):
                        for a in range(2):
                            at = ((wc * 2 + c % 2) * 2 + a) * M
                            last = nc.tensor.matmul(b1[buf][c // 2][:, at:at + M], xg[buf][:, a, c, wc * P:(wc + 1) * P],
                                                    along_h(a), start=True, stop=True)
                    if c % 2:
                        last.then_inc(y_ps[buf], 1)

            def over_w(buf, n):
                pe.wait_ge(y_ready[buf], n * 2 + 2 + 1)
                pe.wait_ge(f_ready[buf], n + 1)
                for pair in range(2):
                    for k in range(4):
                        cs, wc = k // 2, k % 2
                        last = nc.tensor.matmul(b2[buf][:, pair * P:(pair + 1) * P],
                                                y[buf][:, wc, cs, 2 * pair:2 * pair + 2, :].rearrange("p c k -> p (c k)"),
                                                part_w(cs, wc), start=(k == 0), stop=(k == 3))
                last.then_inc(f_ps[buf], 1)

            with pe.Fori(0, S * 4) as n:
                over_h(0, n)
                over_h(1, n)
                over_w(0, n)
                over_w(1, n)

        @block.vector
        def _(dve):
            k = [0]

            def link(ins):
                k[0] += 1
                ins.then_inc(dch, 1)
                dve.wait_ge(dch, k[0])

            for counters in (f_out, f_ps, xg_ready, y_ps, f_ready, y_ready):
                for counter in counters:
                    dve.sem_inc(counter, 1)
            nc.vector.memset(ones[:], 1.0)
            link(nc.vector.memset(expo[:], -0.5))
            dve.wait_ge(here, 32)
            dve.wait_ge(pw, 1)
            link(nc.vector.tensor_copy(gm[:, 0], bs[0][:, 0:S]))
            link(nc.vector.tensor_tensor(dev[:], mv[:, :, 0], gm[:, 0], ALU.subtract))
            link(nc.vector.tensor_tensor(dev[:], dev[:], dev[:], ALU.mult))
            nc.vector.tensor_tensor(var[:], dev[:], mv[:, :, 1], ALU.add).then_inc(prep, 1)
            dve.wait_ge(pw, 2)
            nc.vector.tensor_scalar(dev[:], bs[1][:, 0:S], EPS, None, ALU.add).then_inc(prep, 1)
            dve.wait_ge(pch, 1)
            bc = lambda i: gm[:, i].unsqueeze(2).to_broadcast([P, S, C])
            pb = pick.unsqueeze(1).to_broadcast([P, S, C])
            nc.vector.tensor_tensor(spread[:, 0], bc(0), pb, ALU.mult)
            nc.vector.tensor_tensor(spread[:, 1], bc(1), pb, ALU.mult).then_inc(sp_ready, 1)
            dve.wait_ge(pw, 3)
            link(nc.vector.tensor_scalar(norm[:, 0].rearrange("p s c -> p (s c)"), bs[0][:, 0:S * C], 2.0, None, ALU.mult))
            nc.vector.tensor_copy(norm[:, 1].rearrange("p s c -> p (s c)"), bs[1][:, 0:S * C]).then_inc(norm_ready, 1)
            dve.wait_ge(norm_ready, 1)
            with dve.Fori(0, S) as s:
                dve.wait_ge(xg_ready[0], s * 4 + 1)
                dve.wait_ge(xg_ready[1], s * 4 + 1)
                nc.vector.tensor_copy(mean_now[:], norm[:, 0, bass.ds(s, 1), :].rearrange("p a c -> p (a c)")).then_inc(now_ready, 1)
                dve.wait_ge(now_ready, s + 1)
                for i in range(4):
                    n = dve.snap(s * 4 + i)
                    for buf in range(2):
                        dve.wait_ge(x_here[buf], n * 32 + 32)
                        dve.wait_ge(y_ps[buf], n * 2 + 1)
                        for c in range(0, 4, 2):
                            ch = i * 8 + buf * 4 + c
                            nc.vector.scalar_tensor_tensor(xg[buf][:, 0, c:c + 2, :], xt[buf][:, 0, c:c + 2, :], mean_now[:, ch:ch + 1],
                                                           xt[buf][:, 1, c:c + 2, :], ALU.subtract, ALU.add)
                        nc.vector.tensor_tensor(xg[buf][:, 1], xt[buf][:, 0], xt[buf][:, 1], ALU.subtract).then_inc(xg_ready[buf], 1)

        @block.gpsimd
        def _(pool):
            pool.wait_ge(prep, 2)
            nc.gpsimd.tensor_tensor(gm[:, 1], dev[:], expo[:], ALU.pow).then_inc(pch, 1)

        @block.scalar
        def _(act):
            def copy_y(buf, n):
                for j in range(2):
                    act.wait_ge(y_ps[buf], n * 2 + (j + 1) + 1)
                    act.wait_ge(f_ps[buf], n + 1)
                    for cs in range(2):
                        last = nc.scalar.copy(y[buf][:, :, cs, 2 * j:2 * j + 2, :].rearrange("p x c (a k) -> p x (c a) k", a=2),
                                              b1[buf][j][:].rearrange("p (x c t k) -> p t x c k", x=2, c=4, t=2)[:, cs])
                    last.then_inc(y_ready[buf], 1)

            def copy_f(buf, n, half, i):
                act.wait_ge(f_ps[buf], n + 1 + 1)
                for pair in range(2):
                    k = i * 4 + 2 * buf + pair
                    last = nc.scalar.activation(fs[half][:, k, :], b2[buf][:, pair * P:(pair + 1) * P], ACT.Copy,
                                                scale=rs_now[:, 2 * (8 * half + k):2 * (8 * half + k) + 1])
                last.then_inc(f_ready[buf], 1)

            with act.Fori(0, S) as s:
                act.wait_ge(norm_ready, 1)
                nc.scalar.copy(rs_now[:], norm[:, 1, bass.ds(s, 1), :].rearrange("p a c -> p (a c)")).then_inc(rs_ready, 1)
                act.wait_ge(rs_ready, s + 1)
                for half in range(2):
                    act.wait_ge(f_out[half], s * 64 + 1)
                    for i in range(2):
                        n = act.snap(s * 4 + (half * 2 + i))
                        copy_y(0, n)
                        copy_y(1, n)
                        copy_f(0, n, half, i)
                        copy_f(1, n, half, i)
                    n1 = act.snap(s * 4 + (half * 2 + 2))
                    act.wait_ge(f_ready[0], n1 + 1)
                    act.wait_ge(f_ready[1], n1 + 1)
                    for c in range(2):
                        for a in range(2):
                            p0 = c * M + a * 32
                            act.dma_start(fv[s, c, a, :, 8 * half:8 * half + 8, :], fs[half][p0:p0 + 32]).then_inc(f_out[half], 16)
            for half in range(2):
                act.wait_ge(f_out[half], 64 * S + 1)


def build_mix(nc, f_d, w, t_d, S):
    f32 = mybir.dt.float32
    T = 4
    with ExitStack() as ctx:
        sb = lambda n, s: ctx.enter_context(nc.sbuf_tensor("m_" + n, s, f32))
        ps = lambda n, s: ctx.enter_context(nc.psum_tensor("m_" + n, s, f32))
        sem = lambda n: ctx.enter_context(nc.semaphore("m_" + n))
        ft = [sb(f"ft{i}", [P, S, T, M]) for i in range(2)]
        wt = [sb(f"wt{i}", [P, C, T, M]) for i in range(2)]
        wr = sb("wr", [P, C, T, M])
        to = [sb(f"to{i}", [P, S, M]) for i in range(2)]
        bank = [[[ps(f"bank{i}{g}{h}", [P, 512]) for h in range(2)] for g in range(2)] for i in range(2)]
        here = [sem(f"here{i}") for i in range(2)]
        wr_here, turned, emptied, passed = (sem(n) for n in ("wr_here", "turned", "emptied", "passed"))
        done = sem("done")
        packed = [sem(f"packed{g}") for g in range(2)]
        gone = [sem(f"gone{g}") for g in range(2)]
        block = ctx.enter_context(nc.Block())
        NCK = M // 2 // T
        re = lambda g: slice(g * M, g * M + C)
        im = lambda g: slice(g * M + C, (g + 1) * M)

        @block.sync
        def _(sp):
            for k in range(NCK):
                buf = k % 2
                if k >= 2:
                    sp.wait_ge(done, k - 1)
                for g in range(2):
                    y0 = 32 * g + T * k
                    for part, p in ((0, re(g)), (1, im(g))):
                        for t in range(T):
                            sp.dma_start(ft[buf][p, :, t, :], f_d[:, :, y0 + t, part * M:(part + 1) * M].rearrange("b i n -> i b n")
                                         ).then_inc(here[buf], 16)
                    sp.dma_start(wt[buf][re(g)], w[:, :, y0:y0 + T, :].rearrange("i o t x -> i o (t x)")).then_inc(here[buf], 16)
                if k:
                    sp.wait_ge(turned, k)
                for g in range(2):
                    y0 = 32 * g + T * k
                    lo, n = M - y0 - T + 1, T if y0 else T - 1
                    sp.dma_start(wr[im(g), :, 0:n], w[:, :, lo:lo + n, :].rearrange("i o t x -> i o (t x)")).then_inc(wr_here, 16)
                    if n < T:
                        sp.dma_start(wr[im(g), :, n], w[:, :, 0, :]).then_inc(wr_here, 16)
            for g in range(2):
                sp.wait_ge(gone[g], 16 * NCK)

        @block.tensor
        def _(pe):
            def chunk(buf, n):
                for kx in range(M):
                    half, col = kx // 32, (kx % 32) * S
                    for t in range(T):
                        for g in range(2):
                            pg = slice(g * M, (g + 1) * M)
                            last = nc.tensor.matmul(bank[buf][g][half][t * C:(t + 1) * C, col:col + S], wt[buf][pg, :, t, kx],
                                                    ft[buf][pg, :, t, kx], start=True, stop=True)
                last.then_inc(done, 1)

            with pe.Fori(1, NCK // 2 + 1) as k2:
                for buf in range(2):
                    pe.wait_ge(here[buf], k2 * (18 * 16))
                    pe.wait_ge(turned, k2 * 2 + (buf - 1))
                    pe.wait_ge(emptied, k2 * 2 + (buf - 1))
                    pe.sem_inc(passed, 1)
                    chunk(buf, k2)

        @block.vector
        def _(dve):
            dve.sem_inc(emptied, 2)

            def turn(k):
                dve.wait_ge(wr_here, 16 * (2 * k + 3))
                if k >= 2:
                    dve.wait_ge(done, k - 1)
                for g in range(2):
                    for t in range(T):
                        p, dst, src = im(g), wt[k % 2][im(g), :, t, :], wr[im(g), :, T - 1 - t, :]
                        nc.vector.tensor_copy(dst[:, :, 0:1], src[:, :, 0:1])
                        last = nc.vector.tensor_copy(dst[:, :, 1:M], src[:, :, :0:-1])
                last.then_inc(turned, 1)

            def pack(k):
                for g in range(2):
                    dve.wait_ge(done, k + 1)
                    if k:
                        dve.wait_ge(gone[g], 16 * k)
                    for half in range(2):
                        last = nc.vector.tensor_copy(to[g][:, :, 32 * half:32 * half + 32],
                                                     bank[k % 2][g][half][:, 0:32 * S].rearrange("p (x b) -> p b x", b=S))
                    last.then_inc(packed[g] if g == 0 else emptied, 1)

            turn(0)
            for k in range(NCK):
                if k + 1 < NCK:
                    turn(k + 1)
                pack(k)

        @block.scalar
        def _(act):
            for k in range(NCK):
                for g in range(2):
                    y0 = 32 * g + k * T
                    if g == 0:
                        act.wait_ge(packed[0], k + 1)
                    else:
                        act.wait_ge(emptied, k + 3)
                    act.dma_start(t_d[:, y0:y0 + T].rearrange("b t o x -> (t o) b x"), to[g][:]).then_inc(gone[g], 16)


def build_inverse(nc, t_d, x1d, bias, spec, out_d, S):
    f32 = mybir.dt.float32
    ALU = mybir.AluOpType
    NB = 4
    with ExitStack() as ctx:
        sb = lambda n, s: ctx.enter_context(nc.sbuf_tensor("i_" + n, s, f32))
        ps = lambda n, s: ctx.enter_context(nc.psum_tensor("i_" + n, s, f32))
        sem = lambda n: ctx.enter_context(nc.semaphore("i_" + n))
        back = sb("back", [P, 2 * IMG])
        back_h, back_w = back[:, 0:IMG], back[:, IMG:2 * IMG]
        bias_bc = sb("bias_bc", [P, C])
        t2 = [sb(f"t2{i}", [P, 16, P]) for i in range(2)]
        tt = sb("tt", [P, 16, M])
        u = [sb(f"u{i}", [P, IMG]) for i in range(2)]
        xt = [sb(f"xt{i}", [P, 2, 4, IMG]) for i in range(NB)]
        ot = [sb(f"ot{i}", [P, 2, 4, IMG]) for i in range(NB)]
        ub = [ps(f"ub{i}", [P, 512]) for i in range(2)]
        ob = [ps(f"ob{i}", [P, 512]) for i in range(4)]
        here, zeroed, u_ps, u_ready, o_ps, o_ready = (sem(n) for n in ("here", "zeroed", "u_ps", "u_ready", "o_ps", "o_ready"))
        t_here = sem("t_here")
        t2_ready = [sem(f"t2_ready{i}") for i in range(2)]
        x_here = [sem(f"x_here{i}") for i in range(NB)]
        gone = [sem(f"gone{i}") for i in range(NB)]
        block = ctx.enter_context(nc.Block())
        xv = x1d.rearrange("s c (a p) w -> s a p c w", p=P)
        ov = out_d.rearrange("s c (a p) w -> s a p c w", p=P)

        @block.sync
        def _(sp):
            sp.dma_start(back[:], spec[:, OFF_BACK:OFF_BACK + 2 * IMG]).then_inc(here, 16)
            sp.dma_start(bias_bc[:], bias.rearrange("c a b -> (a b) c").to_broadcast([P, C])).then_inc(here, 16)

            def load_t(s):
                for h in range(2):
                    sp.dma_start(tt[h * M:(h + 1) * M], t_d[s, :, 16 * h:16 * h + 16, :]).then_inc(t_here, 16)

            load_t(0)
            with sp.Fori(0, S) as s:
                for g in range(8):
                    if g == 6:
                        sp.wait_ge(t2_ready[1], s * 2 + 3)
                        load_t(sp.snap((s + 1) % S))
                    b = g % NB
                    sp.wait_ge(o_ready, (s * 32 + 4 * (g - NB) + 4 if g >= NB else s * 32) + 1)
                    for a in range(2):
                        sp.dma_start(xt[b][:, a], xv[s, a, :, 4 * g:4 * g + 4, :]).then_inc(x_here[b], 16)
            for b in range(NB):
                sp.wait_ge(gone[b], 32 * 2 * S + 1)
            sp.wait_ge(t_here, 32 * (S + 1))

        @block.tensor
        def _(pe):
            pe.wait_ge(here, 32)

            def over_ky(c, n):
                pe.wait_ge(u_ready, (n - 1 if c else n) + 1)
                nc.tensor.matmul(ub[c % 2][:, 0:IMG], t2[c // 16][:, c % 16, :], back_h, start=True, stop=True).then_inc(u_ps, 1)

            with pe.Fori(0, S) as s:
                n0 = pe.snap(s * C)
                pe.wait_ge(t2_ready[0], s * 2 + 3)
                over_ky(0, n0)
                for c in range(C):
                    if c + 1 == 16:
                        pe.wait_ge(t2_ready[1], s * 2 + 3)
                    if c + 1 < C:
                        over_ky(c + 1, n0 + (c + 1))
                    pe.wait_ge(u_ready, n0 + (c + 1) + 1)
                    pe.wait_ge(o_ready, (n0 + (c - 3) if c >= 3 else n0) + 1)
                    for a in range(2):
                        last = nc.tensor.matmul(ob[c % 4][:, a * IMG:(a + 1) * IMG], u[c % 2][:, a * P:(a + 1) * P], back_w,
                                                start=True, stop=True)
                    last.then_inc(o_ps, 1)

        @block.scalar
        def _(act):
            def store(s, n0, g):
                act.wait_ge(o_ready, n0 + (4 * g + 5))
                for a in range(2):
                    act.dma_start(ov[s, a, :, 4 * g:4 * g + 4, :], ot[g % NB][:, a]).then_inc(gone[g % NB], 16)

            def spread(h, k, used):
                act.wait_ge(t_here, k * 32)
                act.wait_ge(u_ps, used + 1)
                nc.scalar.copy(t2[h][0:M, :, 0:M], tt[h * M:(h + 1) * M]).then_inc(t2_ready[h], 1)

            act.wait_ge(zeroed, 1)
            spread(0, 1, 0)
            spread(1, 1, 0)
            with act.Fori(0, S) as s:
                n0 = act.snap(s * C)
                for c in range(C):
                    act.wait_ge(u_ps, n0 + (c + 1) + 1)
                    act.wait_ge(o_ps, (n0 + (c - 1) if c else n0) + 1)
                    nc.scalar.copy(u[c % 2][:], ub[c % 2][:, 0:IMG]).then_inc(u_ready, 1)
                    if c % 4 == 2 and c > 4:
                        store(s, n0, c // 4 - 1)
                    if c == C - 4:
                        spread(0, s + 2, n0 + 16)
                spread(1, s + 2, n0 + C)
                store(s, n0, C // 4 - 1)

        @block.vector
        def _(dve):
            for counter in (o_ps, o_ready, u_ready, u_ps, *gone, *t2_ready):
                dve.sem_inc(counter, 1)

            def spread(h, k, used):
                dve.wait_ge(t_here, k * 32)
                dve.wait_ge(u_ps, used + 1)
                nc.vector.tensor_copy(t2[h][M:P, :, M:P], tt[h * M:(h + 1) * M]).then_inc(t2_ready[h], 1)

            nc.vector.memset(t2[0][:], 0.0)
            nc.vector.memset(t2[1][:], 0.0).then_inc(zeroed, 1)
            dve.wait_ge(zeroed, 1)
            spread(0, 1, 0)
            spread(1, 1, 0)
            dve.wait_ge(here, 32)
            with dve.Fori(0, S) as s:
                n0 = dve.snap(s * C)
                for c in range(C):
                    g = c // 4
                    b = g % NB
                    if c % 4 == 0:
                        dve.wait_ge(x_here[b], s * 64 + (g // NB) * 32 + 32)
                        dve.wait_ge(gone[b], s * 64 + (g // NB) * 32 + 1)
                    dve.wait_ge(o_ps, n0 + (c + 1) + 1)
                    nc.vector.scalar_tensor_tensor(ot[b][:, :, c % 4, :], ob[c % 4][:].rearrange("p (a w) -> p a w", a=2),
                                                   bias_bc[:, c:c + 1], xt[b][:, :, c % 4, :], ALU.add, ALU.add).then_inc(o_ready, 1)
                    if c == C - 4:
                        spread(0, s + 2, n0 + 16)
                spread(1, s + 2, n0 + C)


def build(nc, x, w_c1, w_c2, weight1, weight2, weight3, mode_w, bias, consts, spec, out):
    f32, S = mybir.dt.float32, x.shape[0]
    scratch = lambda name, shape: nc.dram_tensor(name, shape, f32, kind="Internal").ap()
    x1 = scratch("x1", [S, C, IMG, IMG])
    x1_stats = scratch("x1_stats", [P, S, 2])
    modes = scratch("modes", [S, C, M, 2 * M])
    mixed_modes = scratch("mixed_modes", [S, M, C, M])
    build_convs(nc, x, w_c1, w_c2, weight1, weight2, weight3, consts, x1, x1_stats, S)
    build_forward(nc, x1, x1_stats, spec, modes, S)
    build_mix(nc, modes, mode_w, mixed_modes, S)
    build_inverse(nc, mixed_modes, x1, bias, spec, out, S)


_INS = ["x", "L0_conv_w_c1", "L0_conv_w_c2", "L0_conv_weight1", "L0_conv_weight2", "L0_conv_weight3",
        "L1_conv_weight", "L1_conv_bias"]


def kernel(**inputs):
    import concourse.bacc as bacc
    from concourse.bass_utils import run_bass_kernel_spmd

    nc = bacc.Bacc("TRN2", target_bir_lowering=False, num_devices=1)
    arrays = {f"in_{name}": np.ascontiguousarray(inputs[name]) for name in _INS}
    arrays["consts"] = constants()
    arrays["spec"] = spectral_constants()
    args = [nc.dram_tensor(n, a.shape, mybir.dt.from_np(a.dtype), kind="ExternalInput").ap() for n, a in arrays.items()]
    out = nc.dram_tensor("out", inputs["x"].shape, mybir.dt.float32, kind="ExternalOutput").ap()
    build(nc, *args, out)
    r = run_bass_kernel_spmd(nc, [arrays], core_ids=[0])
    return r.results[0]["out"]
```

```python
import numpy as np
import concourse.bass as bass
from concourse import mybir
from contextlib import ExitStack

P = 128
C = 32
IMG = 256
W2 = IMG + 2
E = 4
TAPS = 9
Q = 4
CHUNK = 2
NCH = 33
SLOTS = 3
CREDIT = 3
WSCALE = 1024.0
HALF = 2.0
TEMP = 30.0
EPS = 1e-5
MW = 3 * 64


def constants():
    c4 = np.arange(P) // 4
    cq = np.arange(P) % C
    same_group = (c4[:, None] // 2 == c4[None, :] // 2) / 8.0
    to_group = (c4[:, None] // 2 == cq[None, :] // 2) / 8.0
    to_channel = (c4[:, None] == cq[None, :]) / 4.0
    ident = np.eye(P)
    q = np.arange(P) // C
    masks = np.zeros((P, 8))
    masks[:, 0] = (q >= 1) / WSCALE
    masks[:, 1] = (q == 0) / WSCALE
    masks[:, 2] = (q >= 2) / (WSCALE * HALF)
    masks[:, 3] = (q <= 1) / (WSCALE * HALF)
    groupq = (cq[:, None] // 2 == cq[None, :] // 2) / 8.0
    return np.concatenate([same_group, to_group, to_channel, ident, groupq, masks], axis=1).astype(np.float32)


NCONST = 5 * P + 8


def build_convs(nc, x, w_c1, w_c2, w1, w2, w3, consts, x1d, stats1_d, S):
    f32, f16 = mybir.dt.float32, mybir.dt.float16
    ALU, ACT, AX = mybir.AluOpType, mybir.ActivationFunctionType, mybir.AxisListType
    experts_d = [w1, w2, w3]

    with ExitStack() as ctx:
        sb = lambda n, s, d=f32: ctx.enter_context(nc.sbuf_tensor(n, s, d))
        ps = lambda n, s, d=f32: ctx.enter_context(nc.psum_tensor(n, s, d))
        sem = lambda n: ctx.enter_context(nc.semaphore(n))

        cst = sb("cst", [P, NCONST])
        same_group, to_group, to_channel, ident = (cst[:, i * P:(i + 1) * P] for i in range(4))
        mask = lambda i: cst[:, 5 * P + i:5 * P + i + 1]
        zero = mask(4)

        x_in = {k: sb(f"x_in_{k}", [P, 6, IMG]) for k in "CAB"}
        st_in = {k: sb(f"st_in_{k}", [P, 4, 512]) for k in "AB"}
        res = {k: sb(f"res_{k}", [P, n, IMG]) for k, n in (("C", 2), ("A", 6), ("B", 6), ("D", 4))}
        out = {k: sb(f"out_{k}", [P, n, IMG]) for k, n in (("C", 2), ("A", 6), ("B", 6), ("D", 4))}
        ring = [{k: sb(f"ring{n}_{k}", [P, SLOTS * CHUNK, W2], f16) for k in ("Ahi", "Alo", "Bhi", "Blo")}
                for n in range(3)]
        xn = sb("xn", [P, CHUNK, IMG])
        ex = [sb(f"ex{n}", [P, E, 6, C]) for n in range(3)]
        mixed = sb("mixed", [P, E, 6, C])
        w_now = [sb(f"w_now{n}", [P, 2, MW], f16) for n in range(3)]
        w_next = [sb(f"w_next{n}", [P, 2, MW], f16) for n in range(3)]
        stage = sb("stage", [P, 3, C * TAPS])
        taps = sb("taps", [P, 3, 3, 5, C])
        sumsq = sb("sumsq", [P, 3])
        maxsq = sb("maxsq", [P, 3])
        norms = sb("norms", [P, 3])
        alpha = sb("alpha", [P, 3])
        final_scale = sb("final_scale", [P, 1])
        wc1_in = sb("wc1_in", [8, C])
        wc1t = sb("wc1t", [P, 8])
        wc1r = sb("wc1r", [8, P])
        wc2_in = sb("wc2_in", [P, 8])
        wc2t = sb("wc2t", [8, P])
        ones = sb("ones", [P, P])
        bn0 = sb("bn0", [P, 32, 6])
        bn1 = sb("bn1", [P, NCH, 6])
        mv = sb("mv", [P, 2])
        mv1 = sb("mv1", [P, S, 2])
        mv1_now = sb("mv1_now", [P, 2])
        dev = sb("dev", [P, 2])
        me = sb("me", [P, 2])
        stq = sb("stq", [P, 3])
        norm_next = sb("norm_next", [P, 2])
        norm_now = sb("norm_now", [P, 2])
        var_eps = sb("var_eps", [P, 1])
        minus_half = sb("minus_half", [P, 1])
        gap = sb("gap", [P, 1])
        gapb = sb("gapb", [P, P])
        hbs = sb("hbs", [8, P])
        mx = sb("mx", [P, C])
        lg = sb("lg", [P, C, E])
        ex_l = sb("ex_l", [P, C, E])
        den = sb("den", [P, C])
        rden = sb("rden", [P, C])
        coeff = sb("coeff", [P, E, C])
        first = sb("first", [P, 8, 512 * 4])

        bank = [[ps(f"bank{n}{i}", [P, 512]) for i in range(2)] for n in range(3)]
        prep_ps = ps("prep_ps", [P, 512])
        prep_ps2 = ps("prep_ps2", [P, 512])

        first_in = [sem(f"first{i}_in") for i in range(4)]
        loaded, sq_done, mx_done, tr_done, ex_done, zeroed, dch, pch, ach, tiny, res_zeroed, rings_zeroed, passed = (
            sem(n) for n in ("loaded", "sq_done", "mx_done", "tr_done", "ex_done", "zeroed",
                             "dch", "pch", "ach", "tiny", "res_zeroed", "rings_zeroed", "passed"))
        x_here = {k: sem(f"x_here_{k}") for k in "CAB"}
        st_here = {k: sem(f"st_here_{k}") for k in "AB"}
        res_here = {k: sem(f"res_here_{k}") for k in "CABD"}
        stored = {k: sem(f"stored_{k}") for k in "CABD"}
        hi_ready = [sem(f"hi{n}_ready") for n in range(3)]
        lo_ready = [sem(f"lo{n}_ready") for n in range(3)]
        bhi_ready = [sem(f"bhi{n}_ready") for n in range(3)]
        blo_ready = [sem(f"blo{n}_ready") for n in range(3)]
        conv_done = [sem(f"conv{n}_done") for n in range(3)]
        x1_ready, x1_stat, stat_read, bn1_aggr = (sem(n) for n in ("x1_ready", "x1_stat", "stat_read", "bn1_aggr"))
        w_mixed = [sem(f"w{n}_mixed") for n in range(3)]
        w_ready = [sem(f"w{n}_ready") for n in range(3)]
        mean_ready, gm_ready, e_ready, stq_ps, stq_ready, gap_ready, hid_ps, hid_ready, log_ps, lg_ready, exp_ready, \
            coeff_ready, stored_stats = (
                sem(n) for n in ("mean_ready", "gm_ready", "e_ready", "stq_ps", "stq_ready", "gap_ready", "hid_ps",
                                 "hid_ready", "log_ps", "lg_ready", "exp_ready", "coeff_ready", "stored_stats"))

        block = ctx.enter_context(nc.Block())

        def rows(t, s, r0, n):
            return t[s, :, bass.ds(r0, n, 4) if not isinstance(r0, int) else slice(r0, r0 + 4 * (n - 1) + 1, 4), :]

        @block.sync
        def _(sp):
            sp.dma_start(cst[:], consts).then_inc(loaded, 16)
            for n in range(3):
                sp.dma_start(stage[:, n, :], experts_d[n].rearrange("e o c h w -> (e o) (c h w)")).then_inc(loaded, 16)
            sp.dma_start(wc1_in[:], w_c1).then_inc(loaded, 16)
            sp.dma_start(wc2_in[:], w_c2).then_inc(loaded, 16)
            for i in range(4):
                sp.dma_start(first[:, 2 * i:2 * i + 2, :],
                             x[0].rearrange("c (r h) w -> (c r) (h w)", r=4)
                             [:, 4096 * i:4096 * (i + 1)].rearrange("p (a b) -> p a b", a=2)).then_inc(first_in[i], 16)

            xs = x.rearrange("s c (b q) w -> s q c b w", q=Q)
            x1s = x1d.rearrange("s c (b q) w -> s q c b w", q=Q)
            xflat = x.rearrange("s c (r h) w -> s (c r) (h w)", r=4)

            def load_x(buf, s, b0, n):
                for q in range(Q):
                    sp.dma_start(x_in[buf][q * C:(q + 1) * C, 0:n, :], xs[s, q, :, bass.ds(b0, n), :]).then_inc(x_here[buf], 16)

            def shifted(t, s, q, b0, n):
                return t[s, 0, :, bass.ds(b0, n), :] if q == 3 else t[s, q + 1, :, bass.ds(b0 - 1, n), :]

            def load_res(buf, s, b0):
                for q in range(Q):
                    sp.dma_start(res[buf][q * C:(q + 1) * C, :, :], shifted(xs, s, q, b0, 6)).then_inc(res_here[buf], 16)

            def store_out(buf, s, b0):
                for q in range(Q):
                    sp.dma_start(shifted(x1s, s, q, b0, 6), out[buf][q * C:(q + 1) * C, :, :]).then_inc(stored[buf], 16)

            def load_stat(buf, s, k):
                sp.dma_start(st_in[buf][:, :, :], xflat[s, :, bass.ds(2048 * k, 2048)].rearrange("p (a b) -> p a b", a=4)
                             ).then_inc(st_here[buf], 16)

            def edge(q):
                return ((0, 2), (0, 2)) if q == 3 else ((1, 1), (0, 3))

            def load_c(s):
                load_x("C", s, 0, 6)
                for q in range(Q):
                    b, n = edge(q)[0]
                    sp.dma_start(res["C"][q * C:(q + 1) * C, b:b + n, :], shifted(xs, s, q, b, n)).then_inc(res_here["C"], 16)

            def load_first(s, s2):
                load_c(s)
                for g, buf in ((1, "A"), (2, "B")):
                    load_x(buf, s, 6 * g, 6)
                    load_res(buf, s, 6 * g - 4)
                    load_stat(buf, s2, g - 1)

            sp.wait_ge(res_zeroed, 1)
            load_first(0, 1 % S)
            with sp.Fori(0, S) as s:
                nxt = sp.snap((s + 1) % S)
                n0 = sp.snap(s * NCH)
                with sp.Fori(0, 3) as i:
                    ni = sp.snap(n0 + i * 6)
                    for k, buf in ((0, "A"), (1, "B")):
                        g = 1 + k
                        sp.wait_ge(x1_ready, ni + (3 * g + 1) + 1)
                        store_out(buf, s, i * 12 + (6 * g - 4))
                        sp.wait_ge(lo_ready[0], ni + (3 * g + 3) + 1)
                        load_x(buf, s, i * 12 + 6 * (g + 2), 6)
                        load_res(buf, s, i * 12 + (6 * (g + 2) - 4))
                        sp.wait_ge(stat_read, s * 8 + i * 2 + (k + 1))
                        load_stat(buf, nxt, i * 2 + (g + 1))
                for g, buf in ((7, "A"), (8, "B")):
                    sp.wait_ge(x1_ready, n0 + (3 * g + 1) + 1)
                    store_out(buf, s, 6 * g - 4)
                    sp.wait_ge(lo_ready[0], n0 + (3 * g + 3) + 1)
                    load_x(buf, s, 6 * (g + 2), 6 if g == 7 else 4)
                    load_res(buf, s, 6 * (g + 2) - 4)
                    if g == 7:
                        for q in range(Q):
                            b, n = edge(q)[0]
                            sp.dma_start(shifted(x1s, s, q, b, n), out["C"][q * C:(q + 1) * C, b:b + n, :]).then_inc(stored["C"], 16)
                        for q in range(Q):
                            b, n = edge(q)[1]
                            sp.dma_start(res["D"][q * C:(q + 1) * C, b:b + n, :], shifted(xs, s, q, 62 + b, n)).then_inc(res_here["D"], 16)
                        load_c(nxt)
                nxt2 = sp.snap((s + 2) % S)
                sp.wait_ge(stat_read, s * 8 + 8)
                sp.sem_inc(passed, 1)
                for g, buf, done in ((1, "A", 9), (2, "B", 10)):
                    sp.wait_ge(x1_ready, n0 + (3 * done + 1) + 1)
                    store_out(buf, s, 6 * done - 4)
                    load_x(buf, nxt, 6 * g, 6)
                    load_res(buf, nxt, 6 * g - 4)
                    load_stat(buf, nxt2, g - 1)
                sp.wait_ge(x1_ready, n0 + NCH + 1)
                for q in range(Q):
                    b, n = edge(q)[1]
                    sp.dma_start(shifted(x1s, s, q, 62 + b, n), out["D"][q * C:(q + 1) * C, b:b + n, :]).then_inc(stored["D"], 16)
            sp.wait_ge(bn1_aggr, S)
            sp.dma_start(stats1_d, mv1[:]).then_inc(stored_stats, 16)
            for k, n in (("C", 1), ("A", 5), ("B", 5), ("D", 1)):
                sp.wait_ge(stored[k], 64 * n * S + 1)
                if k != "D":
                    sp.wait_ge(x_here[k], 64 * (n * S + 1))
                sp.wait_ge(res_here[k], 64 * (n * S + (k != "D")))
                if k in "AB":
                    sp.wait_ge(st_here[k], 16 * (4 * S + 1))
            sp.wait_ge(stored_stats, 16)

        def taps_view(m, n, dx):
            return taps[:, n, dx, 1 - m:5 - m, :]

        def copy_b(engine, n, kind, slot):
            a, b = ring[n]["A" + kind], ring[n]["B" + kind]
            s0 = slot * CHUNK
            v = lambda t, p, i, k: t[p * 64:(p + 1) * 64, i:i + k, :].bitcast(f32)
            engine(v(b, 1, s0, 2), v(a, 0, s0, 2))
            if slot:
                return engine(v(b, 0, s0, 2), v(a, 1, s0 - 1, 2))
            engine(v(b, 0, 0, 1), v(a, 1, SLOTS * CHUNK - 1, 1))
            return engine(v(b, 0, 1, 1), v(a, 1, 0, 1))

        def spans(n, t, base):
            if t == 0:
                return [(0, 1, mask(0 if n == 1 else 2)), (1, 1, base)]
            if t == NCH - 1:
                return [(0, 1, mask(1 if n == 1 else 3)), (1, 1, None)]
            return [(0, 2, base)]

        @block.tensor
        def _(pe):
            pe.wait_ge(loaded, 6 * 16)
            pe.wait_ge(zeroed, 1)
            for k in range(18):
                n, m, dx = k // 6, (k // 3) % 2, k % 3
                if k >= 2:
                    pe.wait_ge(ex_done, k - 1)
                dst = (prep_ps, prep_ps2)[k % 2]
                nc.tensor.matmul(dst[:, 0:P], taps_view(m, n, dx), ident, start=True, stop=True).then_inc(tr_done, 1)
            pe.wait_ge(ex_done, 18)
            pe.wait_ge(tiny, 1)
            nc.tensor.matmul(prep_ps[:, 0:8], wc1r[:], cst[0:8, 3 * P:3 * P + 8], start=True, stop=True)
            nc.tensor.matmul(prep_ps2[0:8, 0:P], wc2_in[:], ident, start=True, stop=True).then_inc(tr_done, 1)
            pe.wait_ge(tiny, 2)

            def group_mean(k):
                pe.wait_ge(mean_ready, k + 1)
                nc.tensor.matmul(prep_ps[:, 0:1], same_group, mv[:, 0:1], start=True, stop=True).then_inc(gm_ready, 1)

            def moments(k):
                pe.wait_ge(e_ready, k + 1)
                nc.tensor.matmul(prep_ps2[:, 0:2], to_group, me[:, 0:2], start=True, stop=True)
                nc.tensor.matmul(prep_ps[:, 0:1], to_channel, me[:, 0:1], start=True, stop=True).then_inc(stq_ps, 1)

            def hidden(k):
                pe.wait_ge(gap_ready, k + 1)
                nc.tensor.matmul(prep_ps[0:8, 0:P], wc1t[:], gapb[:], start=True, stop=True).then_inc(hid_ps, 1)

            def logits(k):
                pe.wait_ge(hid_ready, k + 1)
                nc.tensor.matmul(prep_ps2[:, 0:P], hbs[:], wc2t[:], start=True, stop=True).then_inc(log_ps, 1)

            def conv(n, t, slot, count, first):
                pe.wait_ge(bhi_ready[n], count + (1 + CREDIT))
                pe.wait_ge(blo_ready[n], count + (1 + CREDIT))
                emptied = x1_ready if n == 2 else lo_ready[n + 1]
                pe.wait_ge(emptied, (count if first else count - 1) + 1)
                r, s0, dst = ring[n], slot * CHUNK, bank[n][t % 2]
                nb = 1 if t == NCH - 1 else CHUNK
                terms = [("hi", 0), ("lo", 0), ("hi", 1)]
                k = 0
                for dx in range(3):
                    for kind, w in terms:
                        for half, side in ((0, "B"), (1, "A")):
                            last = nc.tensor.matmul(dst[64 * half:64 * half + 64, 0:nb * IMG], w_now[n][:, w, 64 * dx:64 * dx + 64],
                                                    r[side + kind][:, s0:s0 + nb, dx:dx + IMG],
                                                    start=(k == 0), stop=(k == 8))
                        k += 1
                last.then_inc(conv_done[n], 1)

            def step(n0, t, after=(None, None, None), weights=None):
                for n in range(3):
                    m = (t - n) % NCH
                    if m == 0 and t >= n:
                        pe.wait_ge(w_ready[n], weights)
                    if t >= n:
                        conv(n, m, m % SLOTS, n0 + (t - n), m == 0)
                    if after[n] is not None:
                        after[n][0](after[n][1])

            group_mean(0)
            moments(0)
            hidden(0)
            logits(0)
            step(0, 0, weights=2)
            step(0, 1, weights=2)
            with pe.Fori(0, S) as s:
                n0 = pe.snap(s * NCH)
                k1 = pe.snap(s + 1)
                step(n0, 2, weights=k1 + 1)
                with pe.Fori(0, 4) as i:
                    ni = pe.snap(n0 + i * 6)
                    for t in range(3, 9):
                        step(ni, t)
                step(n0, 27, ((group_mean, k1), None, (moments, k1)))
                step(n0, 28, (None, None, (hidden, k1)))
                step(n0, 29, (None, (logits, k1), None))
                for t in range(30, NCH + 2):
                    step(n0, t, weights=k1 + 2)

        @block.scalar
        def _(act):
            act.wait_ge(loaded, 6 * 16)
            for n in range(3):
                nc.scalar.activation(mixed[:].rearrange("p e a o -> p (e a o)")[:, 0:C * TAPS], stage[:, n, :], ACT.Square,
                                     accum_out=sumsq[:, n:n + 1]).then_inc(sq_done, 1)
                act.wait_ge(sq_done, n + 1)
            act.wait_ge(mx_done, 1)
            nc.scalar.activation(norms[:], maxsq[:], ACT.Sqrt).then_inc(ach, 1)
            act.wait_ge(zeroed, 1)

            def softmax_exp(k):
                act.wait_ge(lg_ready, k + 1)
                nc.scalar.activation(ex_l[:], lg[:], ACT.Exp, scale=1.0 / TEMP).then_inc(exp_ready, 1)

            def b_ring(n, slot, count):
                act.wait_ge(hi_ready[n], count + 1)
                act.wait_ge(conv_done[n], count - 2 + CREDIT)
                copy_b(nc.scalar.copy, n, "hi", slot).then_inc(bhi_ready[n], 1)

            def hi(n, t, edges, count):
                act.wait_ge(conv_done[n - 1], count + (1 + CREDIT))
                act.wait_ge(conv_done[n], count - 2 + CREDIT)
                slot, src = t % SLOTS, bank[n - 1][t % 2]
                base = 1.0 / WSCALE if n == 1 else 1.0 / (WSCALE * HALF)
                for b, k, sc in spans(n, edges, base):
                    dst = ring[n]["Ahi"][:, slot * CHUNK + b:slot * CHUNK + b + k, 1:1 + IMG]
                    if sc is None:
                        last = nc.scalar.copy(dst, zero.unsqueeze(2).to_broadcast([P, 1, IMG]))
                        continue
                    last = nc.scalar.activation(dst, src[:, b * IMG:(b + k) * IMG].rearrange("p (b w) -> p b w", b=k),
                                                ACT.Copy, scale=sc)
                last.then_inc(hi_ready[n], 1)
                b_ring(n, slot, count)

            def step(n0, t, edges=False):
                m, up, down = (k % NCH for k in (t, t + 1, t - 1))
                hi(1, m, m if edges else None, n0 + t)
                b_ring(0, up % SLOTS, n0 + (t + 1))
                if t:
                    hi(2, down, down if edges else None, n0 + (t - 1))

            softmax_exp(0)
            b_ring(0, 0, 0)
            step(0, 0, True)
            step(0, 1, True)
            with act.Fori(0, S) as s:
                n0 = act.snap(s * NCH)
                step(n0, 2)
                with act.Fori(0, 4) as i:
                    ni = act.snap(n0 + i * 6)
                    for t in range(3, 9):
                        step(ni, t)
                for t in range(27, NCH + 2):
                    if t == 30:
                        softmax_exp(s + 1)
                    step(n0, t, True)

        @block.vector
        def _(dve):
            n_ch = [0]

            def link(ins):
                n_ch[0] += 1
                ins.then_inc(dch, 1)
                dve.wait_ge(dch, n_ch[0])

            nc.vector.memset(res["C"][:], 0.0)
            nc.vector.memset(res["D"][:], 0.0).then_inc(res_zeroed, 1)
            dve.wait_ge(res_zeroed, 1)
            link(nc.vector.memset(taps[:], 0.0))
            dve.wait_ge(loaded, 6 * 16)
            for n in range(3):
                nc.vector.tensor_copy(taps[:, n, :, 1:4, :], stage[:, n, :].rearrange("p (c y x) -> p x y c", y=3, x=3))
            nc.vector.memset(minus_half[:], -0.5)
            link(nc.vector.memset(ones[:], 1.0))
            for n in range(3):
                for counter in (conv_done[n], bhi_ready[n], blo_ready[n]):
                    dve.sem_inc(counter, CREDIT)
                dve.sem_inc(lo_ready[n], 1)
                dve.sem_inc(w_ready[n], 1)
            for counter in (x1_ready, x1_stat, *stored.values()):
                dve.sem_inc(counter, 1)
            nc.vector.memset(dev[:, 0:1], 0.0).then_inc(zeroed, 1)
            dve.wait_ge(ach, 1)
            link(nc.vector.tensor_scalar(alpha[:], norms[:], 1e-15, None, ALU.max))
            link(nc.vector.tensor_tensor(final_scale[:], alpha[:, 0:1], alpha[:, 1:2], ALU.mult))
            link(nc.vector.scalar_tensor_tensor(final_scale[:], final_scale[:], HALF / WSCALE, alpha[:, 2:3], ALU.mult, ALU.mult))
            link(nc.vector.reciprocal(alpha[:], alpha[:]))
            link(nc.vector.tensor_scalar(alpha[:], alpha[:], WSCALE, None, ALU.mult))

            def first_stats(k):
                if k % 8 == 0:
                    dve.wait_ge(first_in[k // 8], 16)
                return nc.vector.bn_stats(bn0[:, k, :], first[:, k // 4, (k % 4) * 512:(k % 4 + 1) * 512])

            for k in range(18):
                n, m, dx = k // 6, (k // 3) % 2, k % 3
                if k >= 2:
                    first_stats(k - 2)
                dve.wait_ge(tr_done, k + 1)
                src = (prep_ps, prep_ps2)[k % 2]
                nc.vector.tensor_scalar(ex[n][:, :, 2 * dx + m, :], src[:, 0:P].rearrange("p (e o) -> p e o", e=E),
                                        alpha[:, n:n + 1], None, ALU.mult).then_inc(ex_done, 1)
            dve.wait_ge(loaded, 6 * 16)
            for q in range(Q):
                nc.vector.tensor_scalar(wc1r[:, q * C:(q + 1) * C], wc1_in[:], 0.25, None, ALU.mult)
            nc.vector.memset(dev[:, 1:2], 0.0).then_inc(tiny, 1)
            dve.wait_ge(tr_done, 19)
            link(nc.vector.tensor_copy(wc1t[:], prep_ps[:, 0:8]))
            nc.vector.tensor_copy(wc2t[:], prep_ps2[0:8, 0:P]).then_inc(tiny, 1)
            dve.wait_ge(tiny, 2)
            for k in range(16, 32):
                ins = first_stats(k)
            link(ins)

            dk = [0]

            def chain(ins, n_before):
                dk[0] += 1
                ins.then_inc(dch, 1)
                dve.wait_ge(dch, n_before + dk[0])

            def take_mean(k, nb):
                dve.sem_inc(passed, 1)
                nc.vector.bn_aggr(mv[:], bn0[:].rearrange("p a b -> p (a b)")).then_inc(mean_ready, 1)
                dve.wait_ge(mean_ready, k + 1)

            def take_dev(k, nb):
                dve.wait_ge(gm_ready, k + 1)
                chain(nc.vector.tensor_tensor(dev[:, 0:1], mv[:, 0:1], prep_ps[:, 0:1], ALU.subtract), nb)
                chain(nc.vector.tensor_copy(me[:, 0:1], mv[:, 0:1]), nb)
                nc.vector.scalar_tensor_tensor(me[:, 1:2], dev[:, 0:1], dev[:, 0:1], mv[:, 1:2], ALU.mult, ALU.add
                                               ).then_inc(e_ready, 1)

            def take_moments(k, nb):
                dve.wait_ge(stq_ps, k + 1)
                chain(nc.vector.tensor_copy(stq[:, 0:2], prep_ps2[:, 0:2]), nb)
                nc.vector.tensor_copy(stq[:, 2:3], prep_ps[:, 0:1]).then_inc(stq_ready, 1)

            def take_hidden(k, nb):
                dve.wait_ge(hid_ps, k + 1)
                nc.vector.tensor_scalar(hbs[:], prep_ps[0:8, 0:P], 0.0, None, ALU.max).then_inc(hid_ready, 1)

            def take_logits(k, nb):
                dve.wait_ge(log_ps, k + 1)
                lp = prep_ps2[:, 0:P].rearrange("p (o e) -> p o e", e=E)
                chain(nc.vector.tensor_reduce(mx[:], lp, AX.X, ALU.max), nb)
                nc.vector.tensor_tensor(lg[:], lp, mx[:].unsqueeze(2).to_broadcast([P, C, E]), ALU.subtract
                                        ).then_inc(lg_ready, 1)

            def take_coeff(k, nb):
                dve.wait_ge(exp_ready, k + 1)
                chain(nc.vector.tensor_reduce(den[:], ex_l[:], AX.X, ALU.add), nb)
                chain(nc.vector.reciprocal(rden[:], den[:]), nb)
                nc.vector.tensor_tensor(coeff[:].rearrange("p e o -> p o e"), ex_l[:],
                                        rden[:].unsqueeze(2).to_broadcast([P, C, E]), ALU.mult).then_inc(coeff_ready, 1)

            def install(n, all_done, k):
                dve.wait_ge(w_mixed[n], k)
                dve.wait_ge(conv_done[n], all_done + CREDIT)
                nc.vector.tensor_copy(w_now[n][:], w_next[n][:]).then_inc(w_ready[n], 1)

            def b_ring(n, slot, count):
                dve.wait_ge(lo_ready[n], count + 1 + 1)
                dve.wait_ge(conv_done[n], count - 2 + CREDIT)
                copy_b(nc.vector.tensor_copy, n, "lo", slot).then_inc(blo_ready[n], 1)

            def lo(n, t, edges, count):
                dve.wait_ge(hi_ready[n], count + 1)
                dve.wait_ge(conv_done[n], count - 2 + CREDIT)
                slot, src = t % SLOTS, bank[n - 1][t % 2]
                base = 1.0 / WSCALE if n == 1 else 1.0 / (WSCALE * HALF)
                for b, k, sc in spans(n, edges, base):
                    at = lambda kind: ring[n][kind][:, slot * CHUNK + b:slot * CHUNK + b + k, 1:1 + IMG]
                    if sc is None:
                        last = nc.vector.memset(ring[n]["Alo"][:, slot * CHUNK + b, :].bitcast(f32), 0.0)
                        continue
                    last = nc.vector.scalar_tensor_tensor(at("Alo"), src[:, b * IMG:(b + k) * IMG].rearrange("p (b w) -> p b w", b=k),
                                                          sc, at("Ahi"), ALU.mult, ALU.subtract)
                last.then_inc(lo_ready[n], 1)
                b_ring(n, slot, count)

            def x1(t, buf, at_block, uses, bn_slot, count):
                dve.wait_ge(conv_done[2], count + (1 + CREDIT))
                if uses is not None:
                    dve.wait_ge(res_here[buf], uses * 64 + 64)
                    dve.wait_ge(stored[buf], uses * 64 + 1)
                nb = 1 if t == NCH - 1 else CHUNK
                dst = out[buf][:, at_block:at_block + nb, :]
                nc.vector.scalar_tensor_tensor(dst, bank[2][t % 2][:, 0:nb * IMG].rearrange("p (b w) -> p b w", b=nb),
                                               final_scale[:], res[buf][:, at_block:at_block + nb, :],
                                               ALU.mult, ALU.add).then_inc(x1_ready, 1)
                dve.wait_ge(x1_ready, count + 1 + 1)
                if t == 0:
                    nc.vector.bn_stats(bn1[:, 0, :], out[buf][:, 1, :])
                    last = nc.vector.bn_stats(bn1[96:128, 32, :], out[buf][96:128, 0, :])
                elif t == NCH - 1:
                    last = nc.vector.bn_stats(bn1[0:96, 32, :], out[buf][0:96, 2, :])
                else:
                    last = nc.vector.bn_stats(bn_slot, out[buf][:, at_block:at_block + CHUNK, :])
                last.then_inc(x1_stat, 1)

            def step(n0, t, x1_args=None, edges=False, extra=None):
                m, up, down = (k % NCH for k in (t, t + 1, t - 1))
                lo(1, m, m if edges else None, n0 + t)
                if extra is not None and t != NCH:
                    extra[0](*extra[1:])
                b_ring(0, up % SLOTS, n0 + (t + 1))
                if t:
                    lo(2, down, down if edges else None, n0 + (t - 1))
                if extra is not None and t == NCH:
                    extra[0](*extra[1:])
                if t >= 2:
                    x1(t - 2, *x1_args, n0 + (t - 2))

            nb0 = n_ch[0]
            take_mean(0, nb0)
            take_dev(0, nb0)
            take_moments(0, nb0)
            take_hidden(0, nb0)
            take_logits(0, nb0)
            take_coeff(0, nb0)
            b_ring(0, 0, 0)
            install(0, 0, 1)
            step(0, 0, edges=True)
            install(1, 0, 1)
            step(0, 1, edges=True)
            install(2, 0, 1)
            before = nb0 + dk[0]
            per_sample = dk[0] + 1
            with dve.Fori(0, S) as s:
                n0 = dve.snap(s * NCH)
                k1 = dve.snap(s + 1)
                nb = dve.snap(s * per_sample + before)
                dk[0] = 0
                step(n0, 2, ("C", 0, s, None))
                with dve.Fori(0, 4) as i:
                    ni = dve.snap(n0 + i * 6)
                    for t in range(3, 9):
                        buf, first_t, k = ("A", 3, 0) if t < 6 else ("B", 6, 1)
                        st = 4 * (2 * i + k)
                        if t == first_t:
                            dve.wait_ge(st_here[buf], s * 64 + i * 16 + 16)
                        for c in ((0, 1), (2,), (3,))[t - first_t]:
                            ins = nc.vector.bn_stats(bn0[:, bass.ds(i * 8 + (4 * k + c), 1), :], st_in[buf][:, c, :])
                        if t - first_t == 2:
                            ins.then_inc(stat_read, 1)
                        step(ni, t, (buf, 2 * (t - first_t), s * 5 + i if t == first_t else None,
                                     bn1[:, bass.ds(i * 6 + (t - 2), 1), :]))
                dve.wait_ge(stat_read, s * 8 + 8)
                take_mean(k1, nb)
                k2 = dve.snap(s + 2)
                for t in range(27, NCH + 2):
                    buf, first_t = ("A", 27) if t < 30 else ("B", 30) if t < 33 else ("D", 33)
                    u = None if t != first_t else s if buf == "D" else s * 5 + 4
                    extra = {27: (take_dev, k1, nb), 29: (take_hidden, k1, nb), 30: (take_coeff, k1, nb),
                             NCH - 1: (install, 0, n0 + NCH, k2), NCH: (install, 1, n0 + NCH, k2)}.get(t)
                    step(n0, t, (buf, 2 * (t - first_t), u, bn1[:, t - 2, :] if t - 2 < 32 else None), edges=True, extra=extra)
                    if t == 27:
                        take_moments(k1, nb)
                    if t == 29:
                        take_logits(k1, nb)
                install(2, n0 + NCH, k2)
                dve.wait_ge(x1_stat, n0 + NCH + 1)
                dve.sem_inc(passed, 1)
                chain(nc.vector.bn_aggr(mv1_now[:], bn1[:].rearrange("p a b -> p (a b)")), nb)
                nc.vector.tensor_copy(mv1[:, bass.ds(s, 1), :].rearrange("p a b -> p (a b)"), mv1_now[:]).then_inc(bn1_aggr, 1)
                dve.wait_ge(bn1_aggr, k1)
                assert dk[0] == per_sample

        @block.gpsimd
        def _(pool):
            for n in range(3):
                for r in ring[n].values():
                    last = nc.gpsimd.memset(r[:].rearrange("p a b -> p (a b)").bitcast(f32), 0.0)
                if n == 0:
                    pool.wait_ge(sq_done, 3)
                    nc.gpsimd.partition_all_reduce(maxsq[:], sumsq[:], P, bass.bass_isa.ReduceOp.max).then_inc(mx_done, 1)
            last.then_inc(rings_zeroed, 1)
            pool.wait_ge(rings_zeroed, 1)
            pool.wait_ge(ex_done, 18)

            def norms_of(k, pb):
                pool.wait_ge(stq_ready, k + 1)
                pool.sem_inc(passed, 1)
                link(nc.gpsimd.tensor_scalar(var_eps[:], stq[:, 1:2], EPS, None, ALU.add), pb)
                link(nc.gpsimd.tensor_tensor(norm_next[:, 0:1], var_eps[:], minus_half[:], ALU.pow), pb)
                link(nc.gpsimd.tensor_scalar(norm_next[:, 1:2], stq[:, 0:1], norm_next[:, 0:1], -1.0, ALU.mult, ALU.mult), pb)
                link(nc.gpsimd.tensor_scalar(gap[:], stq[:, 2:3], norm_next[:, 0:1], norm_next[:, 1:2], ALU.mult, ALU.add), pb)
                nc.gpsimd.tensor_scalar(gapb[:], ones[:], gap[:], None, ALU.mult).then_inc(gap_ready, 1)
                pool.wait_ge(gap_ready, k + 1)
                pool.sem_inc(passed, 1)

            pk = [0]

            def link(ins, before):
                pk[0] += 1
                ins.then_inc(pch, 1)
                pool.wait_ge(pch, before + pk[0])
                pool.sem_inc(passed, 1)

            def weights(n, k, pb):
                link(nc.gpsimd.tensor_tensor(mixed[:], ex[n][:], coeff[:].unsqueeze(2).to_broadcast([P, E, 6, C]), ALU.mult), pb)
                link(nc.gpsimd.tensor_tensor(mixed[:, 0:2], mixed[:, 0:2], mixed[:, 2:4], ALU.add), pb)
                link(nc.gpsimd.tensor_tensor(mixed[:, 0:1], mixed[:, 0:1], mixed[:, 1:2], ALU.add), pb)
                m = mixed[:, 0].rearrange("p a o -> p (a o)")
                link(nc.gpsimd.tensor_scalar(w_next[n][:, 0], m, 1.0, None, ALU.mult), pb)
                nc.gpsimd.tensor_tensor(w_next[n][:, 1], m, w_next[n][:, 0], ALU.subtract).then_inc(w_mixed[n], 1)
                pool.wait_ge(w_mixed[n], k)
                pool.sem_inc(passed, 1)

            def normalise(t, buf, at_block, here, count, pb):
                if here is not None:
                    pool.wait_ge(x_here[buf], here)
                pool.wait_ge(lo_ready[0], count + 1)
                pool.wait_ge(conv_done[0], count - 2 + CREDIT)
                pool.wait_ge(bhi_ready[0], count - 1 + CREDIT)
                pool.wait_ge(blo_ready[0], count - 1 + CREDIT)
                pool.sem_inc(passed, 1)
                s0 = (t % SLOTS) * CHUNK
                hi, lo = (ring[0][k][:, s0:s0 + CHUNK, 1:1 + IMG] for k in ("Ahi", "Alo"))
                if t == NCH - 1:
                    nc.gpsimd.memset(ring[0]["Ahi"][:, s0:s0 + CHUNK, :].rearrange("p a b -> p (a b)").bitcast(f32), 0.0).then_inc(hi_ready[0], 1)
                    nc.gpsimd.memset(ring[0]["Alo"][:, s0:s0 + CHUNK, :].rearrange("p a b -> p (a b)").bitcast(f32), 0.0).then_inc(lo_ready[0], 1)
                    return
                src = x_in[buf][:, at_block:at_block + CHUNK, :]
                nc.gpsimd.tensor_scalar(hi, src, norm_now[:, 0:1], norm_now[:, 1:2], ALU.mult, ALU.add).then_inc(hi_ready[0], 1)
                link(nc.gpsimd.tensor_scalar(xn[:], src, norm_now[:, 0:1], norm_now[:, 1:2], ALU.mult, ALU.add), pb)
                pool.wait_ge(hi_ready[0], count + 1)
                nc.gpsimd.tensor_tensor(lo, xn[:], hi, ALU.subtract).then_inc(lo_ready[0], 1)

            def start(k, count, here, pb):
                pool.wait_ge(lo_ready[0], count + 1)
                pool.sem_inc(passed, 1)
                link(nc.gpsimd.tensor_scalar(norm_now[:], norm_next[:], 1.0, None, ALU.mult), pb)
                for n in range(3):
                    normalise(n, "C", 2 * n, here if n == 0 else None, count + n, pb)
                    pool.wait_ge(coeff_ready, k)
                    pool.wait_ge(w_ready[n], k)
                    pool.sem_inc(passed, 1)
                    weights(n, k, pb)

            norms_of(0, 0)
            start(1, 0, 64, 0)
            before = pk[0]
            in_loop, total = 6, before + 4 * 6 + 5
            pk[0] = 0
            with pool.Fori(0, S) as s:
                s1 = pool.snap(s + 1)
                n0 = pool.snap(s * NCH)
                pb = pool.snap(s * total + before)
                base = pk[0]
                with pool.Fori(0, 4) as i:
                    ni = pool.snap(n0 + i * 6)
                    pi = pool.snap(pb + i * in_loop)
                    for t in range(3, 9):
                        buf, first_t = ("A", 3) if t < 6 else ("B", 6)
                        normalise(t, buf, 2 * (t - first_t), s * 320 + i * 64 + 64 if t == first_t else None, ni + t, pi)
                assert pk[0] == base + in_loop
                pk[0] = base + 4 * in_loop
                for t in range(27, NCH):
                    buf, first_t = ("A", 27) if t < 30 else ("B", 30)
                    normalise(t, buf, 2 * (t - first_t), s * 320 + 320 if t == first_t else None, n0 + t, pb)
                    if t == 29:
                        norms_of(s1, pb)
                start(s + 2, n0 + NCH, s * 64 + 128, pb)
                assert pk[0] == total, (pk[0], total)
                pk[0] = 0


M = 64


def spectral_constants():
    k = np.arange(M) + (IMG // 2 - M // 2)
    ang = 2 * np.pi * ((np.arange(IMG)[:, None] * np.append(k, k[-1] + 1)[None, :]) % IMG) / IMG
    c65, s65 = np.cos(ang), np.sin(ang)
    c, s = c65[:, :M], s65[:, :M]
    half = lambda a: a.reshape(2, P, -1).transpose(1, 0, 2).reshape(P, -1)
    along_h = np.concatenate([c[:P, 0::2], s[:P, 0::2], c[:P, 1::2], s[:P, 1::2]], 1)
    cos_part = half(np.concatenate([c65, s65], 1))
    sin_part = half(np.concatenate([-s65, c65], 1))
    back_h = np.concatenate([c.T, s.T], 0)
    back_w = np.concatenate([(c + s).T, (c - s).T], 0) / (IMG * IMG)
    q, cc = np.arange(P) // C, np.arange(P) % C
    groupq = (cc[:, None] // 2 == cc[None, :] // 2) / 8.0
    pick = (q[:, None] == 0) & (cc[:, None] == np.arange(C)[None, :])
    return np.concatenate([along_h, cos_part, sin_part, back_h, back_w, groupq, pick], axis=1).astype(np.float32)


MW2 = 2 * (M + 1)
OFF_W, OFF_BACK = P, P + 4 * MW2
OFF_GROUP = OFF_BACK + 2 * IMG
OFF_PICK = OFF_GROUP + P
NSPEC = OFF_PICK + C


ROWS = 4


def mode_row(ky):
    order = lambda k: (k % 2) * 16 + k // 2
    return order(ky) if ky < M // 2 else M // 2 + order((M - ky) % (M // 2))


def turn_rows(copy, wt, wr):
    for g in range(2):
        p = slice(g * M + C, (g + 1) * M)
        for t in range(ROWS):
            copy(wt[p, :, t, 0:1], wr[p, :, ROWS - 1 - t, 0:1])
            last = copy(wt[p, :, t, 1:M], wr[p, :, ROWS - 1 - t, :0:-1])
    return last


def load_weights(engine, w, k, wt, here):
    for g in range(2):
        y0 = 32 * g + ROWS * k
        engine.dma_start(wt[g * M:g * M + C], w[:, :, y0:y0 + ROWS, :].rearrange("i o t x -> i o (t x)")).then_inc(here, 16)


def load_opposite(engine, w, k, wr, here):
    for g in range(2):
        y0 = 32 * g + ROWS * k
        lo, n = M - y0 - ROWS + 1, ROWS if y0 else ROWS - 1
        p = slice(g * M + C, (g + 1) * M)
        engine.dma_start(wr[p, :, 0:n], w[:, :, lo:lo + n, :].rearrange("i o t x -> i o (t x)")).then_inc(here, 16)
        if n < ROWS:
            engine.dma_start(wr[p, :, n], w[:, :, 0, :]).then_inc(here, 16)


def build_forward(nc, x1d, stats_d, spec, f_d, w, wt, wr, S):
    f32 = mybir.dt.float32
    ALU, ACT = mybir.AluOpType, mybir.ActivationFunctionType
    with ExitStack() as ctx:
        sb = lambda n, s: ctx.enter_context(nc.sbuf_tensor("f_" + n, s, f32))
        ps = lambda n, s: ctx.enter_context(nc.psum_tensor("f_" + n, s, f32))
        sem = lambda n: ctx.enter_context(nc.semaphore("f_" + n))
        cst = sb("cst", [P, NSPEC])
        along_h = lambda parity: cst[:, parity * M:(parity + 1) * M]
        part_w = lambda cs, wc: cst[:, OFF_W + (2 * cs + wc) * MW2:OFF_W + (2 * cs + wc + 1) * MW2]
        groupq = cst[:, OFF_GROUP:OFF_GROUP + P]
        pick = cst[:, OFF_PICK:OFF_PICK + C]
        mv = sb("mv", [P, S, 2])
        gm = sb("gm", [P, 2, S])
        dev = sb("dev", [P, S])
        var = sb("var", [P, S])
        expo = sb("expo", [P, S])
        ones = sb("ones", [P, P])
        spread = sb("spread", [P, 2, S, C])
        norm = sb("norm", [P, 2, S, C])
        mean_now = sb("mean_now", [P, C])
        rsq = sb("rsq", [P, 2, S, C // 4])
        rs_now = sb("rs_now", [P, 2, C // 4])
        rs_mid = sb("rs_mid", [P, 1])
        xt = [sb(f"xt{i}", [P, 2, 4, IMG]) for i in range(2)]
        xg = [sb(f"xg{i}", [P, 2, 4, IMG]) for i in range(2)]
        y = [sb(f"y{i}", [P, 2, 2, 4, M // 2]) for i in range(2)]
        y_mid = sb("y_mid", [P, 2, C])
        fs = [sb(f"fs{i}", [P, 2, 4, P]) for i in range(2)]
        f_mid = sb("f_mid", [C, P])
        b1 = [[ps(f"b1{i}{j}", [P, 512]) for j in range(2)] for i in range(2)]
        b2 = [ps(f"b2{i}", [P, 512]) for i in range(2)]
        bs = [ps(f"bs{i}", [P, 512]) for i in range(2)]
        here, pch, dch, pw, sp_ready, now_ready, prep, norm_ready, rs_ready = (
            sem(n) for n in ("here", "pch", "dch", "pw", "sp_ready", "now_ready", "prep", "norm_ready", "rs_ready"))
        x_here = [sem(f"x_here{i}") for i in range(2)]
        xg_ready = [sem(f"xg_ready{i}") for i in range(2)]
        y_ps = [sem(f"y_ps{i}") for i in range(2)]
        y_ready = [sem(f"y_ready{i}") for i in range(2)]
        f_ps = [sem(f"f_ps{i}") for i in range(2)]
        f_ready = [sem(f"f_ready{i}") for i in range(2)]
        f_out = [sem(f"f_out{i}") for i in range(2)]
        mid_ps, mid_ready, mid_out, w_here, w_turned = (
            sem(n) for n in ("mid_ps", "mid_ready", "mid_out", "w_here", "w_turned"))
        block = ctx.enter_context(nc.Block())
        xv = x1d.rearrange("s c (a p) w -> s a p c w", p=P)
        fv = f_d.rearrange("s (g c) (m r) n -> s c m r g n", c=4, m=2)

        @block.sync
        def _(sp):
            sp.dma_start(cst[:], spec).then_inc(here, 16)
            sp.dma_start(mv[:], stats_d).then_inc(here, 16)

            def load(buf, s, c0):
                for a in range(2):
                    sp.dma_start(xt[buf][:, a], xv[s, a, :, bass.ds(c0, 4), :]).then_inc(x_here[buf], 16)

            def load_eight(s, i, n):
                for buf in range(2):
                    sp.wait_ge(xg_ready[buf], n + 1)
                    load(buf, s, i * 8 + 4 * buf)

            def store(s, half):
                sp.wait_ge(f_ready[0], s * 4 + (half * 2 + 3))
                sp.wait_ge(f_ready[1], s * 4 + (half * 2 + 3))
                for c in range(4):
                    for m in range(2):
                        sp.dma_start(fv[s, c, m, m:32, 4 * half:4 * half + 4, :],
                                     fs[half][c * C + m:(c + 1) * C, m]).then_inc(f_out[half], 16)

            def store_rest(s):
                store(s, 1)
                sp.wait_ge(mid_ready, s + 2)
                sp.dma_start(f_d[s, :, M // 2, :], f_mid[:]).then_inc(mid_out, 16)

            for i in range(4):
                load_eight(0, i, i)
            store(0, 0)
            with sp.Fori(0, S - 1) as before:
                s = sp.snap(before + 1)
                n = sp.snap(s * 4)
                load_eight(s, 0, n)
                load_eight(s, 1, n + 1)
                store_rest(before)
                load_eight(s, 2, n + 2)
                load_eight(s, 3, n + 3)
                store(s, 0)
            store_rest(S - 1)
            for buf in range(2):
                sp.wait_ge(x_here[buf], 32 * 4 * S)
            for half in range(2):
                sp.wait_ge(f_out[half], 128 * S + 1)
            sp.wait_ge(mid_out, 16 * S + 1)

        @block.tensor
        def _(pe):
            pe.wait_ge(here, 32)
            nc.tensor.matmul(bs[0][:, 0:S], groupq, mv[:, :, 0], start=True, stop=True).then_inc(pw, 1)
            pe.wait_ge(prep, 1)
            nc.tensor.matmul(bs[1][:, 0:S], groupq, var[:], start=True, stop=True).then_inc(pw, 1)
            pe.wait_ge(sp_ready, 1)
            nc.tensor.matmul(bs[0][:, 0:S * C], ones[:], spread[:, 0].rearrange("p s c -> p (s c)"), start=True, stop=True)
            nc.tensor.matmul(bs[1][:, 0:S * C], ones[:], spread[:, 1].rearrange("p s c -> p (s c)"), start=True, stop=True).then_inc(pw, 1)

            def over_h(buf, n):
                pe.wait_ge(xg_ready[buf], n + 1 + 1)
                pe.wait_ge(y_ready[buf], n * 2 + 1)
                for c in range(4):
                    for wc in range(2):
                        for a in range(2):
                            at = ((wc * 2 + c % 2) * 2 + a) * M
                            last = nc.tensor.matmul(b1[buf][c // 2][:, at:at + M], xg[buf][:, a, c, wc * P:(wc + 1) * P],
                                                    along_h(a), start=True, stop=True)
                    if c % 2:
                        last.then_inc(y_ps[buf], 1)

            def over_w(buf, n):
                pe.wait_ge(y_ready[buf], n * 2 + 2 + 1)
                pe.wait_ge(f_ready[buf], n + 1)
                for k in range(4):
                    cs, wc = k // 2, k % 2
                    last = nc.tensor.matmul(b2[buf][:, 0:MW2], y[buf][:, wc, cs].rearrange("p c k -> p (c k)"),
                                            part_w(cs, wc), start=(k == 0), stop=(k == 3))
                last.then_inc(f_ps[buf], 1)

            with pe.Fori(0, S) as s:
                with pe.Fori(0, 4) as i:
                    n = pe.snap(s * 4 + i)
                    over_h(0, n)
                    over_h(1, n)
                    over_w(0, n)
                    over_w(1, n)
                pe.wait_ge(mid_ready, s + 1)
                for wc in range(2):
                    last = nc.tensor.matmul(bs[0][0:C, 0:MW2], y_mid[:, wc, :], part_w(0, wc), start=(wc == 0), stop=(wc == 1))
                last.then_inc(mid_ps, 1)

        @block.vector
        def _(dve):
            k = [0]

            def link(ins):
                k[0] += 1
                ins.then_inc(dch, 1)
                dve.wait_ge(dch, k[0])

            for counters in (f_out, f_ps, xg_ready, y_ps, f_ready, y_ready, (mid_ps, mid_ready, mid_out)):
                for counter in counters:
                    dve.sem_inc(counter, 1)
            nc.vector.memset(ones[:], 1.0)
            link(nc.vector.memset(expo[:], -0.5))
            dve.wait_ge(here, 32)
            dve.wait_ge(pw, 1)
            link(nc.vector.tensor_copy(gm[:, 0], bs[0][:, 0:S]))
            link(nc.vector.tensor_tensor(dev[:], mv[:, :, 0], gm[:, 0], ALU.subtract))
            link(nc.vector.tensor_tensor(dev[:], dev[:], dev[:], ALU.mult))
            nc.vector.tensor_tensor(var[:], dev[:], mv[:, :, 1], ALU.add).then_inc(prep, 1)
            dve.wait_ge(pw, 2)
            nc.vector.tensor_scalar(dev[:], bs[1][:, 0:S], EPS, None, ALU.add).then_inc(prep, 1)
            dve.wait_ge(pch, 1)
            bc = lambda i: gm[:, i].unsqueeze(2).to_broadcast([P, S, C])
            pb = pick.unsqueeze(1).to_broadcast([P, S, C])
            nc.vector.tensor_tensor(spread[:, 0], bc(0), pb, ALU.mult)
            nc.vector.tensor_tensor(spread[:, 1], bc(1), pb, ALU.mult).then_inc(sp_ready, 1)
            dve.wait_ge(pw, 3)
            link(nc.vector.tensor_scalar(norm[:, 0].rearrange("p s c -> p (s c)"), bs[0][:, 0:S * C], 2.0, None, ALU.mult))
            link(nc.vector.tensor_copy(norm[:, 1].rearrange("p s c -> p (s c)"), bs[1][:, 0:S * C]))
            for q in range(4):
                for sign in range(2):
                    pq = slice(q * C, (q + 1) * C)
                    last = nc.vector.tensor_scalar(rsq[pq, sign], norm[pq, 1].rearrange("p s (g c) -> p s g c", c=4)[:, :, :, q],
                                                   1.0 - 2 * sign, None, ALU.mult)
            last.then_inc(norm_ready, 1)
            dve.wait_ge(norm_ready, 1)
            with dve.Fori(0, S) as s:
                dve.wait_ge(xg_ready[0], s * 4 + 1)
                dve.wait_ge(xg_ready[1], s * 4 + 1)
                nc.vector.tensor_copy(mean_now[:], norm[:, 0, bass.ds(s, 1), :].rearrange("p a c -> p (a c)")).then_inc(now_ready, 1)
                dve.wait_ge(now_ready, s + 1)
                for i in range(4):
                    n = dve.snap(s * 4 + i)
                    for buf in range(2):
                        dve.wait_ge(x_here[buf], n * 32 + 32)
                        dve.wait_ge(y_ps[buf], n * 2 + 1)
                        for c in range(0, 4, 2):
                            ch = i * 8 + buf * 4 + c
                            nc.vector.scalar_tensor_tensor(xg[buf][:, 0, c:c + 2, :], xt[buf][:, 0, c:c + 2, :], mean_now[:, ch:ch + 1],
                                                           xt[buf][:, 1, c:c + 2, :], ALU.subtract, ALU.add)
                        nc.vector.tensor_tensor(xg[buf][:, 1], xt[buf][:, 0], xt[buf][:, 1], ALU.subtract).then_inc(xg_ready[buf], 1)

        @block.gpsimd
        def _(pool):
            pool.wait_ge(prep, 2)
            nc.gpsimd.tensor_tensor(gm[:, 1], dev[:], expo[:], ALU.pow).then_inc(pch, 1)
            pool.wait_ge(w_here, 5 * 16)
            pool.wait_ge(pch, 1)
            turned = [0]

            def copy(dst, src):
                turned[0] += 1
                nc.gpsimd.tensor_copy(dst, src).then_inc(w_turned, 1)
                pool.wait_ge(w_turned, turned[0])

            turn_rows(copy, wt, wr)

        @block.scalar
        def _(act):
            def copy_y(buf, n, i, s):
                for j in range(2):
                    act.wait_ge(y_ps[buf], n * 2 + (j + 1) + 1)
                    act.wait_ge(f_ps[buf], n + 1)
                    if i == 0:
                        act.wait_ge(mid_ps, s + 1)
                    made = b1[buf][j][:].rearrange("p (x c a t r) -> p t x c a r", x=2, c=2, a=2, t=2)
                    nc.scalar.copy(y_mid[:, :, i * 8 + 4 * buf + 2 * j:i * 8 + 4 * buf + 2 * j + 2], made[:, 0, :, :, 0, 16])
                    for cs in range(2):
                        last = nc.scalar.copy(y[buf][:, :, cs, 2 * j:2 * j + 2, :].rearrange("p x c (a r) -> p x (c a) r", a=2),
                                              b1[buf][j][:].rearrange("p (x c t r) -> p t x c r", x=2, c=4, t=2)[:, cs, :, :, 0:16])
                    last.then_inc(y_ready[buf], 1)

            def copy_f(buf, n, half, i):
                act.wait_ge(f_ps[buf], n + 1 + 1)
                k = (i % 2) * 2 + buf
                rs = lambda sign: rs_now[:, sign, 4 * half + k:4 * half + k + 1]
                made = b2[buf][:, 0:MW2].rearrange("p (t n) -> p t n", t=2)
                nc.scalar.activation(fs[half][:, 0, k, :].rearrange("p (t n) -> p t n", t=2), made[:, :, 0:M], ACT.Copy, scale=rs(0))
                nc.scalar.activation(fs[half][:, 1, k, 0:M], made[:, 0, M:0:-1], ACT.Copy, scale=rs(0))
                nc.scalar.activation(fs[half][:, 1, k, M:P], made[:, 1, M:0:-1], ACT.Copy, scale=rs(1)).then_inc(f_ready[buf], 1)

            for buf in range(2):
                act.wait_ge(x_here[buf], 32)
            load_weights(act, w, 0, wt, w_here)
            load_opposite(act, w, 0, wr, w_here)
            with act.Fori(0, S) as s:
                act.wait_ge(norm_ready, 1)
                act.wait_ge(mid_ready, s + 1)
                nc.scalar.copy(rs_mid[:], gm[:, 1, bass.ds(s, 1)])
                nc.scalar.copy(rs_now[:].rearrange("p t g -> p t (g)"), rsq[:, :, bass.ds(s, 1), :].rearrange("p t s g -> p t (s g)")
                               ).then_inc(rs_ready, 1)
                act.wait_ge(rs_ready, s + 1)
                for half in range(2):
                    act.wait_ge(f_out[half], s * 128 + 1)
                    for i in range(2 * half, 2 * half + 2):
                        n = act.snap(s * 4 + i)
                        copy_y(0, n, i, s)
                        copy_y(1, n, i, s)
                        copy_f(0, n, half, i)
                        copy_f(1, n, half, i)
                act.wait_ge(mid_ps, s + 1 + 1)
                act.wait_ge(mid_out, s * 16 + 1)
                nc.scalar.activation(f_mid[:].rearrange("c (t n) -> c t n", t=2),
                                     bs[0][0:C, 0:MW2].rearrange("c (t n) -> c t n", t=2)[:, :, 0:M], ACT.Copy,
                                     scale=rs_mid[0:C]).then_inc(mid_ready, 1)


def build_mix(nc, f_d, w, t_d, wt, wr, S):
    f32 = mybir.dt.float32
    T = ROWS
    with ExitStack() as ctx:
        sb = lambda n, s: ctx.enter_context(nc.sbuf_tensor("m_" + n, s, f32))
        ps = lambda n, s: ctx.enter_context(nc.psum_tensor("m_" + n, s, f32))
        sem = lambda n: ctx.enter_context(nc.semaphore("m_" + n))
        ft = [sb(f"ft{i}", [P, S, T, M]) for i in range(2)]
        to = [sb(f"to{i}", [P, S, M]) for i in range(2)]
        bank = [[[ps(f"bank{i}{g}{h}", [P, 512]) for h in range(2)] for g in range(2)] for i in range(2)]
        here = [sem(f"here{i}") for i in range(2)]
        wr_here, turned, emptied, passed = (sem(n) for n in ("wr_here", "turned", "emptied", "passed"))
        done = sem("done")
        packed = [sem(f"packed{g}") for g in range(2)]
        gone = [sem(f"gone{g}") for g in range(2)]
        block = ctx.enter_context(nc.Block())
        NCK = M // 2 // T
        re = lambda g: slice(g * M, g * M + C)
        im = lambda g: slice(g * M + C, (g + 1) * M)

        @block.sync
        def _(sp):
            for k in range(NCK):
                buf = k % 2
                if k == 0:
                    sp.sem_inc(here[0], 32)
                if k:
                    sp.wait_ge(turned, k)
                    load_opposite(sp, w, k, wr, wr_here)
                if k >= 2:
                    sp.wait_ge(done, k - 1)
                for g in range(2):
                    y0 = 32 * g + T * k
                    for part, p in ((0, re(g)), (1, im(g))):
                        for t in range(T):
                            sp.dma_start(ft[buf][p, :, t, :], f_d[:, :, mode_row(y0 + t), part * M:(part + 1) * M].rearrange("b i n -> i b n")
                                         ).then_inc(here[buf], 16)
                if k:
                    load_weights(sp, w, k, wt[buf], here[buf])
            for g in range(2):
                sp.wait_ge(gone[g], 16 * NCK)

        @block.tensor
        def _(pe):
            def chunk(buf, n):
                for kx in range(M):
                    half, col = kx // 32, (kx % 32) * S
                    for t in range(T):
                        for g in range(2):
                            pg = slice(g * M, (g + 1) * M)
                            last = nc.tensor.matmul(bank[buf][g][half][t * C:(t + 1) * C, col:col + S], wt[buf][pg, :, t, kx],
                                                    ft[buf][pg, :, t, kx], start=True, stop=True)
                last.then_inc(done, 1)

            with pe.Fori(1, NCK // 2 + 1) as k2:
                for buf in range(2):
                    pe.wait_ge(here[buf], k2 * (18 * 16))
                    pe.wait_ge(turned, k2 * 2 + (buf - 1))
                    pe.wait_ge(emptied, k2 * 2 + (buf - 1))
                    pe.sem_inc(passed, 1)
                    chunk(buf, k2)

        @block.vector
        def _(dve):
            dve.sem_inc(emptied, 2)

            dve.sem_inc(turned, 1)

            def turn(k):
                dve.wait_ge(wr_here, 16 * (2 * k))
                if k >= 2:
                    dve.wait_ge(done, k - 1)
                turn_rows(nc.vector.tensor_copy, wt[k % 2], wr).then_inc(turned, 1)

            def pack(k):
                for g in range(2):
                    dve.wait_ge(done, k + 1)
                    if k:
                        dve.wait_ge(gone[g], 16 * k)
                    for half in range(2):
                        last = nc.vector.tensor_copy(to[g][:, :, 32 * half:32 * half + 32],
                                                     bank[k % 2][g][half][:, 0:32 * S].rearrange("p (x b) -> p b x", b=S))
                    last.then_inc(packed[g] if g == 0 else emptied, 1)

            for k in range(NCK):
                if k + 1 < NCK:
                    turn(k + 1)
                pack(k)

        @block.scalar
        def _(act):
            for k in range(NCK):
                for g in range(2):
                    y0 = 32 * g + k * T
                    if g == 0:
                        act.wait_ge(packed[0], k + 1)
                    else:
                        act.wait_ge(emptied, k + 3)
                    act.dma_start(t_d[:, y0:y0 + T].rearrange("b t o x -> (t o) b x"), to[g][:]).then_inc(gone[g], 16)


def build_inverse(nc, t_d, x1d, bias, spec, out_d, S):
    f32 = mybir.dt.float32
    ALU = mybir.AluOpType
    NB = 4
    with ExitStack() as ctx:
        sb = lambda n, s: ctx.enter_context(nc.sbuf_tensor("i_" + n, s, f32))
        ps = lambda n, s: ctx.enter_context(nc.psum_tensor("i_" + n, s, f32))
        sem = lambda n: ctx.enter_context(nc.semaphore("i_" + n))
        back = sb("back", [P, 2 * IMG])
        back_h, back_w = back[:, 0:IMG], back[:, IMG:2 * IMG]
        bias_bc = sb("bias_bc", [P, C])
        t2 = [sb(f"t2{i}", [P, 16, P]) for i in range(2)]
        tt = sb("tt", [P, 16, M])
        u = [sb(f"u{i}", [P, IMG]) for i in range(2)]
        xt = [sb(f"xt{i}", [P, 2, 4, IMG]) for i in range(NB)]
        ot = [sb(f"ot{i}", [P, 2, 4, IMG]) for i in range(NB)]
        ub = [ps(f"ub{i}", [P, 512]) for i in range(2)]
        ob = [ps(f"ob{i}", [P, 512]) for i in range(4)]
        here, zeroed, u_ps, u_ready, o_ps, o_ready = (sem(n) for n in ("here", "zeroed", "u_ps", "u_ready", "o_ps", "o_ready"))
        t_here = sem("t_here")
        t2_ready = [sem(f"t2_ready{i}") for i in range(2)]
        x_here = [sem(f"x_here{i}") for i in range(NB)]
        gone = [sem(f"gone{i}") for i in range(NB)]
        block = ctx.enter_context(nc.Block())
        xv = x1d.rearrange("s c (a p) w -> s a p c w", p=P)
        ov = out_d.rearrange("s c (a p) w -> s a p c w", p=P)

        @block.sync
        def _(sp):
            sp.dma_start(back[:], spec[:, OFF_BACK:OFF_BACK + 2 * IMG]).then_inc(here, 16)
            sp.dma_start(bias_bc[:], bias.rearrange("c a b -> (a b) c").to_broadcast([P, C])).then_inc(here, 16)

            def load_t(s):
                for h in range(2):
                    sp.dma_start(tt[h * M:(h + 1) * M], t_d[s, :, 16 * h:16 * h + 16, :]).then_inc(t_here, 16)

            load_t(0)
            with sp.Fori(0, S) as s:
                for g in range(8):
                    if g == 6:
                        sp.wait_ge(t2_ready[1], s * 2 + 3)
                        load_t(sp.snap((s + 1) % S))
                    b = g % NB
                    sp.wait_ge(o_ready, (s * 32 + 4 * (g - NB) + 4 if g >= NB else s * 32) + 1)
                    for a in range(2):
                        sp.dma_start(xt[b][:, a], xv[s, a, :, 4 * g:4 * g + 4, :]).then_inc(x_here[b], 16)
            for b in range(NB):
                sp.wait_ge(gone[b], 32 * 2 * S + 1)
            sp.wait_ge(t_here, 32 * (S + 1))

        @block.tensor
        def _(pe):
            pe.wait_ge(here, 32)

            def over_ky(c, n):
                pe.wait_ge(u_ready, (n - 1 if c else n) + 1)
                nc.tensor.matmul(ub[c % 2][:, 0:IMG], t2[c // 16][:, c % 16, :], back_h, start=True, stop=True).then_inc(u_ps, 1)

            with pe.Fori(0, S) as s:
                n0 = pe.snap(s * C)
                pe.wait_ge(t2_ready[0], s * 2 + 3)
                over_ky(0, n0)
                for c in range(C):
                    if c + 1 == 16:
                        pe.wait_ge(t2_ready[1], s * 2 + 3)
                    if c + 1 < C:
                        over_ky(c + 1, n0 + (c + 1))
                    pe.wait_ge(u_ready, n0 + (c + 1) + 1)
                    pe.wait_ge(o_ready, (n0 + (c - 3) if c >= 3 else n0) + 1)
                    for a in range(2):
                        last = nc.tensor.matmul(ob[c % 4][:, a * IMG:(a + 1) * IMG], u[c % 2][:, a * P:(a + 1) * P], back_w,
                                                start=True, stop=True)
                    last.then_inc(o_ps, 1)

        @block.scalar
        def _(act):
            def store(s, n0, g):
                act.wait_ge(o_ready, n0 + (4 * g + 5))
                for a in range(2):
                    act.dma_start(ov[s, a, :, 4 * g:4 * g + 4, :], ot[g % NB][:, a]).then_inc(gone[g % NB], 16)

            def spread(h, k, used):
                act.wait_ge(t_here, k * 32)
                act.wait_ge(u_ps, used + 1)
                nc.scalar.copy(t2[h][0:M, :, 0:M], tt[h * M:(h + 1) * M]).then_inc(t2_ready[h], 1)

            act.wait_ge(zeroed, 1)
            spread(0, 1, 0)
            spread(1, 1, 0)
            with act.Fori(0, S) as s:
                n0 = act.snap(s * C)
                for c in range(C):
                    act.wait_ge(u_ps, n0 + (c + 1) + 1)
                    act.wait_ge(o_ps, (n0 + (c - 1) if c else n0) + 1)
                    nc.scalar.copy(u[c % 2][:], ub[c % 2][:, 0:IMG]).then_inc(u_ready, 1)
                    if c % 4 == 2 and c > 4:
                        store(s, n0, c // 4 - 1)
                    if c == C - 4:
                        spread(0, s + 2, n0 + 16)
                spread(1, s + 2, n0 + C)
                store(s, n0, C // 4 - 1)

        @block.vector
        def _(dve):
            for counter in (o_ps, o_ready, u_ready, u_ps, *gone, *t2_ready):
                dve.sem_inc(counter, 1)

            def spread(h, k, used):
                dve.wait_ge(t_here, k * 32)
                dve.wait_ge(u_ps, used + 1)
                nc.vector.tensor_copy(t2[h][M:P, :, M:P], tt[h * M:(h + 1) * M]).then_inc(t2_ready[h], 1)

            nc.vector.memset(t2[0][:], 0.0)
            nc.vector.memset(t2[1][:], 0.0).then_inc(zeroed, 1)
            dve.wait_ge(zeroed, 1)
            spread(0, 1, 0)
            spread(1, 1, 0)
            dve.wait_ge(here, 32)
            with dve.Fori(0, S) as s:
                n0 = dve.snap(s * C)
                for c in range(C):
                    g = c // 4
                    b = g % NB
                    if c % 4 == 0:
                        dve.wait_ge(x_here[b], s * 64 + (g // NB) * 32 + 32)
                        dve.wait_ge(gone[b], s * 64 + (g // NB) * 32 + 1)
                    dve.wait_ge(o_ps, n0 + (c + 1) + 1)
                    nc.vector.scalar_tensor_tensor(ot[b][:, :, c % 4, :], ob[c % 4][:].rearrange("p (a w) -> p a w", a=2),
                                                   bias_bc[:, c:c + 1], xt[b][:, :, c % 4, :], ALU.add, ALU.add).then_inc(o_ready, 1)
                    if c == C - 4:
                        spread(0, s + 2, n0 + 16)
                spread(1, s + 2, n0 + C)


def build(nc, x, w_c1, w_c2, weight1, weight2, weight3, mode_w, bias, consts, spec, out):
    f32, S = mybir.dt.float32, x.shape[0]
    scratch = lambda name, shape: nc.dram_tensor(name, shape, f32, kind="Internal").ap()
    x1 = scratch("x1", [S, C, IMG, IMG])
    x1_stats = scratch("x1_stats", [P, S, 2])
    modes = scratch("modes", [S, C, M, 2 * M])
    mixed_modes = scratch("mixed_modes", [S, M, C, M])
    build_convs(nc, x, w_c1, w_c2, weight1, weight2, weight3, consts, x1, x1_stats, S)
    with ExitStack() as ctx:
        weights = lambda name: ctx.enter_context(nc.sbuf_tensor(name, [P, C, ROWS, M], f32))
        wt, wr = [weights(f"m_wt{i}") for i in range(2)], weights("m_wr")
        build_forward(nc, x1, x1_stats, spec, modes, mode_w, wt[0], wr, S)
        build_mix(nc, modes, mode_w, mixed_modes, wt, wr, S)
    build_inverse(nc, mixed_modes, x1, bias, spec, out, S)


_INS = ["x", "L0_conv_w_c1", "L0_conv_w_c2", "L0_conv_weight1", "L0_conv_weight2", "L0_conv_weight3",
        "L1_conv_weight", "L1_conv_bias"]


def kernel(**inputs):
    import concourse.bacc as bacc
    from concourse.bass_utils import run_bass_kernel_spmd

    nc = bacc.Bacc("TRN2", target_bir_lowering=False, num_devices=1)
    arrays = {f"in_{name}": np.ascontiguousarray(inputs[name]) for name in _INS}
    arrays["consts"] = constants()
    arrays["spec"] = spectral_constants()
    args = [nc.dram_tensor(n, a.shape, mybir.dt.from_np(a.dtype), kind="ExternalInput").ap() for n, a in arrays.items()]
    out = nc.dram_tensor("out", inputs["x"].shape, mybir.dt.float32, kind="ExternalOutput").ap()
    build(nc, *args, out)
    r = run_bass_kernel_spmd(nc, [arrays], core_ids=[0])
    return r.results[0]["out"]
```
